# Optimizing a Trainium2 kernel written in Bass

```python
import numpy as np
import jax
import jax.numpy as jnp

def _softmax(x, axis=-1):
    return jax.nn.softmax(x, axis=axis)

def _gelu(x):
    return jax.nn.gelu(x, approximate=True)

def _silu(x):
    return jax.nn.silu(x)

def _sigmoid(x):
    return jax.nn.sigmoid(x)

def _layernorm(x, axis=-1, eps=1e-05):
    m = jnp.mean(x, axis=axis, keepdims=True)
    v = jnp.var(x, axis=axis, keepdims=True)
    return (x - m) / jnp.sqrt(v + eps)

def _scatter_add(tgt, idx, src, axis=0):
    return tgt.at[idx].add(src)

def _segment_sum(src, seg, n):
    return jax.ops.segment_sum(src, seg, n)
kernel_name = 'mk_adaln_d1_jaxref_r8_4039b0'

def setup_inputs(seed: int=0):
    np.random.seed(seed)
    _w = jnp.asarray

    def _L0_attn_setup():
        import jax, jax.numpy as jnp
        import numpy as np
        EMBED_DIM = 128
        NUM_HEADS = 16
        HEAD_DIM = EMBED_DIM // NUM_HEADS
        KERNEL_SIZE = 64
        B, L = (2, 256)
        key = jax.random.key(seed)
        ks = jax.random.split(key, 6)
        x = jax.random.normal(ks[0], (B, L, EMBED_DIM), dtype=jnp.float32)
        qkv_w = jax.random.normal(ks[1], (EMBED_DIM, 3 * EMBED_DIM), dtype=jnp.float32) / np.sqrt(EMBED_DIM)
        qkv_b = jnp.zeros((3 * EMBED_DIM,), dtype=jnp.float32)
        out_w = jax.random.normal(ks[2], (EMBED_DIM, EMBED_DIM), dtype=jnp.float32) / np.sqrt(EMBED_DIM)
        out_b = jnp.zeros((EMBED_DIM,), dtype=jnp.float32)
        proj = jax.random.normal(ks[3], (NUM_HEADS, HEAD_DIM, KERNEL_SIZE), dtype=jnp.float32) / np.sqrt(HEAD_DIM)
        return {'x': x, 'qkv_w': qkv_w, 'qkv_b': qkv_b, 'out_w': out_w, 'out_b': out_b, 'proj': proj}
    _L0_attn_in = _L0_attn_setup()

    def _L0_ffn_setup():
        import jax, jax.numpy as jnp
        import numpy as np
        D_MODEL = 128
        D_FF = 512
        NUM_EXPERTS = 8
        key = jax.random.key(seed)
        ks = jax.random.split(key, 8)
        scale_in = 1.0 / np.sqrt(D_MODEL)
        scale_ff = 1.0 / np.sqrt(D_FF)
        x = jax.random.normal(ks[0], (4, 256, D_MODEL), dtype=jnp.float32)
        gate_w = jax.random.uniform(ks[1], (NUM_EXPERTS, D_MODEL), jnp.float32, -scale_in, scale_in)
        gate_b = jax.random.uniform(ks[2], (NUM_EXPERTS,), jnp.float32, -scale_in, scale_in)
        expert_bias = jnp.zeros((NUM_EXPERTS,), dtype=jnp.float32)
        w1 = jax.random.uniform(ks[3], (NUM_EXPERTS, D_MODEL, D_FF), jnp.float32, -scale_in, scale_in)
        b1 = jax.random.uniform(ks[4], (NUM_EXPERTS, D_FF), jnp.float32, -scale_in, scale_in)
        w2 = jax.random.uniform(ks[5], (NUM_EXPERTS, D_FF, D_MODEL), jnp.float32, -scale_ff, scale_ff)
        b2 = jax.random.uniform(ks[6], (NUM_EXPERTS, D_MODEL), jnp.float32, -scale_ff, scale_ff)
        return {'x': x, 'gate_w': gate_w, 'gate_b': gate_b, 'expert_bias': expert_bias, 'w1': w1, 'b1': b1, 'w2': w2, 'b2': b2}
    _L0_ffn_in = _L0_ffn_setup()
    _L0_c = _w((lambda *s: np.random.randn(*s).astype(np.float32) * 0.05)(8, 128))
    _L0_wmod = _w((lambda *s: np.random.randn(*s).astype(np.float32) * 0.05)(128, 6 * 128) * 128 ** (-0.5))
    _d = {'L0_attn_x': _L0_attn_in['x'], 'L0_attn_qkv_w': _L0_attn_in['qkv_w'], 'L0_attn_qkv_b': _L0_attn_in['qkv_b'], 'L0_attn_out_w': _L0_attn_in['out_w'], 'L0_attn_out_b': _L0_attn_in['out_b'], 'L0_attn_proj': _L0_attn_in['proj'], 'L0_ffn_gate_w': _L0_ffn_in['gate_w'], 'L0_ffn_gate_b': _L0_ffn_in['gate_b'], 'L0_ffn_expert_bias': _L0_ffn_in['expert_bias'], 'L0_ffn_w1': _L0_ffn_in['w1'], 'L0_ffn_b1': _L0_ffn_in['b1'], 'L0_ffn_w2': _L0_ffn_in['w2'], 'L0_ffn_b2': _L0_ffn_in['b2'], 'L0_c': _L0_c, 'L0_wmod': _L0_wmod}
    _x0 = _d['L0_attn_x']
    _d['L0_attn_x'] = jax.random.normal(jax.random.fold_in(jax.random.key(seed), 1), (8, 1024, 128), dtype=_x0.dtype)
    del _x0
    return _d

def reference(L0_attn_x, L0_attn_qkv_w, L0_attn_qkv_b, L0_attn_out_w, L0_attn_out_b, L0_attn_proj, L0_ffn_gate_w, L0_ffn_gate_b, L0_ffn_expert_bias, L0_ffn_w1, L0_ffn_b1, L0_ffn_w2, L0_ffn_b2, L0_c, L0_wmod):

    def _L0_attn_ref(x, qkv_w, qkv_b, out_w, out_b, proj):
        import jax, jax.numpy as jnp
        import numpy as np
        EMBED_DIM = 128
        NUM_HEADS = 16
        HEAD_DIM = EMBED_DIM // NUM_HEADS
        KERNEL_SIZE = 64
        B, L = (2, 256)
        Bn, Ln, E = x.shape
        H, D, M = proj.shape
        qkv = x @ qkv_w + qkv_b
        q, k, v = jnp.split(qkv, 3, axis=-1)
        q = q.reshape(Bn, Ln, H, D).transpose(0, 2, 1, 3)
        k = k.reshape(Bn, Ln, H, D).transpose(0, 2, 1, 3)
        v = v.reshape(Bn, Ln, H, D).transpose(0, 2, 1, 3)
        q_prime = jax.nn.relu(jnp.einsum('bhld,hdm->bhlm', q, proj))
        k_prime = jax.nn.relu(jnp.einsum('bhld,hdm->bhlm', k, proj))
        kv_prod = jnp.einsum('bhlm,bhld->bhlmd', k_prime, v)
        kv_cumsum = jnp.cumsum(kv_prod, axis=2)
        context = jnp.einsum('bhlm,bhlmd->bhld', q_prime, kv_cumsum)
        k_cumsum = jnp.cumsum(k_prime, axis=2)
        norm = jnp.einsum('bhlm,bhlm->bhl', q_prime, k_cumsum)
        out = context / (norm[..., None] + 1e-06)
        out = out.transpose(0, 2, 1, 3).reshape(Bn, Ln, E)
        return out @ out_w + out_b

    def _L0_ffn_ref(x, gate_w, gate_b, expert_bias, w1, b1, w2, b2):
        import jax, jax.numpy as jnp
        import numpy as np
        D_MODEL = 128
        D_FF = 512
        NUM_EXPERTS = 8
        gate_logits = jnp.einsum('bsd,ed->bse', x, gate_w) + gate_b + expert_bias
        top_idx = jnp.argmax(gate_logits, axis=-1)
        out = jnp.zeros_like(x)
        for e in range(NUM_EXPERTS):
            mask = (top_idx == e)[..., None].astype(x.dtype)
            h = jax.nn.relu(jnp.einsum('bsd,df->bsf', x, w1[e]) + b1[e])
            y = jnp.einsum('bsf,fd->bsd', h, w2[e]) + b2[e]
            out = out + mask * y
        return out
    x = L0_attn_x
    mod = (_silu(L0_c) @ L0_wmod).reshape(L0_c.shape[0], 6, 1, -1)
    sa, ca, ga, sb, cb, gb = (mod[:, 0], mod[:, 1], mod[:, 2], mod[:, 3], mod[:, 4], mod[:, 5])
    ga = (2 * (ga >= 0) - 1) * jnp.maximum(jnp.abs(ga), 0.25)
    gb = (2 * (gb >= 0) - 1) * jnp.maximum(jnp.abs(gb), 0.25)
    h = _layernorm(x, axis=-1) * (1 + ca) + sa
    x = x + ga * _L0_attn_ref(h, L0_attn_qkv_w, L0_attn_qkv_b, L0_attn_out_w, L0_attn_out_b, L0_attn_proj)
    h = _layernorm(x, axis=-1) * (1 + cb) + sb
    x = x + gb * _L0_ffn_ref(h, L0_ffn_gate_w, L0_ffn_gate_b, L0_ffn_expert_bias, L0_ffn_w1, L0_ffn_b1, L0_ffn_w2, L0_ffn_b2)
    return x

_drawn_inputs = setup_inputs


def setup_inputs(seed=0):
    import zlib

    import numpy as np

    out = dict(_drawn_inputs(seed))
    spreads = {'L0_attn_qkv_b': (0.0, 0.1),
     'L0_attn_out_b': (0.0, 0.304),
     'L0_ffn_expert_bias': (0.0, 0.1)}
    factors = {'L0_attn_proj': 5.68, 'L0_ffn_gate_b': 2.97, 'L0_ffn_b1': 8.0, 'L0_ffn_b2': 8.0}
    for name, (base, spread) in spreads.items():
        noise = np.random.default_rng([zlib.crc32(name.encode()), seed]).standard_normal(out[name].shape)
        drawn = base * np.exp(spread * noise) if base else spread * noise
        out[name] = jnp.asarray(drawn.astype(out[name].dtype))
    for name, factor in factors.items():
        out[name] = (out[name] * factor).astype(out[name].dtype)
    return out
```

```python
from contextlib import ExitStack

import concourse.bass as bass
from concourse import mybir

P = 128
BATCH, SEQ, E = 8, 1024, 128
HEADS, HD, FEAT = 16, 8, 64
EXPERTS, DFF = 8, 512
TOKENS = BATCH * SEQ
TILES = TOKENS // P
UNROLL = 4
GROUPS = TILES // UNROLL
PER_BATCH = SEQ // P
PAIRS = HEADS // 2
HW = HD + 1
VW = 224
FW = 96
SW = 96
REGION = TOKENS + P
RW = 400
COL_X, COL_G, COL_ID = E, 2 * E, 3 * E
FTILES = TILES + EXPERTS
FUNROLL = 8
NOWHERE = 16384.0
EPS_LN, EPS_NORM = 1e-5, 1e-6
BIG = 3.0e38

F32 = mybir.dt.float32
BF16 = mybir.dt.bfloat16
I32 = mybir.dt.int32
U32 = mybir.dt.uint32
ALU = mybir.AluOpType
ACT = mybir.ActivationFunctionType
AX = mybir.AxisListType


def wait(eng, sem, value):
    if isinstance(value, int) and value <= 0:
        return
    eng.wait_ge(sem, value)


def adaln_block(nc, x, qkv_w, qkv_b, out_w, out_b, proj, gate_w, gate_b, expert_bias, w1, b1, w2, b2, c, wmod, out):
    ctx = ExitStack()
    with ctx:
        def sb(name, shape, dt=F32):
            return ctx.enter_context(nc.sbuf_tensor(name, shape, dt))

        def pb(name, shape):
            return ctx.enter_context(nc.psum_tensor(name, shape, F32))

        def sem(name):
            return ctx.enter_context(nc.semaphore(name))

        dispatch = nc.dram_tensor("dispatch", [EXPERTS * REGION, RW], F32).ap()

        ident = sb("ident", [P, P])
        causal = sb("causal", [P, P])
        earlier = sb("earlier", [P, P], BF16)
        ones = sb("ones", [P, P], BF16)
        batch_sel = sb("batch_sel", [BATCH, BATCH, P])
        iota_i = sb("iota_i", [P, 256], I32)
        tile_no = sb("tile_no", [P, FTILES])
        expert_no = sb("expert_no", [P, EXPERTS])
        expert_rank = sb("expert_rank", [P, EXPERTS])
        region_at = sb("region_at", [P, EXPERTS])
        before = sb("before", [P, EXPERTS, EXPERTS])
        token_no = sb("token_no", [P, TILES])
        row_no = sb("row_no", [P, 1])
        eps_ln = sb("eps_ln", [P, 1])
        lim_hi = sb("lim_hi", [P, GROUPS + 1])
        lim_lo = sb("lim_lo", [P, GROUPS + 1])
        pad_rows = sb("pad_rows", [P, RW])
        wqkv_sb = sb("wqkv_sb", [P, 3 * E])
        qb_col = sb("qb_col", [P, 1])
        kb_col = sb("kb_col", [P, 1])
        vb_row = sb("vb_row", [P, E])
        ob_row = sb("ob_row", [P, E])
        wo_sb = sb("wo_sb", [P, E])
        proj_bd = sb("proj_bd", [P, HEADS * FEAT])
        gw_nat = sb("gw_nat", [EXPERTS, E])
        gwT = sb("gwT", [P, EXPERTS])
        gb_row = sb("gb_row", [P, EXPERTS])
        eb_row = sb("eb_row", [P, EXPERTS])
        gbias = sb("gbias", [P, EXPERTS])
        w1_sb = sb("w1_sb", [P, EXPERTS, DFF])
        w2_sb = sb("w2_sb", [P, EXPERTS, (DFF // P) * E])
        b1_row = sb("b1_row", [P, EXPERTS, DFF])
        b2_row = sb("b2_row", [P, EXPERTS, E])
        c_sb = sb("c_sb", [BATCH, E])
        c_tmp = sb("c_tmp", [BATCH, 3, E])
        cT = sb("cT", [P, BATCH])
        wmod_sb = sb("wmod_sb", [P, 6 * E])
        mod_raw = sb("mod_raw", [BATCH, 6, E])
        mod_tmp = sb("mod_tmp", [BATCH, 3, 2, E])
        mod_rows = sb("mod_rows", [BATCH, 6, E])
        mod_bc = sb("mod_bc", [P, GROUPS, 4, E])
        saT = sb("saT", [P, BATCH, 2])
        caT = sb("caT", [P, BATCH, 2])
        wo_g = sb("wo_g", [P, GROUPS, E])
        ob_g = sb("ob_g", [P, GROUPS, E])

        x_in = [sb(f"x_in{k}", [P, E]) for k in range(4)]
        stats1, mv1, std1, xn1 = sb("stats1", [P, 6]), sb("mv1", [P, 2]), sb("std1", [P, 2]), sb("xn1", [P, 2, E])
        hT = sb("hT", [P, P])
        qkT = sb("qkT", [P, 2, 2, P])
        vaug = [sb(f"vaug{k}", [P, VW]) for k in range(4)]
        q_blk = [sb(f"q_blk{k}", [P, PAIRS, 2, P]) for k in range(2)]
        kfT = sb("kfT", [P, PAIRS, P])
        kf = [sb(f"kf{k}", [P, HEADS * FEAT]) for k in range(2)]
        scoresT = sb("scoresT", [P, HEADS, P])
        state = [sb(f"state{k}", [P, SW]) for k in range(2)]
        o_sb = [sb(f"o_sb{k}", [P, 4 * P]) for k in range(2)]
        den, o_n, onT = sb("den", [P, 2, HEADS]), sb("o_n", [P, HEADS, HD]), sb("onT", [P, P])
        xg = sb("xg", [P, 4, E])
        stats2, mv2, std2, xn2 = sb("stats2", [P, 6]), sb("mv2", [P, 2]), sb("std2", [P, 2]), sb("xn2", [P, E])
        h_tmp = sb("h_tmp", [P, E])
        stage = [sb(f"stage{k}", [P, RW]) for k in range(4)]
        h2T = sb("h2T", [P, P])
        logits, top, score, best = sb("logits", [P, EXPERTS]), sb("top", [P, 1]), sb("score", [P, EXPERTS]), sb("best", [P, 1])
        onehot = sb("onehot", [P, EXPERTS], BF16)
        pos, pos_m, slot = sb("pos", [P, EXPERTS]), sb("pos_m", [P, EXPERTS]), sb("slot", [P, 1])
        slot_i = [sb(f"slot_i{k}", [P, 1], U32) for k in range(4)]
        filled = sb("filled", [P, EXPERTS])

        n_f, n_i, n_s = sb("n_f", [P, EXPERTS]), sb("n_i", [P, EXPERTS], I32), sb("n_s", [P, EXPERTS], I32)
        n_t, t_begin, t_end, t_off = (sb(n, [P, EXPERTS]) for n in ("n_t", "t_begin", "t_end", "t_off"))
        ee = sb("ee", [P, EXPERTS, EXPERTS])
        sel_a, sel_b, sel = (q_blk[0][:, :, :, :].rearrange("p j h t -> p (j h t)")[:, k * 640:k * 640 + FTILES * EXPERTS]
                             .rearrange("p (j e) -> p j e", e=EXPERTS) for k in range(3))
        valid, rows_f, exps_f, nowhere = (sb(n, [P, FTILES]) for n in ("valid", "rows_f", "exps_f", "nowhere"))
        rows_a, rows_b = sb("rows_a", [P, FTILES]), sb("rows_b", [P, FTILES])
        rows_i, exps_i = sb("rows_i", [P, FTILES], I32), sb("exps_i", [P, FTILES], I32)
        pad_at = sb("pad_at", [P, EXPERTS], U32)
        xt = [sb(f"xt{k}", [P, RW]) for k in range(4)]
        spare = q_blk[1][:, :, :, :].rearrange("p j h t -> p (j h t)")
        xt += [spare[:, k * RW:(k + 1) * RW] for k in range(FUNROLL - 4)]
        xtT = sb("xtT", [P, 2, P])
        hid, hidT = (scoresT[:, 8 * w:8 * w + 8, :].rearrange("p (k c) t -> p k (c t)", k=2) for w in range(2))
        y1, y2 = sb("y1", [P, 2, E]), sb("y2", [P, 2, E])
        res = [kfT[:, k, :] for k in range(FUNROLL)]
        res_i = [sb(f"res_i{k}", [P, 1], U32) for k in range(FUNROLL)]

        ring = pb("ring", [P, 4, 512])
        o_ps = pb("o_ps", [P, 512])
        f_ps = pb("f_ps", [P, 2, 512])
        m_ps = pb("m_ps", [P, 512])

        s = {n: sem(n) for n in (
            "waited", "weights_in", "ffn_weights_in", "pool_consts", "dve_setup", "pe_setup", "act_setup", "pool_setup",
            "x_in0", "x_in1", "x_in2", "x_in3", "ln1_steps", "std1_done", "xT_ready", "hT_done", "qkv_ready",
            "qk_done", "v_done", "s_ready", "s_masked", "q_ready", "q_lo_done", "q_hi_done", "k_ready", "k_done",
            "kf_ready", "kf_done", "o_ready", "o_copied", "f_ready", "state_steps", "oT_ready", "norm_steps",
            "onT_ready", "onT_done", "proj_ready", "ln2_steps", "std2_done", "xg_done", "h_steps", "payload_done",
            "h2T_ready", "h2T_done", "gate_ready", "gate_steps", "rank_ready", "rank_steps",
            "scat0", "scat1", "scat2", "scat3", "pads_out", "table_steps",
            *(f"xt{k}" for k in range(FUNROLL)), "xtT_ready", "xtT_done", "hid_ready", "hid_done", "hidT_ready",
            "hidT_done", "y_ready", "y_steps", "res_done", "res_i_done", *(f"out{k}" for k in range(FUNROLL)))}
        x_loaded = [s[f"x_in{k}"] for k in range(4)]
        scattered = [s[f"scat{k}"] for k in range(4)]
        xt_loaded = [s[f"xt{k}"] for k in range(FUNROLL)]
        stored = [s[f"out{k}"] for k in range(FUNROLL)]

        N_W = 11 + HEADS
        N_FFN_LOADS = 3 + EXPERTS
        SETUP_SILU, SETUP_CT, SETUP_ROWS = 34, 36, 48
        SETUP_TABLES = SETUP_ROWS + 2 + 2 * BATCH
        SETUP_DONE = SETUP_TABLES + 1
        PADS_KNOWN, TABLES_DONE = 1, 22
        x_t = x.rearrange("b (n p) e -> (b n) p e", p=P).rearrange("t p e -> (t p) e")
        out_rows = out.rearrange("b s e -> (b s) e")

        def steps(engine, body, first, last):
            lo, hi = 1, GROUPS - 1
            for n in range(first, lo * UNROLL):
                body(n, n // UNROLL, n % UNROLL, lambda k, n=n: 0 <= n + k < TILES)
            with engine.Fori(lo, hi) as i:
                for u in range(UNROLL):
                    body(i * UNROLL + u, i, u, lambda k: True)
            for n in range(hi * UNROLL, last + 1):
                body(n, n // UNROLL, n % UNROLL, lambda k, n=n: 0 <= n + k < TILES)

        def ffn_steps(engine, body):
            last = FTILES // FUNROLL - 1
            for m in range(-2, FUNROLL):
                body(m, m // FUNROLL, m % FUNROLL, lambda k, m=m: 0 <= m + k < FTILES)
            with engine.Fori(1, last) as i:
                for u in range(FUNROLL):
                    body(i * FUNROLL + u, i, u, lambda k: True)
            for m in range(last * FUNROLL, FTILES + 1):
                body(m, m // FUNROLL, m % FUNROLL, lambda k, m=m: 0 <= m + k < FTILES)

        def y_ps(k):
            return o_ps[:, 0:E] if k == 0 else f_ps[:, 0, 0:E]

        def settled(eng):
            eng.sem_inc(s["waited"], 1)

        FIRST, LAST = -3, TILES + 2

        block = ctx.enter_context(nc.Block())

        @block.sync
        def _(sp):
            def load(dst, src, signal):
                sp.dma_start(dst, src).then_inc(s[signal], 16)

            load(c_sb[:, :], c, "weights_in")
            load(wmod_sb[:, :], wmod, "weights_in")
            load(wqkv_sb[:, :], qkv_w, "weights_in")
            load(wo_sb[:, :], out_w, "weights_in")
            load(gw_nat[:, :], gate_w, "weights_in")
            load(vb_row[:, :], qkv_b[2 * E:3 * E][None, :].to_broadcast([P, E]), "weights_in")
            load(ob_row[:, :], out_b[None, :].to_broadcast([P, E]), "weights_in")
            load(gb_row[:, :], gate_b[None, :].to_broadcast([P, EXPERTS]), "weights_in")
            load(eb_row[:, :], expert_bias[None, :].to_broadcast([P, EXPERTS]), "weights_in")
            with nc.allow_non_contiguous_dma(reason="bias columns"):
                load(qb_col[:, :], qkv_b[0:E][:, None], "weights_in")
                load(kb_col[:, :], qkv_b[E:2 * E][:, None], "weights_in")
            for t in range(4):
                sp.dma_start(x_in[t][:, :], x_t[t * P:(t + 1) * P, :]).then_inc(x_loaded[t], 16)
            sp.wait_ge(s["pool_consts"], 2)
            for h in range(HEADS):
                load(proj_bd[h * HD:(h + 1) * HD, h * FEAT:(h + 1) * FEAT], proj[h, :, :], "weights_in")
            load(w1_sb[:, :, :], w1.rearrange("e d f -> d e f"), "ffn_weights_in")
            for e in range(EXPERTS):
                load(w2_sb[:, e, :].rearrange("p (c d) -> p c d", c=DFF // P),
                     w2[e, :, :].rearrange("(c p) d -> p c d", p=P), "ffn_weights_in")
            load(b1_row[:, :, :], b1.rearrange("e f -> (e f)")[None, :].to_broadcast([P, EXPERTS * DFF])
                 .rearrange("p (e f) -> p e f", e=EXPERTS), "ffn_weights_in")
            load(b2_row[:, :, :], b2.rearrange("e f -> (e f)")[None, :].to_broadcast([P, EXPERTS * E])
                 .rearrange("p (e f) -> p e f", e=EXPERTS), "ffn_weights_in")

            with sp.Fori(1, GROUPS) as i:
                for u in range(4):
                    t = i * 4 + u
                    sp.wait_ge(s["ln1_steps"], (t - 4) * 4 + 4)
                    settled(sp)
                    sp.wait_ge(s["xg_done"], t - 3)
                    settled(sp)
                    sp.dma_start(x_in[u][:, :], x_t[bass.ds(t * P, P), :]).then_inc(x_loaded[u], 16)

            sp.wait_ge(s["table_steps"], TABLES_DONE)
            for k in range(4):
                sp.wait_ge(scattered[k], 16 * GROUPS)
            sp.wait_ge(s["pads_out"], 16 * EXPERTS)

            def load_rows(j, u):
                settled(sp)
                at = sp.value_load(rows_i[0:1, bass.ds(j, 1)], min_val=0, max_val=EXPERTS * REGION - P)
                sp.dma_start(xt[u][:, :], dispatch[bass.ds(at, P), :]).then_inc(xt_loaded[u], 16)
            for u in range(FUNROLL):
                load_rows(u, u)
            with sp.Fori(1, FTILES // FUNROLL) as i:
                for u in range(FUNROLL):
                    sp.wait_ge(s["res_done"], (i - 1) * FUNROLL + u + 1)
                    settled(sp)
                    load_rows(i * FUNROLL + u, u)

        @block.gpsimd
        def _(pool):
            g = nc.gpsimd
            g.memset(proj_bd[:, 0:512], 0.0).then_inc(s["pool_consts"], 1)
            g.memset(proj_bd[:, 512:1024], 0.0).then_inc(s["pool_consts"], 1)
            g.memset(ident[:, :], 0.0).then_inc(s["pool_consts"], 1)
            g.memset(causal[:, :], 1.0).then_inc(s["pool_consts"], 1)
            g.memset(earlier[:, :], 1.0).then_inc(s["pool_consts"], 1)
            g.memset(batch_sel[:, :, :], 0.0).then_inc(s["pool_consts"], 1)
            g.memset(before[:, :, :], 1.0).then_inc(s["pool_consts"], 1)
            g.memset(ones[:, :], 1.0).then_inc(s["pool_consts"], 1)
            pool.wait_ge(s["pool_consts"], 8)
            g.affine_select(out=ident[:, :], in_=ident[:, :], compare_op=ALU.not_equal, fill=1.0, base=0,
                            pattern=[[-1, P]], channel_multiplier=1).then_inc(s["pool_consts"], 1)
            g.affine_select(out=causal[:, :], in_=causal[:, :], compare_op=ALU.is_ge, fill=0.0, base=0,
                            pattern=[[1, P]], channel_multiplier=-1).then_inc(s["pool_consts"], 1)
            g.affine_select(out=earlier[:, :], in_=earlier[:, :], compare_op=ALU.is_gt, fill=0.0, base=0,
                            pattern=[[1, P]], channel_multiplier=-1).then_inc(s["pool_consts"], 1)
            g.affine_select(out=batch_sel[:, :, :], in_=batch_sel[:, :, :], compare_op=ALU.not_equal, fill=1.0,
                            base=0, pattern=[[-1, BATCH], [0, P]], channel_multiplier=1).then_inc(s["pool_consts"], 1)
            g.affine_select(out=before[:, :, :], in_=before[:, :, :], compare_op=ALU.is_gt, fill=0.0, base=0,
                            pattern=[[1, EXPERTS], [-1, EXPERTS]], channel_multiplier=0).then_inc(s["pool_consts"], 1)
            g.iota(iota_i[:, 0:FTILES], pattern=[[1, FTILES]], base=0, channel_multiplier=0).then_inc(s["pool_consts"], 1)
            g.iota(iota_i[:, 80:88], pattern=[[-1, EXPERTS]], base=EXPERTS, channel_multiplier=0).then_inc(s["pool_consts"], 1)
            g.iota(iota_i[:, 88:96], pattern=[[REGION, EXPERTS]], base=0, channel_multiplier=0).then_inc(s["pool_consts"], 1)
            g.iota(iota_i[:, 96:97], pattern=[[1, 1]], base=0, channel_multiplier=1).then_inc(s["pool_consts"], 1)
            g.iota(iota_i[:, 128:128 + TILES], pattern=[[P, TILES]], base=0, channel_multiplier=1).then_inc(s["pool_consts"], 1)
            pool.wait_ge(s["dve_setup"], SETUP_TABLES)
            g.tensor_tensor(ob_g[:, :, :], mod_bc[:, :, 0, :], ob_row[:, None, :].to_broadcast([P, GROUPS, E]),
                            ALU.mult).then_inc(s["pool_setup"], 1)
            pool.wait_ge(s["pool_setup"], 1)

            def step(n, gr, u, exists):
                def grp(k):
                    return gr + (u + k) // 4
                if exists(1):
                    t, k = n + 1, (u + 1) % 4
                    pool.wait_ge(x_loaded[k], 16 * (grp(1) + 1))
                    wait(pool, s["ln2_steps"], 5 * (n - 3) + 1)
                    settled(pool)
                    g.tensor_tensor(xg[:, k, :], x_in[k][:, :], ob_g[:, grp(1), :], ALU.add).then_inc(s["xg_done"], 1)
                if exists(-1):
                    t, k = n - 1, (u - 1) % 4
                    wait(pool, scattered[k], 16 * grp(-1))
                    settled(pool)
                    g.tensor_copy(stage[k][:, COL_G:COL_G + E], mod_bc[:, grp(-1), 3, :]).then_inc(s["payload_done"], 1)
                    g.tensor_copy(stage[k][:, COL_ID:COL_ID + 1], token_no[:, bass.ds(t, 1)]).then_inc(s["payload_done"], 1)
                    wait(pool, s["h_steps"], 2 * t)
                    pool.wait_ge(s["ln2_steps"], 5 * t + 5)
                    settled(pool)
                    g.tensor_tensor(h_tmp[:, :], xn2[:, :], mod_bc[:, grp(-1), 2, :], ALU.mult).then_inc(s["h_steps"], 1)
                    pool.wait_ge(s["h_steps"], 2 * t + 1)
                    settled(pool)
                    g.tensor_tensor(stage[k][:, 0:E], h_tmp[:, :], mod_bc[:, grp(-1), 1, :],
                                    ALU.add).then_inc(s["h_steps"], 1)
                if exists(-3):
                    t, k = n - 3, (u - 3) % 4
                    pool.wait_ge(s["rank_steps"], 4 * t + 4)
                    pool.wait_ge(s["h_steps"], 2 * t + 2)
                    pool.wait_ge(s["payload_done"], 2 * t + 2)
                    pool.wait_ge(s["ln2_steps"], 5 * t + 1)
                    settled(pool)
                    g.indirect_dma_start(out=dispatch[:, :], out_offset=bass.IndirectOffsetOnAxis(ap=slot_i[k][:, 0:1], axis=0),
                                         in_=stage[k][:, :], in_offset=None).then_inc(scattered[k], 16)
            steps(pool, step, FIRST, LAST)

            pool.wait_ge(s["table_steps"], PADS_KNOWN)
            for e in range(EXPERTS):
                g.indirect_dma_start(out=dispatch[:, :], out_offset=bass.IndirectOffsetOnAxis(ap=pad_at[:, e:e + 1], axis=0),
                                     in_=pad_rows[:, :], in_offset=None).then_inc(s["pads_out"], 16)

            def finish(j, u, i):
                wait(pool, stored[u], 16 * i)
                pool.wait_ge(s["y_steps"], 3 * j + 3)
                g.tensor_tensor(res[u][:, :], y2[:, u % 2, :], xt[u][:, COL_X:COL_X + E], ALU.add).then_inc(s["res_done"], 1)
                pool.wait_ge(s["res_done"], j + 1)
                settled(pool)
                g.indirect_dma_start(out=out_rows, out_offset=bass.IndirectOffsetOnAxis(ap=res_i[u][:, 0:1], axis=0),
                                     in_=res[u][:, :], in_offset=None, bounds_check=TOKENS - 1,
                                     oob_is_err=False).then_inc(stored[u], 16)
            for u in range(FUNROLL):
                finish(u, u, 0)
            with pool.Fori(1, FTILES // FUNROLL) as i:
                for u in range(FUNROLL):
                    finish(i * FUNROLL + u, u, i)
            for u in range(FUNROLL):
                pool.wait_ge(stored[u], 16 * (FTILES // FUNROLL))

        @block.scalar
        def _(act):
            a = nc.scalar
            act.wait_ge(s["weights_in"], 16 * N_W)
            a.activation(c_tmp[:, 0, :], c_sb[:, :], ACT.Exp, scale=-1.0).then_inc(s["act_setup"], 1)

            def step(n, gr, u, exists):
                def grp(k):
                    return gr + (u + k) // 4
                if exists(2):
                    t = n + 2
                    act.wait_ge(s["xT_ready"], t + 1)
                    wait(act, s["qkv_ready"], t)
                    b2_ = grp(2)
                    settled(act)
                    a.activation(hT[:, :], m_ps[:, 0:P], ACT.Identity, scale=caT_g(b2_),
                                 bias=saT_g(b2_)).then_inc(s["hT_done"], 1)
                    act.wait_ge(s["qkv_ready"], t + 1)
                    wait(act, s["kf_ready"], 2 * (n + 2 - 2) + 2)
                    a.activation(qkT[:, u % 2, 0, :], m_ps[:, 0:P], ACT.Identity, bias=qb_col[:, 0:1]).then_inc(s["qk_done"], 1)
                    a.activation(qkT[:, u % 2, 1, :], m_ps[:, P:2 * P], ACT.Identity, bias=kb_col[:, 0:1]).then_inc(s["qk_done"], 1)
                if exists(3):
                    act.wait_ge(s["ln1_steps"], 4 * (n + 3) + 2)
                    a.activation(std1[:, 0:1], mv1[:, 1:2], ACT.Sqrt, bias=eps_ln[:, 0:1]).then_inc(s["std1_done"], 1)
                base = 2 * (u + 1)
                if exists(1):
                    t, par = n + 1, (u + 1) % 2
                    wait(act, s["o_ready"], n + 1 - 1)
                    for h in range(2):
                        act.wait_ge(s["q_ready"], 2 * t + h + 1)
                        a.activation(q_blk[par][0:64, 4 * h:4 * h + 4, 0, :],
                                     ring[0:64, (base + 4 + h) % 4, :].rearrange("p (j t) -> p j t", j=4),
                                     ACT.Relu).then_inc(s["q_lo_done"], 1)
                if exists(-1):
                    act.wait_ge(s["onT_ready"], n)
                    wait(act, s["proj_ready"], n - 1)
                    a.activation(onT[:, :], m_ps[:, 0:P], ACT.Copy).then_inc(s["onT_done"], 1)
                if exists(1):
                    t = n + 1
                    wait(act, s["s_ready"], 4 * n + 4)
                    for h in range(2):
                        act.wait_ge(s["k_ready"], 2 * t + h + 1)
                        a.activation(kfT[:, 4 * h:4 * h + 4, :],
                                     ring[:, (base + 6 + h) % 4, :].rearrange("p (j t) -> p j t", j=4),
                                     ACT.Relu).then_inc(s["k_done"], 1)
                if exists(-1):
                    act.wait_ge(s["ln2_steps"], 5 * (n - 1) + 3)
                    a.activation(std2[:, 0:1], mv2[:, 1:2], ACT.Sqrt, bias=eps_ln[:, 0:1]).then_inc(s["std2_done"], 1)
                if exists(-2):
                    act.wait_ge(s["h2T_ready"], n - 1)
                    wait(act, s["gate_ready"], n - 2)
                    a.activation(h2T[:, :], m_ps[:, 0:P], ACT.Copy).then_inc(s["h2T_done"], 1)
                if exists(1):
                    t, par = n + 1, (u + 1) % 2
                    wait(act, s["f_ready"], n + 1 - 1)
                    for h in range(2):
                        act.wait_ge(s["kf_ready"], 2 * t + h + 1)
                        a.activation(kf[par][:, 512 * h:512 * h + 512], ring[:, (base + 8 + h) % 4, :],
                                     ACT.Relu).then_inc(s["kf_done"], 1)

            def caT_g(i):
                return caT[:, :, :].rearrange("p b k -> p (b k)")[:, bass.ds(i, 1)]

            def saT_g(i):
                return saT[:, :, :].rearrange("p b k -> p (b k)")[:, bass.ds(i, 1)]

            act.wait_ge(s["dve_setup"], SETUP_DONE)
            steps(act, step, FIRST, LAST)

            def ffn(m, gr, u, exists):
                if exists(2):
                    act.wait_ge(s["xtT_ready"], m + 3)
                    wait(act, s["hid_ready"], m + 1)
                    a.activation(xtT[:, u % 2, :], m_ps[:, 0:P], ACT.Copy).then_inc(s["xtT_done"], 1)
                if exists(0):
                    act.wait_ge(s["hidT_ready"], m + 1)
                    wait(act, s["y_ready"], m - 1)
                    a.activation(hidT[:, u % 2, :], ring[:, 2 + u % 2, :], ACT.Relu).then_inc(s["hidT_done"], 1)
            ffn_steps(act, ffn)

        @block.vector
        def _(dve):
            v = nc.vector
            count = [0]

            def setup(ins, chained=True):
                count[0] += 1
                ins.then_inc(s["dve_setup"], 1)
                if chained:
                    dve.wait_ge(s["dve_setup"], count[0])

            for k in range(2):
                setup(v.memset(q_blk[k][:, :, :, :], 0.0), False)
                setup(v.memset(state[k][:, :], 0.0), False)
            for k in range(4):
                setup(v.memset(vaug[k][:, 0:HEADS * HW], 1.0), False)
                setup(v.memset(vaug[k][:, HEADS * HW:VW], 0.0), False)
                setup(v.memset(stage[k][:, COL_ID:RW], 0.0), False)
            setup(v.memset(eps_ln[:, :], EPS_LN), False)
            setup(v.memset(pad_rows[:, :], 0.0), False)
            setup(v.memset(lim_hi[:, :], BIG), False)
            setup(v.memset(lim_lo[:, :], -BIG))
            setup(v.memset(pad_rows[:, COL_ID:COL_ID + 1], float(TOKENS)), False)
            setup(v.memset(lim_hi[:, 0:GROUPS:2], 0.0), False)
            setup(v.memset(lim_lo[:, 0:GROUPS:2], 0.0))
            dve.wait_ge(s["pool_consts"], 18)
            setup(v.tensor_copy(tile_no[:, :], iota_i[:, 0:FTILES]), False)
            setup(v.tensor_copy(expert_no[:, :], iota_i[:, 0:EXPERTS]), False)
            setup(v.tensor_copy(expert_rank[:, :], iota_i[:, 80:88]), False)
            setup(v.tensor_copy(region_at[:, :], iota_i[:, 88:96]), False)
            setup(v.tensor_copy(filled[:, :], iota_i[:, 88:96]), False)
            setup(v.tensor_copy(row_no[:, :], iota_i[:, 96:97]), False)
            setup(v.tensor_copy(token_no[:, :], iota_i[:, 128:128 + TILES]), False)
            dve.wait_ge(s["act_setup"], 1)
            setup(v.tensor_tensor(gbias[:, :], gb_row[:, :], eb_row[:, :], ALU.add), False)
            setup(v.tensor_scalar(c_tmp[:, 1, :], c_tmp[:, 0, :], 1.0, None, ALU.add))
            setup(v.reciprocal(c_tmp[:, 2, :], c_tmp[:, 1, :]))
            setup(v.tensor_tensor(c_sb[:, :], c_sb[:, :], c_tmp[:, 2, :], ALU.mult))
            assert count[0] == SETUP_SILU, count[0]
            dve.wait_ge(s["pe_setup"], 2)
            setup(v.tensor_copy(cT[:, :], m_ps[:, 0:BATCH]), False)
            setup(v.tensor_copy(gwT[:, :], m_ps[:, 8:8 + EXPERTS]))
            assert count[0] == SETUP_CT, count[0]
            dve.wait_ge(s["pe_setup"], 4)
            setup(v.tensor_copy(mod_raw[:, 0:3, :], ring[0:BATCH, 0, 0:384].rearrange("p (k e) -> p k e", k=3)), False)
            setup(v.tensor_copy(mod_raw[:, 3:6, :], ring[0:BATCH, 1, 0:384].rearrange("p (k e) -> p k e", k=3)))
            gates = mod_raw[:, 2:6:3, :]
            setup(v.tensor_scalar(mod_tmp[:, 0, :, :], gates, -1.0, None, ALU.mult))
            setup(v.tensor_tensor(mod_tmp[:, 1, :, :], mod_tmp[:, 0, :, :], gates, ALU.max))
            setup(v.tensor_scalar(mod_tmp[:, 0, :, :], mod_tmp[:, 1, :, :], 0.25, None, ALU.max))
            setup(v.tensor_scalar(mod_tmp[:, 1, :, :], gates, 0.0, 2.0, ALU.is_ge, ALU.mult))
            setup(v.tensor_scalar(mod_tmp[:, 2, :, :], mod_tmp[:, 1, :, :], -1.0, None, ALU.add))
            setup(v.tensor_tensor(mod_rows[:, 0:4:3, :], mod_tmp[:, 0, :, :], mod_tmp[:, 2, :, :], ALU.mult), False)
            setup(v.tensor_copy(mod_rows[:, 1, :], mod_raw[:, 3, :]), False)
            setup(v.tensor_scalar(mod_rows[:, 2, :], mod_raw[:, 4, :], 1.0, None, ALU.add), False)
            setup(v.tensor_copy(mod_rows[:, 4, :], mod_raw[:, 0, :]), False)
            setup(v.tensor_scalar(mod_rows[:, 5, :], mod_raw[:, 1, :], 1.0, None, ALU.add))
            assert count[0] == SETUP_ROWS, count[0]
            dve.wait_ge(s["pe_setup"], 5)
            setup(v.tensor_copy(saT[:, :, :], m_ps[:, 16:24][:, :, None].to_broadcast([P, BATCH, 2])), False)
            setup(v.tensor_copy(caT[:, :, :], m_ps[:, 24:32][:, :, None].to_broadcast([P, BATCH, 2])), False)
            for b in range(BATCH):
                dve.wait_ge(s["pe_setup"], 6 + b)
                for k in range(2):
                    setup(v.tensor_copy(mod_bc[:, 2 * b + k, :, :], ring[:, b % 4, :].rearrange("p (k e) -> p k e", k=4)), False)
            dve.wait_ge(s["dve_setup"], count[0])
            assert count[0] == SETUP_TABLES, count[0]
            setup(v.tensor_tensor(wo_g[:, :, :], mod_bc[:, :, 0, :], wo_sb[:, None, :].to_broadcast([P, GROUPS, E]),
                                  ALU.mult))
            assert count[0] == SETUP_DONE, count[0]

            def step(n, gr, u, exists):
                def grp(k):
                    return gr + (u + k) // 4
                base = 2 * (u + 1)

                def mask(k):
                    dve.wait_ge(s["s_ready"], 4 * n + k + 1)
                    v.tensor_tensor(scoresT[:, 4 * k:4 * k + 4, :],
                                    ring[:, (base + k) % 4, :].rearrange("p (j t) -> p j t", j=4),
                                    causal[:, None, :].to_broadcast([P, 4, P]), ALU.mult).then_inc(s["s_masked"], 1)
                if exists(0):
                    wait(dve, s["o_ready"], n)
                    mask(0)
                    mask(1)
                if exists(2):
                    t = n + 2
                    k = (u + 2) % 4
                    dve.wait_ge(s["qk_done"], 2 * t + 2)
                    wait(dve, s["f_ready"], n - 1)
                    v.tensor_tensor(vaug[k][:, 0:HEADS * HW].rearrange("p (h d) -> p h d", h=HEADS)[:, :, 0:HD],
                                    m_ps[:, 2 * P:3 * P].rearrange("p (h d) -> p h d", h=HEADS),
                                    vb_row[:, :].rearrange("p (h d) -> p h d", h=HEADS), ALU.add).then_inc(s["v_done"], 1)
                if exists(0):
                    mask(2)
                    mask(3)
                if exists(3):
                    t, k, par = n + 3, (u + 3) % 4, (u + 3) % 2
                    dve.wait_ge(x_loaded[k], 16 * (grp(3) + 1))
                    v.bn_stats(stats1[:, :], x_in[k][:, :]).then_inc(s["ln1_steps"], 1)
                    dve.wait_ge(s["ln1_steps"], 4 * t + 1)
                    settled(dve)
                    v.bn_aggr(mv1[:, :], stats1[:, :]).then_inc(s["ln1_steps"], 1)
                    dve.wait_ge(s["std1_done"], t + 1)
                    v.reciprocal(std1[:, 1:2], std1[:, 0:1]).then_inc(s["ln1_steps"], 1)
                    dve.wait_ge(s["ln1_steps"], 4 * t + 3)
                    wait(dve, s["xT_ready"], n + 3 - 1)
                    v.tensor_scalar(xn1[:, par, :], x_in[k][:, :], mv1[:, 0:1], std1[:, 1:2],
                                    ALU.subtract, ALU.mult).then_inc(s["ln1_steps"], 1)
                if exists(-1):
                    t = n - 1
                    sums = m_ps[:, :].rearrange("p (h k) -> p h k", h=HEADS)
                    dve.wait_ge(s["oT_ready"], t + 1)
                    wait(dve, s["onT_ready"], n - 1)
                    v.tensor_scalar(den[:, 0, :], sums[:, :, HD], EPS_NORM, None, ALU.add).then_inc(s["norm_steps"], 1)
                    dve.wait_ge(s["norm_steps"], 3 * t + 1)
                    v.reciprocal(den[:, 1, :], den[:, 0, :]).then_inc(s["norm_steps"], 1)
                    dve.wait_ge(s["norm_steps"], 3 * t + 2)
                    v.tensor_tensor(o_n[:, :, :], sums[:, :, 0:HD], den[:, 1, :][:, :, None].to_broadcast([P, HEADS, HD]),
                                    ALU.mult).then_inc(s["norm_steps"], 1)
                if exists(1):
                    t, par = n + 1, (u + 1) % 2
                    wait(dve, s["o_ready"], n)
                    for h in range(2):
                        dve.wait_ge(s["q_ready"], 2 * t + h + 1)
                        v.tensor_scalar(q_blk[par][64:128, 4 * h:4 * h + 4, 1, :],
                                        ring[64:128, (base + 4 + h) % 4, :].rearrange("p (j t) -> p j t", j=4),
                                        0.0, None, ALU.max).then_inc(s["q_hi_done"], 1)
                if exists(-1):
                    t, k = n - 1, (u - 1) % 4
                    dve.wait_ge(s["proj_ready"], t + 1)
                    dve.wait_ge(s["xg_done"], t + 1)
                    wait(dve, scattered[k], 16 * grp(-1))
                    x1 = stage[k][:, COL_X:COL_X + E]
                    v.tensor_tensor(x1, m_ps[:, P:2 * P], xg[:, k, :], ALU.add).then_inc(s["ln2_steps"], 1)
                    dve.wait_ge(s["ln2_steps"], 5 * t + 1)
                    v.bn_stats(stats2[:, :], x1).then_inc(s["ln2_steps"], 1)
                    dve.wait_ge(s["ln2_steps"], 5 * t + 2)
                    settled(dve)
                    v.bn_aggr(mv2[:, :], stats2[:, :]).then_inc(s["ln2_steps"], 1)
                if exists(0):
                    dve.wait_ge(s["o_ready"], n + 1)
                    wait(dve, s["oT_ready"], n - 1)
                    v.tensor_copy(o_sb[u % 2][:, :], o_ps[:, :]).then_inc(s["o_copied"], 1)
                if exists(-1):
                    dve.wait_ge(s["std2_done"], n)
                    v.reciprocal(std2[:, 1:2], std2[:, 0:1]).then_inc(s["ln2_steps"], 1)
                    dve.wait_ge(s["ln2_steps"], 5 * (n - 1) + 4)
                    wait(dve, s["h_steps"], 2 * (n - 2) + 1)
                    v.tensor_scalar(xn2[:, :], stage[(u - 1) % 4][:, COL_X:COL_X + E], mv2[:, 0:1], std2[:, 1:2],
                                    ALU.subtract, ALU.mult).then_inc(s["ln2_steps"], 1)
                if exists(-3):
                    t, k = n - 3, (u - 3) % 4
                    dve.wait_ge(s["rank_ready"], t + 1)
                    if exists(-2):
                        dve.wait_ge(s["gate_ready"], n - 1)
                    wait(dve, s["rank_steps"], 4 * (n - 4) + 2)
                    v.tensor_tensor(pos[:, :], m_ps[:, 400:408], filled[:, :], ALU.add).then_inc(s["rank_steps"], 1)
                    dve.wait_ge(s["rank_steps"], 4 * t + 1)
                    v.tensor_tensor(filled[:, :], m_ps[:, 408:416], filled[:, :], ALU.add).then_inc(s["rank_steps"], 1)
                    dve.wait_ge(s["gate_steps"], 5 * t + 5)
                    v.tensor_tensor_reduce(out=pos_m[:, :], in0=pos[:, :], in1=onehot[:, :], scale=1.0, scalar=0.0,
                                           op0=ALU.mult, op1=ALU.add, accum_out=slot[:, 0:1]).then_inc(s["rank_steps"], 1)
                    dve.wait_ge(s["rank_steps"], 4 * t + 3)
                    wait(dve, scattered[k], 16 * grp(-3))
                    v.tensor_copy(slot_i[k][:, :], slot[:, :]).then_inc(s["rank_steps"], 1)
                if exists(-2):
                    t = n - 2
                    dve.wait_ge(s["gate_ready"], t + 1)
                    v.tensor_tensor(logits[:, :], m_ps[:, 384:392], gbias[:, :], ALU.add).then_inc(s["gate_steps"], 1)
                    dve.wait_ge(s["gate_steps"], 5 * t + 1)
                    v.reduce_max(top[:, :], logits[:, :], AX.X).then_inc(s["gate_steps"], 1)
                    dve.wait_ge(s["gate_steps"], 5 * t + 2)
                    v.scalar_tensor_tensor(out=score[:, :], in0=logits[:, :], scalar=top[:, 0:1], in1=expert_rank[:, :],
                                           op0=ALU.is_equal, op1=ALU.mult).then_inc(s["gate_steps"], 1)
                    dve.wait_ge(s["gate_steps"], 5 * t + 3)
                    v.reduce_max(best[:, :], score[:, :], AX.X).then_inc(s["gate_steps"], 1)
                    dve.wait_ge(s["gate_steps"], 5 * t + 4)
                    v.tensor_scalar(onehot[:, :], expert_rank[:, :], best[:, 0:1], None, ALU.is_equal).then_inc(s["gate_steps"], 1)
                if exists(0):
                    old, new = state[u % 2], state[(u + 1) % 2]
                    done = 9 * gr + 2 * u
                    dve.wait_ge(s["f_ready"], n + 1)
                    wait(dve, s["state_steps"], done)
                    for half in range(2):
                        r = slice(64 * half, 64 * half + 64)
                        v.tensor_tensor(new[r, 0:PAIRS * HW].rearrange("p (b j c) -> p b j c", b=2, j=4),
                                        f_ps[r, :, 0:4 * FW].rearrange("p b (j c) -> p b j c", j=4)[:, :, :, HW * half:HW * half + HW],
                                        old[r, 0:PAIRS * HW].rearrange("p (b j c) -> p b j c", b=2, j=4),
                                        ALU.add).then_inc(s["state_steps"], 1)
                    if u == 3:
                        dve.wait_ge(s["state_steps"], done + 2)
                        v.tensor_scalar(new[:, 0:PAIRS * HW], new[:, 0:PAIRS * HW], lim_hi[:, bass.ds(gr + 1, 1)],
                                        lim_lo[:, bass.ds(gr + 1, 1)], ALU.min, ALU.max).then_inc(s["state_steps"], 1)
            steps(dve, step, FIRST, LAST)

            n_table = [0]

            def table(ins):
                n_table[0] += 1
                ins.then_inc(s["table_steps"], 1)
                dve.wait_ge(s["table_steps"], n_table[0])
            dve.wait_ge(s["rank_steps"], 4 * TILES)
            table(v.tensor_scalar(pad_at[:, :], filled[:, :], row_no[:, 0:1], None, ALU.add))
            assert n_table[0] == PADS_KNOWN
            table(v.tensor_tensor(n_f[:, :], filled[:, :], region_at[:, :], ALU.subtract))
            table(v.tensor_scalar(n_i[:, :], n_f[:, :], float(P - 1), None, ALU.add))
            table(v.tensor_scalar(n_s[:, :], n_i[:, :], 7, None, ALU.logical_shift_right))
            table(v.tensor_copy(n_t[:, :], n_s[:, :]))
            table(v.tensor_tensor(ee[:, :, :], before[:, :, :], n_t[:, None, :].to_broadcast([P, EXPERTS, EXPERTS]), ALU.mult))
            table(v.reduce_sum(t_begin[:, :], ee[:, :, :], AX.X))
            table(v.tensor_tensor(t_end[:, :], t_begin[:, :], n_t[:, :], ALU.add))
            table(v.scalar_tensor_tensor(out=t_off[:, :], in0=t_begin[:, :], scalar=-float(P), in1=region_at[:, :],
                                         op0=ALU.mult, op1=ALU.add))
            tiles_bc = tile_no[:, :, None].to_broadcast([P, FTILES, EXPERTS])

            def over(a):
                return a[:, None, :].to_broadcast([P, FTILES, EXPERTS])
            table(v.tensor_tensor(sel_a[:, :, :], tiles_bc, over(t_begin[:, :]), ALU.is_ge))
            table(v.tensor_tensor(sel_b[:, :, :], tiles_bc, over(t_end[:, :]), ALU.is_lt))
            table(v.tensor_tensor(sel[:, :, :], sel_a[:, :, :], sel_b[:, :, :], ALU.mult))
            table(v.reduce_sum(valid[:, :], sel[:, :, :], AX.X))
            table(v.tensor_tensor(sel_a[:, :, :], sel[:, :, :], over(t_off[:, :]), ALU.mult))
            table(v.reduce_sum(rows_f[:, :], sel_a[:, :, :], AX.X))
            table(v.tensor_tensor(sel_b[:, :, :], sel[:, :, :], over(expert_no[:, :]), ALU.mult))
            table(v.reduce_sum(exps_f[:, :], sel_b[:, :, :], AX.X))
            table(v.scalar_tensor_tensor(out=rows_a[:, :], in0=tile_no[:, :], scalar=float(P), in1=valid[:, :],
                                         op0=ALU.mult, op1=ALU.mult))
            table(v.tensor_tensor(rows_b[:, :], rows_a[:, :], rows_f[:, :], ALU.add))
            table(v.tensor_copy(rows_i[:, :], rows_b[:, :]))
            table(v.tensor_copy(exps_i[:, :], exps_f[:, :]))
            table(v.tensor_scalar(nowhere[:, :], valid[:, :], -NOWHERE, NOWHERE, ALU.mult, ALU.add))
            assert n_table[0] == TABLES_DONE, n_table[0]

            def ffn(m, gr, u, exists):
                if exists(1):
                    e = dve.value_load(exps_i[0:1, bass.ds(m + 1, 1)], min_val=0, max_val=EXPERTS - 1)
                    k = (u + 1) % 2
                    dve.wait_ge(s["hid_ready"], m + 2)
                    wait(dve, s["hidT_ready"], m)
                    v.tensor_tensor(hid[:, k, :], ring[:, k, :], b1_row[:, e, :], ALU.add).then_inc(s["hid_done"], 1)
                if exists(-1):
                    j = m - 1
                    slot_ = (u - 1) % FUNROLL
                    k = slot_ % 2
                    e = dve.value_load(exps_i[0:1, bass.ds(j, 1)], min_val=0, max_val=EXPERTS - 1)
                    turn = gr + (u - 1) // FUNROLL
                    wait(dve, stored[slot_], 16 * turn)
                    v.tensor_scalar(res_i[slot_][:, :], xt[slot_][:, COL_ID:COL_ID + 1], nowhere[:, bass.ds(j, 1)], None,
                                    ALU.add).then_inc(s["res_i_done"], 1)
                    dve.wait_ge(s["y_ready"], j + 1)
                    wait(dve, s["res_done"], j - 1)
                    v.tensor_tensor(y1[:, k, :], y_ps(k), b2_row[:, e, :], ALU.add).then_inc(s["y_steps"], 1)
                    dve.wait_ge(s["y_steps"], 3 * j + 1)
                    dve.wait_ge(s["res_i_done"], j + 1)
                    v.tensor_tensor(y2[:, k, :], y1[:, k, :], xt[slot_][:, COL_G:COL_G + E], ALU.mult).then_inc(s["y_steps"], 2)

            dve.wait_ge(s["ffn_weights_in"], 16 * N_FFN_LOADS)
            ffn_steps(dve, ffn)

        @block.tensor
        def _(pe):
            mm = nc.tensor.matmul

            def tp(dst, src, n_part=P):
                return nc.tensor.transpose(dst, src, ident[0:n_part, 0:n_part])

            pe.wait_ge(s["pool_consts"], 18)
            pe.wait_ge(s["dve_setup"], SETUP_SILU)
            tp(m_ps[:, 0:BATCH], c_sb[:, :], BATCH).then_inc(s["pe_setup"], 1)
            tp(m_ps[:, 8:8 + EXPERTS], gw_nat[:, :], EXPERTS).then_inc(s["pe_setup"], 1)
            pe.wait_ge(s["dve_setup"], SETUP_CT)
            for k in range(2):
                mm(ring[0:BATCH, k, 0:384], cT[:, :], wmod_sb[:, 384 * k:384 * k + 384], start=True, stop=True).then_inc(s["pe_setup"], 1)
            pe.wait_ge(s["dve_setup"], SETUP_ROWS)
            tp(m_ps[:, 16:24], mod_rows[:, 4, :], BATCH)
            tp(m_ps[:, 24:32], mod_rows[:, 5, :], BATCH).then_inc(s["pe_setup"], 1)
            for b in range(BATCH):
                if b >= 4:
                    pe.wait_ge(s["dve_setup"], SETUP_ROWS + 2 + 2 * (b - 3))
                mm(ring[:, b % 4, :], batch_sel[:, b, :], mod_rows[:, 0:4, :], start=True, stop=True).then_inc(s["pe_setup"], 1)
            pe.wait_ge(s["dve_setup"], SETUP_DONE)

            USES = [("xT", 2, [("hT_done", 1, 1)]),
                    ("qkv", 2, [("qk_done", 2, 2), ("v_done", 1, 1)]),
                    ("oT", -1, [("norm_steps", 3, 3)]),
                    ("onT", -1, [("onT_done", 1, 1)]),
                    ("proj", -1, [("ln2_steps", 5, 1)]),
                    ("h2T", -2, [("h2T_done", 1, 1)]),
                    ("rank", -3, [("rank_steps", 4, 2)]),
                    ("gate", -2, [("gate_steps", 5, 1)])]

            def small_bank_free(use, n, exists):
                at = [name for name, _, _ in USES].index(use)
                back = 0
                while True:
                    at -= 1
                    if at < 0:
                        at, back = len(USES) - 1, back + 1
                    name, off, readers = USES[at]
                    if isinstance(n, int) and back > 3:
                        return
                    if exists(off - back):
                        for signal, per_tile, k in readers:
                            wait(pe, s[signal], per_tile * (n - back + off) + k)
                        if name == "gate" and exists(-3 - back):
                            wait(pe, s["rank_steps"], 4 * (n - back - 3) + 2)
                        return

            def step(n, gr, u, exists):
                def grp(k):
                    return gr + (u + k) // 4
                base = 2 * (u + 1)
                if exists(2):
                    t, par = n + 2, u % 2
                    small_bank_free("xT", n, exists)
                    pe.wait_ge(s["ln1_steps"], 4 * t + 4)
                    tp(m_ps[:, 0:P], xn1[:, par, :]).then_inc(s["xT_ready"], 1)

                def scores(k):
                    if k < 2:
                        pe.wait_ge(s["k_done"], 2 * n + k + 1)
                    else:
                        pe.wait_ge(s["kf_done"], 2 * n + k - 1)
                    for j in (2 * k, 2 * k + 1):
                        last = mm(ring[:, (base + k) % 4, 256 * (j % 2):256 * (j % 2) + 256], kfT[:, j, :],
                                  q_blk[u % 2][:, j, :, :], start=True, stop=True)
                    last.then_inc(s["s_ready"], 1)
                if exists(0):
                    pe.wait_ge(s["q_lo_done"], 2 * n + 2)
                    pe.wait_ge(s["q_hi_done"], 2 * n + 2)
                    pe.wait_ge(s["k_done"], 2 * n + 2)
                    scores(0)
                    scores(1)
                if exists(2):
                    t = n + 2
                    pe.wait_ge(s["hT_done"], t + 1)
                    mm(m_ps[:, 0:P], wqkv_sb[:, 0:E], hT[:, :], start=True, stop=True)
                    mm(m_ps[:, P:2 * P], wqkv_sb[:, E:2 * E], hT[:, :], start=True, stop=True)
                    mm(m_ps[:, 2 * P:3 * P], hT[:, :], wqkv_sb[:, 2 * E:3 * E], start=True, stop=True).then_inc(s["qkv_ready"], 1)
                if exists(0):
                    scores(2)
                    scores(3)
                if exists(-1):
                    small_bank_free("oT", n, exists)
                    pe.wait_ge(s["o_copied"], n)
                    for k in range(4):
                        last = tp(m_ps[:, k * P:(k + 1) * P], o_sb[(u - 1) % 2][:, k * P:(k + 1) * P])
                    last.then_inc(s["oT_ready"], 1)

                def features(signal, k, pos, src):
                    for j in range(4 * k, 4 * k + 4):
                        last = mm(ring[:, (base + pos) % 4, P * (j % 4):P * (j % 4) + P], proj_bd[:, P * j:P * j + P],
                                  qkT[:, (u + 1) % 2, src, :], start=True, stop=True)
                    last.then_inc(s[signal], 1)
                if exists(1):
                    t = n + 1
                    pe.wait_ge(s["qk_done"], 2 * t + 2)
                    for k in range(2):
                        wait(pe, s["s_masked"], 4 * n + k + 1)
                        features("q_ready", k, 4 + k, 0)
                if exists(-1):
                    pe.wait_ge(s["norm_steps"], 3 * (n - 1) + 3)
                    tp(m_ps[:, 0:P], o_n[:, :, :].rearrange("p h d -> p (h d)")).then_inc(s["onT_ready"], 1)
                if exists(1):
                    for k in range(2):
                        wait(pe, s["s_masked"], 4 * n + k + 3)
                        features("k_ready", k, 6 + k, 1)
                if exists(-1):
                    pe.wait_ge(s["onT_done"], n)
                    mm(m_ps[:, P:2 * P], onT[:, :], wo_g[:, grp(-1), :], start=True, stop=True).then_inc(s["proj_ready"], 1)
                if exists(0):
                    wait(pe, s["o_copied"], n)
                    wait(pe, s["state_steps"], 9 * gr + 2 * u)
                    pe.wait_ge(s["v_done"], n + 1)
                    pe.wait_ge(s["s_masked"], 4 * n + 4)
                    for G in range(4):
                        for k in range(4):
                            h = 4 * G + k
                            dst = o_ps[32 * k:32 * k + 32, G * P:(G + 1) * P]
                            j = h // 2
                            mm(dst, state[u % 2][:, HW * j:HW * j + 32], q_blk[u % 2][:, j, h % 2, :], start=True, stop=False,
                               tile_position=(0, 32 * k))
                        for k in range(4):
                            h = 4 * G + k
                            dst = o_ps[32 * k:32 * k + 32, G * P:(G + 1) * P]
                            last = mm(dst, vaug[u % 4][:, HW * h:HW * h + 32], scoresT[:, h, :], start=False, stop=True,
                                      tile_position=(0, 32 * k))
                    last.then_inc(s["o_ready"], 1)
                if exists(-2):
                    small_bank_free("h2T", n, exists)
                    pe.wait_ge(s["h_steps"], 2 * (n - 2) + 2)
                    tp(m_ps[:, 0:P], stage[(u - 2) % 4][:, 0:E]).then_inc(s["h2T_ready"], 1)
                if exists(1):
                    t = n + 1
                    for k in range(2):
                        pe.wait_ge(s["q_lo_done"], 2 * t + k + 1)
                        pe.wait_ge(s["q_hi_done"], 2 * t + k + 1)
                        mm(ring[:, (base + 8 + k) % 4, :], qkT[:, (u + 1) % 2, 1, :], proj_bd[:, 512 * k:512 * k + 512],
                           start=True, stop=True).then_inc(s["kf_ready"], 1)
                if exists(-3):
                    if exists(-2):
                        pe.wait_ge(s["h2T_done"], n - 1)
                    else:
                        small_bank_free("rank", n, exists)
                    pe.wait_ge(s["gate_steps"], 5 * (n - 3) + 5)
                    mm(m_ps[:, 400:408], earlier[:, :], onehot[:, :], start=True, stop=True)
                    mm(m_ps[:, 408:416], ones[:, :], onehot[:, :], start=True, stop=True).then_inc(s["rank_ready"], 1)
                if exists(-2):
                    pe.wait_ge(s["h2T_done"], n - 1)
                    mm(m_ps[:, 384:392], h2T[:, :], gwT[:, :], start=True, stop=True).then_inc(s["gate_ready"], 1)
                if exists(0):
                    wait(pe, s["state_steps"], 9 * gr + 2 * u)
                    pe.wait_ge(s["kf_done"], 2 * n + 2)
                    for j in range(PAIRS):
                        last = mm(f_ps[:, j // 4, FW * (j % 4):FW * (j % 4) + FW], kf[u % 2][:, P * j:P * j + P],
                                  vaug[u % 4][:, 2 * HW * j:2 * HW * j + FW], start=True, stop=True)
                    last.then_inc(s["f_ready"], 1)
            steps(pe, step, FIRST, LAST)

            def ffn(m, gr, u, exists):
                if exists(2):
                    wait(pe, s["xtT_done"], m + 2)
                    pe.wait_ge(xt_loaded[(u + 2) % FUNROLL], 16 * (gr + (u + 2) // FUNROLL + 1))
                    tp(m_ps[:, 0:P], xt[(u + 2) % FUNROLL][:, 0:E]).then_inc(s["xtT_ready"], 1)
                if exists(1):
                    e = pe.value_load(exps_i[0:1, bass.ds(m + 1, 1)], min_val=0, max_val=EXPERTS - 1)
                    k = (u + 1) % 2
                    pe.wait_ge(s["xtT_done"], m + 2)
                    wait(pe, s["hid_done"], m)
                    mm(ring[:, k, :], xtT[:, k, :], w1_sb[:, e, :], start=True, stop=True).then_inc(s["hid_ready"], 1)
                if exists(0):
                    pe.wait_ge(s["hid_done"], m + 1)
                    wait(pe, s["hidT_done"], m - 1)
                    for q in range(4):
                        last = tp(ring[:, 2 + u % 2, q * P:(q + 1) * P], hid[:, u % 2, q * P:(q + 1) * P])
                    last.then_inc(s["hidT_ready"], 1)
                if exists(-1):
                    k = (u - 1) % 2
                    e = pe.value_load(exps_i[0:1, bass.ds(m - 1, 1)], min_val=0, max_val=EXPERTS - 1)
                    pe.wait_ge(s["hidT_done"], m)
                    wait(pe, s["y_steps"], 3 * (m - 3) + 1)
                    for q in range(4):
                        last = mm(y_ps(k), hidT[:, k, q * P:(q + 1) * P], w2_sb[:, e, q * E:(q + 1) * E],
                                  start=(q == 0), stop=(q == 3))
                    last.then_inc(s["y_ready"], 1)
            pe.wait_ge(s["table_steps"], TABLES_DONE)
            pe.wait_ge(s["ffn_weights_in"], 16 * N_FFN_LOADS)
            ffn_steps(pe, ffn)


_INS = ["L0_attn_x", "L0_attn_qkv_w", "L0_attn_qkv_b", "L0_attn_out_w", "L0_attn_out_b", "L0_attn_proj",
        "L0_ffn_gate_w", "L0_ffn_gate_b", "L0_ffn_expert_bias", "L0_ffn_w1", "L0_ffn_b1", "L0_ffn_w2", "L0_ffn_b2",
        "L0_c", "L0_wmod"]
_OUT = ((BATCH, SEQ, E), "float32")


def kernel(**inputs):
    import numpy as _np
    import concourse.bacc as _bacc
    from concourse.bass_utils import run_bass_kernel_spmd as _run

    nc = _bacc.Bacc("TRN2", target_bir_lowering=False, num_devices=1)
    arrays, args = {}, []
    for name in _INS:
        a = _np.ascontiguousarray(inputs[name])
        arrays[f"in_{name}"] = a
        args.append(nc.dram_tensor(f"in_{name}", a.shape, mybir.dt.from_np(a.dtype), kind="ExternalInput").ap())
    shape, dtype = _OUT
    args.append(nc.dram_tensor("out_x", shape, mybir.dt.from_np(_np.dtype(dtype)), kind="ExternalOutput").ap())
    adaln_block(nc, *args)
    r = _run(nc, [arrays], core_ids=[0])
    return r.results[0]["out_x"]
```

```python
from contextlib import ExitStack

import concourse.bass as bass
from concourse import mybir

P = 128
BATCH, SEQ, E = 8, 1024, 128
HEADS, HD, FEAT = 16, 8, 64
EXPERTS, DFF = 8, 512
CHUNKS = DFF // P
COL_B1, COL_B2 = DFF, DFF + CHUNKS
WW = COL_B2 + E
TOKENS = BATCH * SEQ
TILES = TOKENS // P
UNROLL = 4
GROUPS = TILES // UNROLL
PER_BATCH = SEQ // P
PAIRS = HEADS // 2
HW = HD + 1
WIN = 32
VH = 2 * HW
VW = HEADS * VH + 8
PARTS = 3
ROWS2 = 2 * HD
SLOT_A, SLOT_W = (0, 1, 2, 0, 1, 0), (0, 0, 0, 1, 1, 2)
STACK = len(SLOT_A) * ROWS2
SW = PAIRS * VH + 16
REGION = TOKENS + P
RW = 400
COL_X, COL_G, COL_ID = E, 2 * E, 3 * E
FTILES = TILES + EXPERTS
FUNROLL = 8
NOWHERE = 16384.0
EPS_LN, EPS_NORM = 1e-5, 1e-6
BIG = 3.0e38

F32 = mybir.dt.float32
BF16 = mybir.dt.bfloat16
I32 = mybir.dt.int32
U32 = mybir.dt.uint32
ALU = mybir.AluOpType
ACT = mybir.ActivationFunctionType
AX = mybir.AxisListType


def wait(eng, sem, value):
    if isinstance(value, int) and value <= 0:
        return
    eng.wait_ge(sem, value)


def adaln_block(nc, x, qkv_w, qkv_b, out_w, out_b, proj, gate_w, gate_b, expert_bias, w1, b1, w2, b2, c, wmod, out):
    ctx = ExitStack()
    with ctx:
        def sb(name, shape, dt=F32):
            return ctx.enter_context(nc.sbuf_tensor(name, shape, dt))

        def pb(name, shape):
            return ctx.enter_context(nc.psum_tensor(name, shape, F32))

        def sem(name):
            return ctx.enter_context(nc.semaphore(name))

        parts_dram = nc.dram_tensor("parts_dram", [2, PAIRS, PARTS, ROWS2, 2 * P], BF16).ap()
        dispatch = nc.dram_tensor("dispatch", [EXPERTS * REGION, RW], F32).ap()

        ident = sb("ident", [P, P])
        causal = sb("causal", [P, P])
        earlier = sb("earlier", [P, P], BF16)
        ones = sb("ones", [P, P], BF16)
        batch_sel = sb("batch_sel", [BATCH, BATCH, P])
        iota_i = sb("iota_i", [P, 256], I32)
        tile_no = sb("tile_no", [P, FTILES])
        expert_no = sb("expert_no", [P, EXPERTS])
        expert_rank = sb("expert_rank", [P, EXPERTS])
        region_at = sb("region_at", [P, EXPERTS])
        before = sb("before", [P, EXPERTS, EXPERTS])
        token_no = sb("token_no", [P, TILES])
        row_no = sb("row_no", [P, 1])
        eps_ln = sb("eps_ln", [P, 1])
        lim_hi = sb("lim_hi", [P, GROUPS + 1])
        lim_lo = sb("lim_lo", [P, GROUPS + 1])
        pad_rows = sb("pad_rows", [P, RW])
        wqkv_sb = sb("wqkv_sb", [P, 3 * E])
        qb_col = sb("qb_col", [P, 1])
        kb_col = sb("kb_col", [P, 1])
        vb_row = sb("vb_row", [P, E])
        ob_row = sb("ob_row", [P, E])
        wo_sb = sb("wo_sb", [P, E])
        proj_st = sb("proj_st", [STACK, PAIRS, P], BF16)
        slot_of_part = sb("slot_of_part", [STACK, PARTS])
        gw_nat = sb("gw_nat", [EXPERTS, E])
        gwT = sb("gwT", [P, EXPERTS])
        gb_row = sb("gb_row", [P, EXPERTS])
        eb_row = sb("eb_row", [P, EXPERTS])
        gbias = sb("gbias", [P, EXPERTS])
        w1_sb = sb("w1_sb", [P, EXPERTS, WW])
        w2_sb = sb("w2_sb", [P, EXPERTS, CHUNKS * E])
        c_sb = sb("c_sb", [BATCH, E])
        c_tmp = sb("c_tmp", [BATCH, 3, E])
        cT = sb("cT", [P, BATCH])
        mod_rows = sb("mod_rows", [BATCH, 6, E])
        mod_bc = sb("mod_bc", [P, GROUPS, 3, E])
        saT = sb("saT", [P, BATCH, 2])
        caT = sb("caT", [P, BATCH, 2])
        wo_g = sb("wo_g", [P, GROUPS, E])
        ob_g = sb("ob_g", [P, GROUPS, E])

        x_in = [sb(f"x_in{k}", [P, E]) for k in range(4)]
        stats1, mv1, std1, xn1 = sb("stats1", [P, 6]), sb("mv1", [P, 2]), sb("std1", [P, 2]), sb("xn1", [P, 2, E])
        hT = sb("hT", [P, P])
        qkT = sb("qkT", [P, 2, 2, P])
        vaug = [sb(f"vaug{k}", [P, VW]) for k in range(4)]
        qfT = [sb(f"qfT{k}", [P, PAIRS, P]) for k in range(2)]
        kf_blk = sb("kf_blk", [P, PAIRS, 2, P])
        kf = [sb(f"kf{k}", [P, HEADS * FEAT]) for k in range(2)]
        scoresT = sb("scoresT", [P, HEADS, P])
        split_r = sb("split_r", [P, 2, P])
        parts = [sb(f"parts{k}", [P, PARTS, 2, P], BF16) for k in range(2)]
        stack = [sb(f"stack{k}", [STACK, PAIRS, 2, P], BF16) for k in range(2)]
        wmod_sb = kf[1][:, 0:6 * E]
        mod_raw = kf[0][0:BATCH, 0:6 * E].rearrange("p (k e) -> p k e", k=6)
        mod_tmp = scoresT[0:BATCH, 0:6, :].rearrange("p (a b) e -> p a b e", a=3)
        proj_f, proj_sum = qfT[0][0:STACK, :, :], qfT[1][0:STACK, :, :]
        state = [sb(f"state{k}", [P, SW]) for k in range(2)]
        state_sum = sb("state_sum", [P, 2, P])
        o_sb = [sb(f"o_sb{k}", [P, 2 * P]) for k in range(2)]
        den, o_n, onT = sb("den", [P, 2, HEADS]), sb("o_n", [P, HEADS, HD]), sb("onT", [P, P])
        xg = sb("xg", [P, 4, E])
        stats2, mv2, std2, xn2 = sb("stats2", [P, 6]), sb("mv2", [P, 2]), sb("std2", [P, 2]), sb("xn2", [P, E])
        h_tmp = sb("h_tmp", [P, E])
        stage = [sb(f"stage{k}", [P, RW]) for k in range(4)]
        h2T = sb("h2T", [P, P])
        logits, top, score, best = sb("logits", [P, EXPERTS]), sb("top", [P, 1]), sb("score", [P, EXPERTS]), sb("best", [P, 1])
        onehot = sb("onehot", [P, EXPERTS], BF16)
        pos, pos_m, slot = sb("pos", [P, EXPERTS]), sb("pos_m", [P, EXPERTS]), sb("slot", [P, 1])
        slot_i = [sb(f"slot_i{k}", [P, 1], U32) for k in range(4)]
        filled = sb("filled", [P, EXPERTS])

        n_f, n_i, n_s = sb("n_f", [P, EXPERTS]), sb("n_i", [P, EXPERTS], I32), sb("n_s", [P, EXPERTS], I32)
        n_t, t_begin, t_end, t_off = (sb(n, [P, EXPERTS]) for n in ("n_t", "t_begin", "t_end", "t_off"))
        ee = sb("ee", [P, EXPERTS, EXPERTS])
        sel_a, sel_b, sel = (kf_blk[:, :, :, :].rearrange("p j h t -> p (j h t)")[:, k * 640:k * 640 + FTILES * EXPERTS]
                             .rearrange("p (j e) -> p j e", e=EXPERTS) for k in range(3))
        valid, rows_f, exps_f, nowhere = (sb(n, [P, FTILES]) for n in ("valid", "rows_f", "exps_f", "nowhere"))
        rows_a, rows_b = sb("rows_a", [P, FTILES]), sb("rows_b", [P, FTILES])
        rows_i, exps_i = sb("rows_i", [P, FTILES], I32), sb("exps_i", [P, FTILES], I32)
        pad_at = sb("pad_at", [P, EXPERTS], U32)
        xt = [sb(f"xt{k}", [P, RW]) for k in range(4)]
        xt += [qfT[k // 2][:, :, :].rearrange("p j t -> p (j t)")[:, (k % 2) * RW:(k % 2 + 1) * RW] for k in range(FUNROLL - 4)]
        xtT = sb("xtT", [P, 2, P])
        w1_now = [kf[k][:, 0:WW] for k in range(2)] + [sb(f"w1_now{k}", [P, WW])[:, :] for k in range(2)]
        hidT = [scoresT[:, CHUNKS * k:CHUNKS * k + CHUNKS, :] for k in range(2)]
        y1, y2 = sb("y1", [P, 2, E]), sb("y2", [P, 2, E])
        res = [kf_blk[:, k, 0, :] for k in range(FUNROLL)]
        res_i = [sb(f"res_i{k}", [P, 1], U32) for k in range(FUNROLL)]

        ring = pb("ring", [P, 4, 512])
        o_ps = pb("o_ps", [P, 512])
        f_ps = pb("f_ps", [P, 2, 512])
        m_ps = pb("m_ps", [P, 512])

        s = {n: sem(n) for n in (
            "waited", "weights_in", "proj_in", "split_act", "split_pool", "parts_out", "stack0", "stack1", "ffn_weights_in", "pool_consts", "dve_setup", "pe_setup", "act_setup", "pool_setup",
            "x_in0", "x_in1", "x_in2", "x_in3", "ln1_steps", "std1_done", "xT_ready", "hT_done", "qkv_ready",
            "qk_done", "v_done", "s_ready", "s_masked", "q_ready", "q_done", "k_ready", "k_lo_done", "k_hi_done",
            "kf_ready", "kf_done", "o_ready", "o_copied", "f_ready", "state_steps", "state_turned", "state_done", "oT_ready", "norm_steps",
            "onT_ready", "onT_done", "proj_ready", "ln2_steps", "std2_done", "xg_done", "h_steps", "payload_done",
            "h2T_ready", "h2T_done", "gate_ready", "gate_steps", "rank_ready", "rank_steps",
            "scat0", "scat1", "scat2", "scat3", "pads_out", "table_steps",
            *(f"xt{k}" for k in range(FUNROLL)), "w1_set", "xtT_ready", "xtT_done", "hid_ready", "hid_lo_done",
            "hid_hi_done", "y_ready", "y_steps", "res_done", "res_i_done", *(f"out{k}" for k in range(FUNROLL)))}
        stacked = [s[f"stack{k}"] for k in range(2)]
        x_loaded = [s[f"x_in{k}"] for k in range(4)]
        scattered = [s[f"scat{k}"] for k in range(4)]
        xt_loaded = [s[f"xt{k}"] for k in range(FUNROLL)]
        stored = [s[f"out{k}"] for k in range(FUNROLL)]

        N_W, N_PROJ = 11, 2 * len(SLOT_A)
        N_FFN_LOADS = 2 + CHUNKS + EXPERTS
        SETUP_ZERO = 2
        SETUP_SILU, SETUP_CT, SETUP_ROWS = 45, 47, 59
        SETUP_DONE = SETUP_ROWS + 2 + 3 * BATCH
        PADS_KNOWN, TABLES_DONE = 1, 22
        x_t = x.rearrange("b (n p) e -> (b n) p e", p=P).rearrange("t p e -> (t p) e")
        out_rows = out.rearrange("b s e -> (b s) e")

        def steps(engine, body, first, last):
            lo, hi = 1, GROUPS - 1
            for n in range(first, lo * UNROLL):
                body(n, n // UNROLL, n % UNROLL, lambda k, n=n: 0 <= n + k < TILES)
            with engine.Fori(lo, hi) as i:
                for u in range(UNROLL):
                    body(i * UNROLL + u, i, u, lambda k: True)
            for n in range(hi * UNROLL, last + 1):
                body(n, n // UNROLL, n % UNROLL, lambda k, n=n: 0 <= n + k < TILES)

        def ffn_steps(engine, body):
            last = FTILES // FUNROLL - 1
            for m in range(-3, FUNROLL):
                body(m, m // FUNROLL, m % FUNROLL, lambda k, m=m: 0 <= m + k < FTILES)
            with engine.Fori(1, last) as i:
                for u in range(FUNROLL):
                    body(i * FUNROLL + u, i, u, lambda k: True)
            for m in range(last * FUNROLL, FTILES + 1):
                body(m, m // FUNROLL, m % FUNROLL, lambda k, m=m: 0 <= m + k < FTILES)

        def y_ps(k):
            return o_ps[:, 0:E] if k == 0 else f_ps[:, 0, 0:E]

        def hid_ps(k, q):
            return ring[:, 2 * k + q // 2, (q % 2) * P:(q % 2 + 1) * P]

        def turn2(n, gr, u):
            return n // 2 + 1 if isinstance(n, int) else 2 * gr + u // 2 + 1

        def settled(eng):
            eng.sem_inc(s["waited"], 1)

        FIRST, LAST = -3, TILES + 2

        block = ctx.enter_context(nc.Block())

        @block.sync
        def _(sp):
            def load(dst, src, signal):
                sp.dma_start(dst, src).then_inc(s[signal], 16)

            load(c_sb[:, :], c, "weights_in")
            load(wmod_sb[:, :], wmod, "weights_in")
            load(wqkv_sb[:, :], qkv_w, "weights_in")
            load(wo_sb[:, :], out_w, "weights_in")
            load(gw_nat[:, :], gate_w, "weights_in")
            load(vb_row[:, :], qkv_b[2 * E:3 * E][None, :].to_broadcast([P, E]), "weights_in")
            load(ob_row[:, :], out_b[None, :].to_broadcast([P, E]), "weights_in")
            load(gb_row[:, :], gate_b[None, :].to_broadcast([P, EXPERTS]), "weights_in")
            load(eb_row[:, :], expert_bias[None, :].to_broadcast([P, EXPERTS]), "weights_in")
            with nc.allow_non_contiguous_dma(reason="bias columns"):
                load(qb_col[:, :], qkv_b[0:E][:, None], "weights_in")
                load(kb_col[:, :], qkv_b[E:2 * E][:, None], "weights_in")
            for t in range(4):
                sp.dma_start(x_in[t][:, :], x_t[t * P:(t + 1) * P, :]).then_inc(x_loaded[t], 16)
            sp.wait_ge(s["dve_setup"], SETUP_ZERO)
            for k in range(len(SLOT_A)):
                for h in range(2):
                    load(proj_f[k * ROWS2 + h * HD:k * ROWS2 + (h + 1) * HD, :, h * FEAT:(h + 1) * FEAT],
                         proj.rearrange("(j h) d m -> h d j m", h=2)[h], "proj_in")
            load(w1_sb[:, :, 0:DFF], w1.rearrange("e d f -> d e f"), "ffn_weights_in")
            for e in range(EXPERTS):
                load(w2_sb[:, e, :].rearrange("p (c d) -> p c d", c=CHUNKS),
                     w2[e, :, :].rearrange("(c p) d -> p c d", p=P), "ffn_weights_in")
            with nc.allow_non_contiguous_dma(reason="bias columns"):
                for q in range(CHUNKS):
                    load(w1_sb[:, :, COL_B1 + q], b1[:, q * P:(q + 1) * P].rearrange("e p -> p e"), "ffn_weights_in")
            load(w1_sb[:, :, COL_B2:WW], b2.rearrange("e f -> (e f)")[None, :].to_broadcast([P, EXPERTS * E])
                 .rearrange("p (e f) -> p e f", e=EXPERTS), "ffn_weights_in")

            def step(n, gr, u, exists):
                t_now = n + 4
                if exists(4) and not (isinstance(n, int) and t_now < 4):
                    sp.wait_ge(s["ln1_steps"], 4 * n + 4)
                    settled(sp)
                    sp.wait_ge(s["xg_done"], n + 1)
                    settled(sp)
                    sp.dma_start(x_in[u][:, :], x_t[bass.ds(t_now * P, P), :]).then_inc(x_loaded[u], 16)
                if exists(2):
                    t, par = n + 2, u % 2
                    wait(sp, stacked[par], turn2(n, gr, u) * 48)
                    for k, (signal, value) in enumerate((("split_act", 2 * t + 1), ("split_act", 2 * t + 2), ("split_pool", 2 * t + 2))):
                        sp.wait_ge(s[signal], value)
                        if k == 0:
                            settled(sp)
                        sp.dma_start(parts_dram[par, :, k, :, :],
                                     parts[par][:, k, :, :].rearrange("p q t -> p (q t)")).then_inc(s["parts_out"], 16)
                    settled(sp)
                    sp.wait_ge(s["parts_out"], 48 * t + 48)
                    settled(sp)
                    wait(sp, s["kf_ready"], 2 * n + 2)
                    for rows, first in ((3, 0), (2, 3), (1, 5)):
                        sp.dma_start(stack[par][first * ROWS2:(first + rows) * ROWS2, :, :, :].rearrange("p j q t -> p j (q t)"),
                                     parts_dram[par, :, 0:rows, :, :].rearrange("j k r c -> (k r) j c")).then_inc(stacked[par], 16)

            steps(sp, step, FIRST, LAST)

            sp.wait_ge(s["table_steps"], TABLES_DONE)
            for k in range(4):
                sp.wait_ge(scattered[k], 16 * GROUPS)
            sp.wait_ge(s["pads_out"], 16 * EXPERTS)

            def load_rows(j, u):
                at = sp.value_load(rows_i[0:1, bass.ds(j, 1)], min_val=0, max_val=EXPERTS * REGION - P)
                sp.dma_start(xt[u][:, :], dispatch[bass.ds(at, P), :]).then_inc(xt_loaded[u], 16)
            for u in range(FUNROLL):
                load_rows(u, u)
            with sp.Fori(1, FTILES // FUNROLL) as i:
                for u in range(FUNROLL):
                    sp.wait_ge(s["res_done"], (i - 1) * FUNROLL + u + 1)
                    settled(sp)
                    sp.wait_ge(s["res_i_done"], (i - 1) * FUNROLL + u + 1)
                    settled(sp)
                    load_rows(i * FUNROLL + u, u)

        @block.gpsimd
        def _(pool):
            g = nc.gpsimd
            g.memset(slot_of_part[:, :], 1.0).then_inc(s["pool_consts"], 1)
            g.memset(ident[:, :], 0.0).then_inc(s["pool_consts"], 1)
            g.memset(causal[:, :], 1.0).then_inc(s["pool_consts"], 1)
            g.memset(earlier[:, :], 1.0).then_inc(s["pool_consts"], 1)
            g.memset(batch_sel[:, :, :], 0.0).then_inc(s["pool_consts"], 1)
            g.memset(before[:, :, :], 1.0).then_inc(s["pool_consts"], 1)
            g.memset(ones[:, :], 1.0).then_inc(s["pool_consts"], 1)
            pool.wait_ge(s["pool_consts"], 7)
            for k, (first, end) in enumerate(((0, 48), (48, 80), (80, 96))):
                g.affine_select(out=slot_of_part[:, k:k + 1], in_=slot_of_part[:, k:k + 1], compare_op=ALU.is_ge, fill=0.0,
                                base=-first, pattern=[[0, 1]], channel_multiplier=1).then_inc(s["pool_consts"], 1)
                pool.wait_ge(s["pool_consts"], 8 + 2 * k)
                g.affine_select(out=slot_of_part[:, k:k + 1], in_=slot_of_part[:, k:k + 1], compare_op=ALU.is_gt, fill=0.0,
                                base=end, pattern=[[0, 1]], channel_multiplier=-1).then_inc(s["pool_consts"], 1)
            g.affine_select(out=ident[:, :], in_=ident[:, :], compare_op=ALU.not_equal, fill=1.0, base=0,
                            pattern=[[-1, P]], channel_multiplier=1).then_inc(s["pool_consts"], 1)
            g.affine_select(out=causal[:, :], in_=causal[:, :], compare_op=ALU.is_ge, fill=0.0, base=0,
                            pattern=[[1, P]], channel_multiplier=-1).then_inc(s["pool_consts"], 1)
            g.affine_select(out=earlier[:, :], in_=earlier[:, :], compare_op=ALU.is_gt, fill=0.0, base=0,
                            pattern=[[1, P]], channel_multiplier=-1).then_inc(s["pool_consts"], 1)
            g.affine_select(out=batch_sel[:, :, :], in_=batch_sel[:, :, :], compare_op=ALU.not_equal, fill=1.0,
                            base=0, pattern=[[-1, BATCH], [0, P]], channel_multiplier=1).then_inc(s["pool_consts"], 1)
            g.affine_select(out=before[:, :, :], in_=before[:, :, :], compare_op=ALU.is_gt, fill=0.0, base=0,
                            pattern=[[1, EXPERTS], [-1, EXPERTS]], channel_multiplier=0).then_inc(s["pool_consts"], 1)
            g.iota(iota_i[:, 0:FTILES], pattern=[[1, FTILES]], base=0, channel_multiplier=0).then_inc(s["pool_consts"], 1)
            g.iota(iota_i[:, 80:88], pattern=[[-1, EXPERTS]], base=EXPERTS, channel_multiplier=0).then_inc(s["pool_consts"], 1)
            g.iota(iota_i[:, 88:96], pattern=[[REGION, EXPERTS]], base=0, channel_multiplier=0).then_inc(s["pool_consts"], 1)
            g.iota(iota_i[:, 96:97], pattern=[[1, 1]], base=0, channel_multiplier=1).then_inc(s["pool_consts"], 1)
            g.iota(iota_i[:, 128:128 + TILES], pattern=[[P, TILES]], base=0, channel_multiplier=1).then_inc(s["pool_consts"], 1)
            pool.wait_ge(s["dve_setup"], SETUP_DONE)

            def step(n, gr, u, exists):
                def grp(k):
                    return gr + (u + k) // 4
                if exists(1):
                    t, k = n + 1, (u + 1) % 4
                    pool.wait_ge(x_loaded[k], 16 * (grp(1) + 1))
                    wait(pool, s["ln2_steps"], 5 * (n - 3) + 1)
                    settled(pool)
                    g.tensor_tensor(xg[:, k, :], x_in[k][:, :], ob_g[:, grp(1), :], ALU.add).then_inc(s["xg_done"], 1)
                if exists(2):
                    t, par = n + 2, u % 2
                    wait(pool, s["split_pool"], 2 * t)
                    pool.wait_ge(s["split_act"], 2 * t + 1)
                    g.tensor_tensor(split_r[:, :, :], qkT[:, par, :, :], parts[par][:, 0, :, :],
                                    ALU.subtract).then_inc(s["split_pool"], 1)
                    pool.wait_ge(s["split_act"], 2 * t + 2)
                    g.tensor_tensor(parts[par][:, 2, :, :], split_r[:, :, :], parts[par][:, 1, :, :],
                                    ALU.subtract).then_inc(s["split_pool"], 1)
                if exists(-1):
                    t, k = n - 1, (u - 1) % 4
                    wait(pool, scattered[k], 16 * grp(-1))
                    settled(pool)
                    g.tensor_copy(stage[k][:, COL_G:COL_G + E], mod_bc[:, grp(-1), 2, :]).then_inc(s["payload_done"], 1)
                    g.tensor_copy(stage[k][:, COL_ID:COL_ID + 1], token_no[:, bass.ds(t, 1)]).then_inc(s["payload_done"], 1)
                    wait(pool, s["h_steps"], 2 * t)
                    pool.wait_ge(s["ln2_steps"], 5 * t + 5)
                    settled(pool)
                    g.tensor_tensor(h_tmp[:, :], xn2[:, :], mod_bc[:, grp(-1), 1, :], ALU.mult).then_inc(s["h_steps"], 1)
                    pool.wait_ge(s["h_steps"], 2 * t + 1)
                    settled(pool)
                    g.tensor_tensor(stage[k][:, 0:E], h_tmp[:, :], mod_bc[:, grp(-1), 0, :],
                                    ALU.add).then_inc(s["h_steps"], 1)
                if exists(-3):
                    t, k = n - 3, (u - 3) % 4
                    pool.wait_ge(s["rank_steps"], 4 * t + 4)
                    pool.wait_ge(s["h_steps"], 2 * t + 2)
                    pool.wait_ge(s["payload_done"], 2 * t + 2)
                    pool.wait_ge(s["ln2_steps"], 5 * t + 1)
                    settled(pool)
                    g.indirect_dma_start(out=dispatch[:, :], out_offset=bass.IndirectOffsetOnAxis(ap=slot_i[k][:, 0:1], axis=0),
                                         in_=stage[k][:, :], in_offset=None).then_inc(scattered[k], 16)
            steps(pool, step, FIRST, LAST)

            pool.wait_ge(s["table_steps"], PADS_KNOWN)
            for e in range(EXPERTS):
                g.indirect_dma_start(out=dispatch[:, :], out_offset=bass.IndirectOffsetOnAxis(ap=pad_at[:, e:e + 1], axis=0),
                                     in_=pad_rows[:, :], in_offset=None).then_inc(s["pads_out"], 16)

            def finish(j, u, i):
                wait(pool, stored[u], 16 * i)
                pool.wait_ge(s["y_steps"], 3 * j + 3)
                g.tensor_tensor(res[u][:, :], y2[:, u % 2, :], xt[u][:, COL_X:COL_X + E], ALU.add).then_inc(s["res_done"], 1)
                pool.wait_ge(s["res_done"], j + 1)
                pool.wait_ge(s["res_i_done"], j + 1)
                settled(pool)
                g.indirect_dma_start(out=out_rows, out_offset=bass.IndirectOffsetOnAxis(ap=res_i[u][:, 0:1], axis=0),
                                     in_=res[u][:, :], in_offset=None, bounds_check=TOKENS - 1,
                                     oob_is_err=False).then_inc(stored[u], 16)
            for u in range(FUNROLL):
                finish(u, u, 0)
            with pool.Fori(1, FTILES // FUNROLL) as i:
                for u in range(FUNROLL):
                    finish(i * FUNROLL + u, u, i)
            for u in range(FUNROLL):
                pool.wait_ge(stored[u], 16 * (FTILES // FUNROLL))

        @block.scalar
        def _(act):
            a = nc.scalar
            act.wait_ge(s["weights_in"], 16 * N_W)
            a.activation(c_tmp[:, 0, :], c_sb[:, :], ACT.Exp, scale=-1.0).then_inc(s["act_setup"], 1)

            def step(n, gr, u, exists):
                def grp(k):
                    return gr + (u + k) // 4
                if exists(2):
                    t = n + 2
                    act.wait_ge(s["xT_ready"], t + 1)
                    wait(act, s["qkv_ready"], t)
                    b2_ = grp(2)
                    settled(act)
                    a.activation(hT[:, :], m_ps[:, 0:P], ACT.Identity, scale=caT_g(b2_),
                                 bias=saT_g(b2_)).then_inc(s["hT_done"], 1)
                    act.wait_ge(s["qkv_ready"], t + 1)
                    wait(act, s["split_pool"], 2 * n + 1)
                    a.activation(qkT[:, u % 2, 0, :], m_ps[:, 0:P], ACT.Identity, bias=qb_col[:, 0:1]).then_inc(s["qk_done"], 1)
                    a.activation(qkT[:, u % 2, 1, :], m_ps[:, P:2 * P], ACT.Identity, bias=kb_col[:, 0:1]).then_inc(s["qk_done"], 1)
                if exists(2):
                    t, par = n + 2, u % 2
                    wait(act, s["parts_out"], 48 * n + 48)
                    act.wait_ge(s["qk_done"], 2 * t + 2)
                    a.activation(parts[par][:, 0, :, :], qkT[:, par, :, :], ACT.Copy).then_inc(s["split_act"], 1)
                if exists(3):
                    act.wait_ge(s["ln1_steps"], 4 * (n + 3) + 2)
                    a.activation(std1[:, 0:1], mv1[:, 1:2], ACT.Sqrt, bias=eps_ln[:, 0:1]).then_inc(s["std1_done"], 1)
                if exists(2):
                    t, par = n + 2, u % 2
                    act.wait_ge(s["split_pool"], 2 * t + 1)
                    a.activation(parts[par][:, 1, :, :], split_r[:, :, :], ACT.Copy).then_inc(s["split_act"], 1)
                base = 2 * (u + 1)
                if exists(1):
                    t, par = n + 1, (u + 1) % 2
                    wait(act, s["o_ready"], n + 1 - 1)
                    for h in range(2):
                        act.wait_ge(s["q_ready"], 2 * t + h + 1)
                        a.activation(qfT[par][:, 4 * h:4 * h + 4, :],
                                     ring[:, (base + 4 + h) % 4, :].rearrange("p (j t) -> p j t", j=4),
                                     ACT.Relu).then_inc(s["q_done"], 1)
                if exists(-1):
                    act.wait_ge(s["onT_ready"], n)
                    wait(act, s["proj_ready"], n - 1)
                    a.activation(onT[:, :], m_ps[:, 0:P], ACT.Copy).then_inc(s["onT_done"], 1)
                if exists(1):
                    t = n + 1
                    wait(act, s["s_ready"], 4 * n + 4)
                    for h in range(2):
                        act.wait_ge(s["k_ready"], 2 * t + h + 1)
                        a.activation(kf_blk[0:FEAT, 4 * h:4 * h + 4, 0, :],
                                     ring[0:FEAT, (base + 6 + h) % 4, :].rearrange("p (j t) -> p j t", j=4),
                                     ACT.Relu).then_inc(s["k_lo_done"], 1)
                if exists(-2):
                    act.wait_ge(s["h2T_ready"], n - 1)
                    wait(act, s["gate_ready"], n - 2)
                    a.activation(h2T[:, :], m_ps[:, 0:P], ACT.Copy).then_inc(s["h2T_done"], 1)
                if exists(-1):
                    act.wait_ge(s["ln2_steps"], 5 * (n - 1) + 3)
                    a.activation(std2[:, 0:1], mv2[:, 1:2], ACT.Sqrt, bias=eps_ln[:, 0:1]).then_inc(s["std2_done"], 1)
                if exists(0):
                    act.wait_ge(s["o_ready"], n + 1)
                    wait(act, s["oT_ready"], n - 1)
                    a.activation(o_sb[u % 2][:, :], o_ps[:, 0:2 * P], ACT.Copy).then_inc(s["o_copied"], 1)
                    act.wait_ge(s["state_turned"], n + 1)
                    turned = f_ps[:, 1, 0:2 * P].rearrange("p (j c) -> p j c", c=WIN)
                    new = state[(u + 1) % 2][:, 0:PAIRS * VH].rearrange("p (j c) -> p j c", c=VH)
                    for h in range(2):
                        a.activation(new[FEAT * h:FEAT * h + FEAT, :, HW * h:HW * h + HW],
                                     turned[FEAT * h:FEAT * h + FEAT, :, VH * h:VH * h + HW],
                                     ACT.Copy).then_inc(s["state_done"], 1)
                if exists(1):
                    t, par = n + 1, (u + 1) % 2
                    wait(act, s["f_ready"], n + 1 - 1)
                    for h in range(2):
                        act.wait_ge(s["kf_ready"], 2 * t + h + 1)
                        a.activation(kf[par][:, 512 * h:512 * h + 512], ring[:, (base + 8 + h) % 4, :],
                                     ACT.Relu).then_inc(s["kf_done"], 1)

            def caT_g(i):
                return caT[:, :, :].rearrange("p b k -> p (b k)")[:, bass.ds(i, 1)]

            def saT_g(i):
                return saT[:, :, :].rearrange("p b k -> p (b k)")[:, bass.ds(i, 1)]

            act.wait_ge(s["dve_setup"], SETUP_DONE)
            steps(act, step, FIRST, LAST)

            def ffn(m, gr, u, exists):
                if exists(3):
                    e = act.value_load(exps_i[0:1, bass.ds(m + 3, 1)], min_val=0, max_val=EXPERTS - 1)
                if exists(2):
                    act.wait_ge(s["xtT_ready"], m + 3)
                    wait(act, s["hid_ready"], m + 1)
                    a.activation(xtT[:, u % 2, :], m_ps[:, 0:P], ACT.Copy).then_inc(s["xtT_done"], 1)
                if exists(1):
                    k = (u + 1) % 2
                    act.wait_ge(s["hid_ready"], m + 2)
                    wait(act, s["y_ready"], m)
                    for q in range(CHUNKS // 2):
                        a.activation(hidT[k][:, q, :], hid_ps(k, q), ACT.Relu,
                                     bias=w1_now[(u + 1) % 4][:, COL_B1 + q:COL_B1 + q + 1]).then_inc(s["hid_lo_done"], 1)
                if exists(3):
                    wait(act, s["y_steps"], 3 * (m - 1) + 1)
                    settled(act)
                    a.activation(w1_now[(u + 3) % 4], w1_sb[:, e, :], ACT.Copy).then_inc(s["w1_set"], 1)
            act.wait_ge(s["table_steps"], TABLES_DONE)
            act.wait_ge(s["ffn_weights_in"], 16 * N_FFN_LOADS)
            ffn_steps(act, ffn)

        @block.vector
        def _(dve):
            v = nc.vector
            count = [0]

            def setup(ins, chained=True):
                count[0] += 1
                ins.then_inc(s["dve_setup"], 1)
                if chained:
                    dve.wait_ge(s["dve_setup"], count[0])

            for k in range(2):
                setup(v.memset(qfT[k][:, :, :], 0.0), False)
            setup(v.memset(kf_blk[:, :, :, :], 0.0), False)
            setup(v.memset(state_sum[:, :, :], 0.0), False)
            for k in range(2):
                setup(v.memset(state[k][:, :], 0.0), False)
            for k in range(4):
                setup(v.memset(vaug[k][:, :], 0.0), False)
                setup(v.memset(stage[k][:, COL_ID:RW], 0.0), False)
            setup(v.memset(eps_ln[:, :], EPS_LN), False)
            setup(v.memset(pad_rows[:, :], 0.0), False)
            setup(v.memset(lim_hi[:, :], BIG), False)
            setup(v.memset(lim_lo[:, :], -BIG))
            setup(v.memset(pad_rows[:, COL_ID:COL_ID + 1], float(TOKENS)), False)
            for k in range(4):
                setup(v.memset(vaug[k][:, 0:HEADS * VH].rearrange("p (h c) -> p h c", c=VH)[:, :, HD:HW], 1.0), False)
            setup(v.memset(lim_hi[:, 0:GROUPS:2], 0.0), False)
            setup(v.memset(lim_lo[:, 0:GROUPS:2], 0.0))
            dve.wait_ge(s["pool_consts"], 23)
            setup(v.tensor_copy(tile_no[:, :], iota_i[:, 0:FTILES]), False)
            setup(v.tensor_copy(expert_no[:, :], iota_i[:, 0:EXPERTS]), False)
            setup(v.tensor_copy(expert_rank[:, :], iota_i[:, 80:88]), False)
            setup(v.tensor_copy(region_at[:, :], iota_i[:, 88:96]), False)
            setup(v.tensor_copy(filled[:, :], iota_i[:, 88:96]), False)
            setup(v.tensor_copy(row_no[:, :], iota_i[:, 96:97]), False)
            setup(v.tensor_copy(token_no[:, :], iota_i[:, 128:128 + TILES]), False)
            dve.wait_ge(s["proj_in"], 16 * N_PROJ)
            setup(v.tensor_copy(proj_st[:, :, :], proj_f))
            setup(v.tensor_tensor(proj_f, proj_f, proj_st[:, :, :], ALU.subtract), False)
            setup(v.tensor_scalar(proj_sum, proj_st[:, :, :], slot_of_part[:, 0:1], None, ALU.mult))
            for k in (1, 2):
                setup(v.tensor_copy(proj_st[:, :, :], proj_f))
                if k == 1:
                    setup(v.tensor_tensor(proj_f, proj_f, proj_st[:, :, :], ALU.subtract), False)
                setup(v.scalar_tensor_tensor(out=proj_sum, in0=proj_st[:, :, :], scalar=slot_of_part[:, k:k + 1],
                                             in1=proj_sum, op0=ALU.mult, op1=ALU.add))
            setup(v.tensor_copy(proj_st[:, :, :], proj_sum))
            dve.wait_ge(s["act_setup"], 1)
            setup(v.tensor_tensor(gbias[:, :], gb_row[:, :], eb_row[:, :], ALU.add), False)
            setup(v.tensor_scalar(c_tmp[:, 1, :], c_tmp[:, 0, :], 1.0, None, ALU.add))
            setup(v.reciprocal(c_tmp[:, 2, :], c_tmp[:, 1, :]))
            setup(v.tensor_tensor(c_sb[:, :], c_sb[:, :], c_tmp[:, 2, :], ALU.mult))
            assert count[0] == SETUP_SILU, count[0]
            dve.wait_ge(s["pe_setup"], 2)
            setup(v.tensor_copy(cT[:, :], m_ps[:, 0:BATCH]), False)
            setup(v.tensor_copy(gwT[:, :], m_ps[:, 8:8 + EXPERTS]))
            assert count[0] == SETUP_CT, count[0]
            dve.wait_ge(s["pe_setup"], 4)
            setup(v.tensor_copy(mod_raw[:, 0:3, :], ring[0:BATCH, 0, 0:384].rearrange("p (k e) -> p k e", k=3)), False)
            setup(v.tensor_copy(mod_raw[:, 3:6, :], ring[0:BATCH, 1, 0:384].rearrange("p (k e) -> p k e", k=3)))
            gates = mod_raw[:, 2:6:3, :]
            setup(v.tensor_scalar(mod_tmp[:, 0, :, :], gates, -1.0, None, ALU.mult))
            setup(v.tensor_tensor(mod_tmp[:, 1, :, :], mod_tmp[:, 0, :, :], gates, ALU.max))
            setup(v.tensor_scalar(mod_tmp[:, 0, :, :], mod_tmp[:, 1, :, :], 0.25, None, ALU.max))
            setup(v.tensor_scalar(mod_tmp[:, 1, :, :], gates, 0.0, 2.0, ALU.is_ge, ALU.mult))
            setup(v.tensor_scalar(mod_tmp[:, 2, :, :], mod_tmp[:, 1, :, :], -1.0, None, ALU.add))
            setup(v.tensor_tensor(mod_rows[:, 0:4:3, :], mod_tmp[:, 0, :, :], mod_tmp[:, 2, :, :], ALU.mult), False)
            setup(v.tensor_copy(mod_rows[:, 1, :], mod_raw[:, 3, :]), False)
            setup(v.tensor_scalar(mod_rows[:, 2, :], mod_raw[:, 4, :], 1.0, None, ALU.add), False)
            setup(v.tensor_copy(mod_rows[:, 4, :], mod_raw[:, 0, :]), False)
            setup(v.tensor_scalar(mod_rows[:, 5, :], mod_raw[:, 1, :], 1.0, None, ALU.add))
            assert count[0] == SETUP_ROWS, count[0]
            dve.wait_ge(s["pe_setup"], 5)
            setup(v.tensor_copy(saT[:, :, :], m_ps[:, 16:24][:, :, None].to_broadcast([P, BATCH, 2])), False)
            setup(v.tensor_copy(caT[:, :, :], m_ps[:, 24:32][:, :, None].to_broadcast([P, BATCH, 2])), False)
            for b in range(BATCH):
                dve.wait_ge(s["pe_setup"], 6 + b)
                two = slice(2 * b, 2 * b + 2)
                rows = ring[:, b % 4, :]
                setup(v.tensor_tensor(wo_g[:, two, :], rows[:, None, 0:E].to_broadcast([P, 2, E]),
                                      wo_sb[:, None, :].to_broadcast([P, 2, E]), ALU.mult), False)
                setup(v.tensor_tensor(ob_g[:, two, :], rows[:, None, 0:E].to_broadcast([P, 2, E]),
                                      ob_row[:, None, :].to_broadcast([P, 2, E]), ALU.mult), False)
                setup(v.tensor_copy(mod_bc[:, two, :, :].rearrange("p g k e -> p g (k e)"),
                                    rows[:, None, E:4 * E].to_broadcast([P, 2, 3 * E])), False)
            dve.wait_ge(s["dve_setup"], count[0])
            assert count[0] == SETUP_DONE, count[0]

            def step(n, gr, u, exists):
                def grp(k):
                    return gr + (u + k) // 4
                base = 2 * (u + 1)

                def mask(k):
                    dve.wait_ge(s["s_ready"], 4 * n + k + 1)
                    v.tensor_tensor(scoresT[:, 4 * k:4 * k + 4, :],
                                    ring[:, (base + k) % 4, :].rearrange("p (j t) -> p j t", j=4),
                                    causal[:, None, :].to_broadcast([P, 4, P]), ALU.mult).then_inc(s["s_masked"], 1)
                def high_keys(k):
                    dve.wait_ge(s["k_ready"], 2 * (n + 1) + k + 1)
                    v.tensor_scalar(kf_blk[FEAT:P, 4 * k:4 * k + 4, 1, :],
                                    ring[FEAT:P, (base + 6 + k) % 4, :].rearrange("p (j t) -> p j t", j=4),
                                    0.0, None, ALU.max).then_inc(s["k_hi_done"], 1)
                if exists(3):
                    t, k = n + 3, (u + 3) % 4
                    dve.wait_ge(x_loaded[k], 16 * (grp(3) + 1))
                    v.bn_stats(stats1[:, :], x_in[k][:, :]).then_inc(s["ln1_steps"], 1)
                    dve.wait_ge(s["ln1_steps"], 4 * t + 1)
                    settled(dve)
                    v.bn_aggr(mv1[:, :], stats1[:, :]).then_inc(s["ln1_steps"], 1)
                if exists(0):
                    wait(dve, s["o_ready"], n)
                    mask(0)
                    mask(1)
                if exists(2):
                    t = n + 2
                    k = (u + 2) % 4
                    dve.wait_ge(s["qk_done"], 2 * t + 2)
                    wait(dve, s["o_ready"], n - 1)
                    v.tensor_tensor(vaug[k][:, 0:HEADS * VH].rearrange("p (h d) -> p h d", h=HEADS)[:, :, 0:HD],
                                    m_ps[:, 2 * P:3 * P].rearrange("p (h d) -> p h d", h=HEADS),
                                    vb_row[:, :].rearrange("p (h d) -> p h d", h=HEADS), ALU.add).then_inc(s["v_done"], 1)
                if exists(0):
                    mask(2)
                    mask(3)
                if exists(-1):
                    t = n - 1
                    sums = m_ps[:, 0:2 * P].rearrange("p (j c) -> p j c", c=WIN)[:, :, 0:VH].rearrange(
                        "p j (h d) -> p j h d", h=2)
                    dve.wait_ge(s["oT_ready"], t + 1)
                    wait(dve, s["onT_ready"], n - 1)
                    v.tensor_scalar(den[:, 0, :].rearrange("p (j h) -> p j h", h=2), sums[:, :, :, HD], EPS_NORM, None, ALU.add).then_inc(s["norm_steps"], 1)
                    dve.wait_ge(s["norm_steps"], 3 * t + 1)
                    v.reciprocal(den[:, 1, :], den[:, 0, :]).then_inc(s["norm_steps"], 1)
                    dve.wait_ge(s["norm_steps"], 3 * t + 2)
                    v.tensor_tensor(o_n[:, :, :].rearrange("p (j h) d -> p j h d", h=2), sums[:, :, :, 0:HD],
                                    den[:, 1, :].rearrange("p (j h) -> p j h", h=2)[:, :, :, None].to_broadcast([P, PAIRS, 2, HD]),
                                    ALU.mult).then_inc(s["norm_steps"], 1)
                if exists(3):
                    t, k, par = n + 3, (u + 3) % 4, (u + 3) % 2
                    dve.wait_ge(s["std1_done"], t + 1)
                    v.reciprocal(std1[:, 1:2], std1[:, 0:1]).then_inc(s["ln1_steps"], 1)
                    dve.wait_ge(s["ln1_steps"], 4 * t + 3)
                    wait(dve, s["xT_ready"], n + 3 - 1)
                    v.tensor_scalar(xn1[:, par, :], x_in[k][:, :], mv1[:, 0:1], std1[:, 1:2],
                                    ALU.subtract, ALU.mult).then_inc(s["ln1_steps"], 1)
                if exists(0):
                    done = 5 * gr + u
                    dve.wait_ge(s["f_ready"], n + 1)
                    wait(dve, s["state_steps"], done)
                    wait(dve, s["state_turned"], n)
                    v.tensor_tensor(state_sum[:, :, :], f_ps[:, 0, 0:2 * P].rearrange("p (a f) -> p a f", a=2),
                                    state_sum[:, :, :], ALU.add).then_inc(s["state_steps"], 1)
                    if u == 3:
                        dve.wait_ge(s["state_steps"], done + 1)
                        v.tensor_scalar(state_sum[:, :, :], state_sum[:, :, :], lim_hi[:, bass.ds(gr + 1, 1)],
                                        lim_lo[:, bass.ds(gr + 1, 1)], ALU.min, ALU.max).then_inc(s["state_steps"], 1)
                if exists(1):
                    t = n + 1
                    wait(dve, s["s_ready"], 4 * n + 4)
                    high_keys(0)
                if exists(-1):
                    t, k = n - 1, (u - 1) % 4
                    dve.wait_ge(s["proj_ready"], t + 1)
                    dve.wait_ge(s["xg_done"], t + 1)
                    wait(dve, scattered[k], 16 * grp(-1))
                    x1 = stage[k][:, COL_X:COL_X + E]
                    v.tensor_tensor(x1, m_ps[:, P:2 * P], xg[:, k, :], ALU.add).then_inc(s["ln2_steps"], 1)
                    dve.wait_ge(s["ln2_steps"], 5 * t + 1)
                    v.bn_stats(stats2[:, :], x1).then_inc(s["ln2_steps"], 1)
                if exists(1):
                    high_keys(1)
                if exists(-1):
                    t = n - 1
                    dve.wait_ge(s["ln2_steps"], 5 * t + 2)
                    settled(dve)
                    v.bn_aggr(mv2[:, :], stats2[:, :]).then_inc(s["ln2_steps"], 1)
                    dve.wait_ge(s["std2_done"], n)
                    v.reciprocal(std2[:, 1:2], std2[:, 0:1]).then_inc(s["ln2_steps"], 1)
                    dve.wait_ge(s["ln2_steps"], 5 * (n - 1) + 4)
                    wait(dve, s["h_steps"], 2 * (n - 2) + 1)
                    v.tensor_scalar(xn2[:, :], stage[(u - 1) % 4][:, COL_X:COL_X + E], mv2[:, 0:1], std2[:, 1:2],
                                    ALU.subtract, ALU.mult).then_inc(s["ln2_steps"], 1)
                if exists(-3):
                    t, k = n - 3, (u - 3) % 4
                    dve.wait_ge(s["rank_ready"], t + 1)
                    if exists(-2):
                        dve.wait_ge(s["gate_ready"], n - 1)
                    wait(dve, s["rank_steps"], 4 * (n - 4) + 2)
                    v.tensor_tensor(pos[:, :], m_ps[:, 400:408], filled[:, :], ALU.add).then_inc(s["rank_steps"], 1)
                    dve.wait_ge(s["rank_steps"], 4 * t + 1)
                    v.tensor_tensor(filled[:, :], m_ps[:, 408:416], filled[:, :], ALU.add).then_inc(s["rank_steps"], 1)
                if exists(-2):
                    t = n - 2
                    dve.wait_ge(s["gate_ready"], t + 1)
                    v.tensor_tensor(logits[:, :], m_ps[:, 384:392], gbias[:, :], ALU.add).then_inc(s["gate_steps"], 1)
                if exists(-3):
                    t, k = n - 3, (u - 3) % 4
                    v.tensor_tensor_reduce(out=pos_m[:, :], in0=pos[:, :], in1=onehot[:, :], scale=1.0, scalar=0.0,
                                           op0=ALU.mult, op1=ALU.add, accum_out=slot[:, 0:1]).then_inc(s["rank_steps"], 1)
                if exists(-2):
                    t = n - 2
                    dve.wait_ge(s["gate_steps"], 5 * t + 1)
                    v.reduce_max(top[:, :], logits[:, :], AX.X).then_inc(s["gate_steps"], 1)
                if exists(-3):
                    t, k = n - 3, (u - 3) % 4
                    dve.wait_ge(s["rank_steps"], 4 * t + 3)
                    wait(dve, scattered[k], 16 * grp(-3))
                    v.tensor_copy(slot_i[k][:, :], slot[:, :]).then_inc(s["rank_steps"], 1)
                if exists(-2):
                    t = n - 2
                    dve.wait_ge(s["gate_steps"], 5 * t + 2)
                    v.scalar_tensor_tensor(out=score[:, :], in0=logits[:, :], scalar=top[:, 0:1], in1=expert_rank[:, :],
                                           op0=ALU.is_equal, op1=ALU.mult).then_inc(s["gate_steps"], 1)
                    dve.wait_ge(s["gate_steps"], 5 * t + 3)
                    v.reduce_max(best[:, :], score[:, :], AX.X).then_inc(s["gate_steps"], 1)
                    dve.wait_ge(s["gate_steps"], 5 * t + 4)
                    v.tensor_scalar(onehot[:, :], expert_rank[:, :], best[:, 0:1], None, ALU.is_equal).then_inc(s["gate_steps"], 1)
            steps(dve, step, FIRST, LAST)

            n_table = [0]

            def table(ins):
                n_table[0] += 1
                ins.then_inc(s["table_steps"], 1)
                dve.wait_ge(s["table_steps"], n_table[0])
            dve.wait_ge(s["rank_steps"], 4 * TILES)
            table(v.tensor_scalar(pad_at[:, :], filled[:, :], row_no[:, 0:1], None, ALU.add))
            assert n_table[0] == PADS_KNOWN
            table(v.tensor_tensor(n_f[:, :], filled[:, :], region_at[:, :], ALU.subtract))
            table(v.tensor_scalar(n_i[:, :], n_f[:, :], float(P - 1), None, ALU.add))
            table(v.tensor_scalar(n_s[:, :], n_i[:, :], 7, None, ALU.logical_shift_right))
            table(v.tensor_copy(n_t[:, :], n_s[:, :]))
            table(v.tensor_tensor(ee[:, :, :], before[:, :, :], n_t[:, None, :].to_broadcast([P, EXPERTS, EXPERTS]), ALU.mult))
            table(v.reduce_sum(t_begin[:, :], ee[:, :, :], AX.X))
            table(v.tensor_tensor(t_end[:, :], t_begin[:, :], n_t[:, :], ALU.add))
            table(v.scalar_tensor_tensor(out=t_off[:, :], in0=t_begin[:, :], scalar=-float(P), in1=region_at[:, :],
                                         op0=ALU.mult, op1=ALU.add))
            tiles_bc = tile_no[:, :, None].to_broadcast([P, FTILES, EXPERTS])

            def over(a):
                return a[:, None, :].to_broadcast([P, FTILES, EXPERTS])
            table(v.tensor_tensor(sel_a[:, :, :], tiles_bc, over(t_begin[:, :]), ALU.is_ge))
            table(v.tensor_tensor(sel_b[:, :, :], tiles_bc, over(t_end[:, :]), ALU.is_lt))
            table(v.tensor_tensor(sel[:, :, :], sel_a[:, :, :], sel_b[:, :, :], ALU.mult))
            table(v.reduce_sum(valid[:, :], sel[:, :, :], AX.X))
            table(v.tensor_tensor(sel_a[:, :, :], sel[:, :, :], over(t_off[:, :]), ALU.mult))
            table(v.reduce_sum(rows_f[:, :], sel_a[:, :, :], AX.X))
            table(v.tensor_tensor(sel_b[:, :, :], sel[:, :, :], over(expert_no[:, :]), ALU.mult))
            table(v.reduce_sum(exps_f[:, :], sel_b[:, :, :], AX.X))
            table(v.scalar_tensor_tensor(out=rows_a[:, :], in0=tile_no[:, :], scalar=float(P), in1=valid[:, :],
                                         op0=ALU.mult, op1=ALU.mult))
            table(v.tensor_tensor(rows_b[:, :], rows_a[:, :], rows_f[:, :], ALU.add))
            table(v.tensor_copy(rows_i[:, :], rows_b[:, :]))
            table(v.tensor_copy(exps_i[:, :], exps_f[:, :]))
            table(v.tensor_scalar(nowhere[:, :], valid[:, :], -NOWHERE, NOWHERE, ALU.mult, ALU.add))
            assert n_table[0] == TABLES_DONE, n_table[0]

            def ffn(m, gr, u, exists):
                j, slot_ = m - 1, (u - 1) % FUNROLL

                def relu(q):
                    dve.wait_ge(s["hid_ready"], m + 2)
                    dve.wait_ge(s["w1_set"], m + 2)
                    wait(dve, s["y_ready"], m)
                    v.tensor_scalar(hidT[(u + 1) % 2][:, q, :], hid_ps((u + 1) % 2, q),
                                    w1_now[(u + 1) % 4][:, COL_B1 + q:COL_B1 + q + 1], 0.0,
                                    ALU.add, ALU.max).then_inc(s["hid_hi_done"], 1)
                if exists(-1):
                    dve.wait_ge(s["y_ready"], j + 1)
                    wait(dve, s["res_done"], j - 1)
                    v.tensor_tensor(y1[:, slot_ % 2, :], y_ps(slot_ % 2), w1_now[slot_ % 4][:, COL_B2:WW], ALU.add).then_inc(s["y_steps"], 1)
                if exists(1):
                    relu(2)
                if exists(-1):
                    dve.wait_ge(s["y_steps"], 3 * j + 1)
                    v.tensor_tensor(y2[:, slot_ % 2, :], y1[:, slot_ % 2, :], xt[slot_][:, COL_G:COL_G + E], ALU.mult).then_inc(s["y_steps"], 2)
                if exists(1):
                    relu(3)
                if exists(-1):
                    wait(dve, stored[slot_], 16 * (gr + (u - 1) // FUNROLL))
                    v.tensor_scalar(res_i[slot_][:, :], xt[slot_][:, COL_ID:COL_ID + 1], nowhere[:, bass.ds(j, 1)], None,
                                    ALU.add).then_inc(s["res_i_done"], 1)

            dve.wait_ge(s["ffn_weights_in"], 16 * N_FFN_LOADS)
            ffn_steps(dve, ffn)

        @block.tensor
        def _(pe):
            mm = nc.tensor.matmul

            def tp(dst, src, n_part=P):
                return nc.tensor.transpose(dst, src, ident[0:n_part, 0:n_part])

            pe.wait_ge(s["pool_consts"], 23)
            pe.wait_ge(s["dve_setup"], SETUP_SILU)
            tp(m_ps[:, 0:BATCH], c_sb[:, :], BATCH).then_inc(s["pe_setup"], 1)
            tp(m_ps[:, 8:8 + EXPERTS], gw_nat[:, :], EXPERTS).then_inc(s["pe_setup"], 1)
            pe.wait_ge(s["dve_setup"], SETUP_CT)
            for k in range(2):
                mm(ring[0:BATCH, k, 0:384], cT[:, :], wmod_sb[:, 384 * k:384 * k + 384], start=True, stop=True).then_inc(s["pe_setup"], 1)
            pe.wait_ge(s["dve_setup"], SETUP_ROWS)
            tp(m_ps[:, 16:24], mod_rows[:, 4, :], BATCH)
            tp(m_ps[:, 24:32], mod_rows[:, 5, :], BATCH).then_inc(s["pe_setup"], 1)
            for b in range(BATCH):
                if b >= 4:
                    pe.wait_ge(s["dve_setup"], SETUP_ROWS + 2 + 3 * (b - 3))
                mm(ring[:, b % 4, :], batch_sel[:, b, :], mod_rows[:, 0:4, :], start=True, stop=True).then_inc(s["pe_setup"], 1)
            pe.wait_ge(s["dve_setup"], SETUP_DONE)

            USES = [("xT", 2, [("hT_done", 1, 1)]),
                    ("qkv", 2, [("qk_done", 2, 2), ("v_done", 1, 1)]),
                    ("oT", -1, [("norm_steps", 3, 3)]),
                    ("onT", -1, [("onT_done", 1, 1)]),
                    ("proj", -1, [("ln2_steps", 5, 1)]),
                    ("h2T", -2, [("h2T_done", 1, 1)]),
                    ("rank", -3, [("rank_steps", 4, 2)]),
                    ("gate", -2, [("gate_steps", 5, 1)])]

            def small_bank_free(use, n, exists):
                at = [name for name, _, _ in USES].index(use)
                back = 0
                while True:
                    at -= 1
                    if at < 0:
                        at, back = len(USES) - 1, back + 1
                    name, off, readers = USES[at]
                    if isinstance(n, int) and back > 3:
                        return
                    if exists(off - back):
                        for signal, per_tile, k in readers:
                            wait(pe, s[signal], per_tile * (n - back + off) + k)
                        if name == "gate" and exists(-3 - back):
                            wait(pe, s["rank_steps"], 4 * (n - back - 3) + 2)
                        return

            def step(n, gr, u, exists):
                def grp(k):
                    return gr + (u + k) // 4
                base = 2 * (u + 1)
                def scores(k, first=0, end=4):
                    if k >= 2:
                        pe.wait_ge(s["kf_done"], 2 * n + k - 1)
                    for h in range(4 * k + first, 4 * k + end):
                        last = mm(ring[:, (base + k) % 4, P * (h % 4):P * (h % 4) + P], kf_blk[:, h // 2, h % 2, :],
                                  qfT[u % 2][:, h // 2, :], start=True, stop=True)
                    if end == 4:
                        last.then_inc(s["s_ready"], 1)
                if exists(0):
                    pe.wait_ge(s["q_done"], 2 * n + 2)
                    pe.wait_ge(s["k_lo_done"], 2 * n + 2)
                    pe.wait_ge(s["k_hi_done"], 2 * n + 2)
                    scores(0)
                if exists(2):
                    t, par = n + 2, u % 2
                    small_bank_free("xT", n, exists)
                    pe.wait_ge(s["ln1_steps"], 4 * t + 4)
                    tp(m_ps[:, 0:P], xn1[:, par, :]).then_inc(s["xT_ready"], 1)
                if exists(0):
                    scores(1)
                    scores(2, 0, 2)
                if exists(2):
                    t = n + 2
                    pe.wait_ge(s["hT_done"], t + 1)
                    mm(m_ps[:, 0:P], wqkv_sb[:, 0:E], hT[:, :], start=True, stop=True)
                    mm(m_ps[:, P:2 * P], wqkv_sb[:, E:2 * E], hT[:, :], start=True, stop=True)
                    mm(m_ps[:, 2 * P:3 * P], hT[:, :], wqkv_sb[:, 2 * E:3 * E], start=True, stop=True).then_inc(s["qkv_ready"], 1)
                if exists(0):
                    scores(2, 2, 4)
                    scores(3)
                if exists(-1):
                    small_bank_free("oT", n, exists)
                    pe.wait_ge(s["o_copied"], n)
                    for k in range(2):
                        last = tp(m_ps[:, k * P:(k + 1) * P], o_sb[(u - 1) % 2][:, k * P:(k + 1) * P])
                    last.then_inc(s["oT_ready"], 1)

                def features(signal, k, pos, src):
                    for j in range(4 * k, 4 * k + 4):
                        last = mm(ring[:, (base + pos) % 4, P * (j % 4):P * (j % 4) + P], proj_st[:, j, :],
                                  stack[(u + 1) % 2][:, j, src, :], start=True, stop=True)
                    last.then_inc(s[signal], 1)
                if exists(1):
                    t = n + 1
                    pe.wait_ge(stacked[(u + 1) % 2], 48 * turn2(n + 1, gr, u + 1))
                    for k in range(2):
                        wait(pe, s["s_masked"], 4 * n + k + 1)
                        features("q_ready", k, 4 + k, 0)

                if exists(0):
                    wait(pe, s["state_steps"], 5 * gr + u)
                    pe.wait_ge(s["v_done"], n + 1)
                    pe.wait_ge(s["kf_done"], 2 * n + 2)
                    for j in range(PAIRS):
                        last = mm(f_ps[WIN * (j % 4):WIN * (j % 4) + WIN, 0, (j // 4) * P:(j // 4 + 1) * P],
                                  vaug[u % 4][:, 2 * VH * j:2 * VH * j + WIN], kf[u % 2][:, P * j:P * j + P],
                                  start=True, stop=True, tile_position=(0, WIN * (j % 4)))
                    last.then_inc(s["f_ready"], 1)
                def key_features(k):
                    wait(pe, s["s_masked"], 4 * n + k + 3)
                    features("k_ready", k, 6 + k, 1)
                if exists(1):
                    key_features(0)
                    key_features(1)
                if exists(-1):
                    pe.wait_ge(s["norm_steps"], 3 * (n - 1) + 3)
                    tp(m_ps[:, 0:P], o_n[:, :, :].rearrange("p h d -> p (h d)")).then_inc(s["onT_ready"], 1)

                def sums(G):
                    def dst(j):
                        return o_ps[WIN * (j % 4):WIN * (j % 4) + WIN, G * P:(G + 1) * P]
                    for j in range(4 * G, 4 * G + 4):
                        mm(dst(j), state[u % 2][:, VH * j:VH * j + WIN], qfT[u % 2][:, j, :], start=True, stop=False,
                           tile_position=(0, WIN * (j % 4)))
                    for h in range(2):
                        wait(pe, s["s_masked"], 4 * n + 2 * G + 2)
                        for j in range(4 * G, 4 * G + 4):
                            at = VH * 2 * j + HW * h
                            last = mm(dst(j), vaug[u % 4][:, at:at + WIN], scoresT[:, 2 * j + h, :], start=False, stop=(h == 1),
                                      tile_position=(0, WIN * (j % 4)))
                    return last
                if exists(0):
                    wait(pe, s["o_copied"], n)
                    wait(pe, s["state_done"], 2 * n)
                    sums(0)
                if exists(-1):
                    pe.wait_ge(s["onT_done"], n)
                    mm(m_ps[:, P:2 * P], onT[:, :], wo_g[:, grp(-1), :], start=True, stop=True).then_inc(s["proj_ready"], 1)
                if exists(0):
                    sums(1).then_inc(s["o_ready"], 1)
                if exists(-2):
                    small_bank_free("h2T", n, exists)
                    pe.wait_ge(s["h_steps"], 2 * (n - 2) + 2)
                    tp(m_ps[:, 0:P], stage[(u - 2) % 4][:, 0:E]).then_inc(s["h2T_ready"], 1)
                if exists(0):
                    pe.wait_ge(s["state_steps"], 5 * gr + u + (2 if u == 3 else 1))
                    wait(pe, s["state_done"], 2 * n)
                    for k in range(2):
                        last = tp(f_ps[:, 1, k * P:(k + 1) * P], state_sum[:, k, :])
                    last.then_inc(s["state_turned"], 1)
                if exists(1):
                    t = n + 1
                    for k in range(2):
                        pe.wait_ge(s["q_done"], 2 * t + k + 1)
                        for j in range(4 * k, 4 * k + 4):
                            last = mm(ring[:, (base + 8 + k) % 4, P * (j % 4):P * (j % 4) + P], stack[(u + 1) % 2][:, j, 1, :],
                                      proj_st[:, j, :], start=True, stop=True)
                        last.then_inc(s["kf_ready"], 1)
                if exists(-3):
                    if exists(-2):
                        pe.wait_ge(s["h2T_done"], n - 1)
                    else:
                        small_bank_free("rank", n, exists)
                    pe.wait_ge(s["gate_steps"], 5 * (n - 3) + 5)
                    mm(m_ps[:, 400:408], earlier[:, :], onehot[:, :], start=True, stop=True)
                    mm(m_ps[:, 408:416], ones[:, :], onehot[:, :], start=True, stop=True).then_inc(s["rank_ready"], 1)
                if exists(-2):
                    pe.wait_ge(s["h2T_done"], n - 1)
                    mm(m_ps[:, 384:392], h2T[:, :], gwT[:, :], start=True, stop=True).then_inc(s["gate_ready"], 1)
            steps(pe, step, FIRST, LAST)

            def ffn(m, gr, u, exists):
                if exists(2):
                    wait(pe, s["xtT_done"], m + 2)
                    pe.wait_ge(xt_loaded[(u + 2) % FUNROLL], 16 * (gr + (u + 2) // FUNROLL + 1))
                    tp(m_ps[:, 0:P], xt[(u + 2) % FUNROLL][:, 0:E]).then_inc(s["xtT_ready"], 1)
                if exists(1):
                    pe.wait_ge(s["xtT_done"], m + 2)
                    pe.wait_ge(s["w1_set"], m + 2)
                    wait(pe, s["hid_lo_done"], CHUNKS // 2 * m)
                    wait(pe, s["hid_hi_done"], CHUNKS // 2 * m)
                    for q in range(CHUNKS):
                        last = mm(hid_ps((u + 1) % 2, q), w1_now[(u + 1) % 4][:, q * P:(q + 1) * P], xtT[:, (u + 1) % 2, :],
                                  start=True, stop=True)
                    last.then_inc(s["hid_ready"], 1)
                if exists(0):
                    e = pe.value_load(exps_i[0:1, bass.ds(m, 1)], min_val=0, max_val=EXPERTS - 1)
                    pe.wait_ge(s["hid_lo_done"], CHUNKS // 2 * (m + 1))
                    pe.wait_ge(s["hid_hi_done"], CHUNKS // 2 * (m + 1))
                    wait(pe, s["y_steps"], 3 * (m - 2) + 1)
                    for q in range(CHUNKS):
                        last = mm(y_ps(u % 2), hidT[u % 2][:, q, :], w2_sb[:, e, q * E:(q + 1) * E],
                                  start=(q == 0), stop=(q == CHUNKS - 1))
                    last.then_inc(s["y_ready"], 1)
            pe.wait_ge(s["table_steps"], TABLES_DONE)
            pe.wait_ge(s["ffn_weights_in"], 16 * N_FFN_LOADS)
            ffn_steps(pe, ffn)


_INS = ["L0_attn_x", "L0_attn_qkv_w", "L0_attn_qkv_b", "L0_attn_out_w", "L0_attn_out_b", "L0_attn_proj",
        "L0_ffn_gate_w", "L0_ffn_gate_b", "L0_ffn_expert_bias", "L0_ffn_w1", "L0_ffn_b1", "L0_ffn_w2", "L0_ffn_b2",
        "L0_c", "L0_wmod"]
_OUT = ((BATCH, SEQ, E), "float32")


def kernel(**inputs):
    import numpy as _np
    import concourse.bacc as _bacc
    from concourse.bass_utils import run_bass_kernel_spmd as _run

    nc = _bacc.Bacc("TRN2", target_bir_lowering=False, num_devices=1)
    arrays, args = {}, []
    for name in _INS:
        a = _np.ascontiguousarray(inputs[name])
        arrays[f"in_{name}"] = a
        args.append(nc.dram_tensor(f"in_{name}", a.shape, mybir.dt.from_np(a.dtype), kind="ExternalInput").ap())
    shape, dtype = _OUT
    args.append(nc.dram_tensor("out_x", shape, mybir.dt.from_np(_np.dtype(dtype)), kind="ExternalOutput").ap())
    adaln_block(nc, *args)
    r = _run(nc, [arrays], core_ids=[0])
    return r.results[0]["out_x"]
```

```python
from contextlib import ExitStack

import concourse.bass as bass
from concourse import mybir

P = 128
BATCH, SEQ, E = 8, 1024, 128
HEADS, HD, FEAT = 16, 8, 64
EXPERTS, DFF = 8, 512
CHUNKS = DFF // P
COL_B1, COL_B2 = DFF, DFF + CHUNKS
WW = COL_B2 + E
TOKENS = BATCH * SEQ
TILES = TOKENS // P
UNROLL = 4
GROUPS = TILES // UNROLL
PER_BATCH = SEQ // P
PAIRS = HEADS // 2
HW = HD + 1
WIN = 32
VH = 2 * HW
VW = HEADS * VH + 8
PARTS = 3
ROWS2 = 2 * HD
SLOT_A, SLOT_W = (0, 1, 2, 0, 1, 0), (0, 0, 0, 1, 1, 2)
STACK = len(SLOT_A) * ROWS2
SW = PAIRS * VH + 16
REGION = TOKENS + P
RW = 400
COL_X, COL_G, COL_ID = E, 2 * E, 3 * E
FTILES = TILES + EXPERTS
FUNROLL = 8
NOWHERE = 16384.0
EPS_LN, EPS_NORM = 1e-5, 1e-6
BIG = 3.0e38

F32 = mybir.dt.float32
BF16 = mybir.dt.bfloat16
I32 = mybir.dt.int32
U32 = mybir.dt.uint32
ALU = mybir.AluOpType
ACT = mybir.ActivationFunctionType
AX = mybir.AxisListType


def wait(eng, sem, value):
    if isinstance(value, int) and value <= 0:
        return
    eng.wait_ge(sem, value)


def adaln_block(nc, x, qkv_w, qkv_b, out_w, out_b, proj, gate_w, gate_b, expert_bias, w1, b1, w2, b2, c, wmod, out):
    ctx = ExitStack()
    with ctx:
        def sb(name, shape, dt=F32):
            return ctx.enter_context(nc.sbuf_tensor(name, shape, dt))

        def pb(name, shape):
            return ctx.enter_context(nc.psum_tensor(name, shape, F32))

        def sem(name):
            return ctx.enter_context(nc.semaphore(name))

        parts_dram = nc.dram_tensor("parts_dram", [2, PAIRS, PARTS, ROWS2, 2 * P], BF16).ap()
        proj_dram = nc.dram_tensor("proj_dram", [PARTS, PAIRS, ROWS2, P], BF16).ap()
        dispatch = nc.dram_tensor("dispatch", [EXPERTS * REGION, RW], F32).ap()

        ident = sb("ident", [P, P])
        causal = sb("causal", [P, P])
        earlier = sb("earlier", [P, P], BF16)
        ones = sb("ones", [P, P], BF16)
        batch_sel = sb("batch_sel", [BATCH, BATCH, P])
        iota_i = sb("iota_i", [P, 256], I32)
        tile_no = sb("tile_no", [P, FTILES])
        expert_rank = sb("expert_rank", [P, EXPERTS])
        region_at = sb("region_at", [P, EXPERTS])
        upto = sb("upto", [P, EXPERTS, EXPERTS])
        token_no = sb("token_no", [P, TILES])
        row_no = sb("row_no", [P, 1])
        eps_ln = sb("eps_ln", [P, 1])
        lim_hi = sb("lim_hi", [P, GROUPS + 1])
        lim_lo = sb("lim_lo", [P, GROUPS + 1])
        pad_rows = sb("pad_rows", [P, RW])
        wqkv_sb = sb("wqkv_sb", [P, 3 * E])
        qb_col = sb("qb_col", [P, 1])
        kb_col = sb("kb_col", [P, 1])
        vb_row = sb("vb_row", [P, E])
        ob_row = sb("ob_row", [P, E])
        wo_sb = sb("wo_sb", [P, E])
        proj_st = sb("proj_st", [STACK, PAIRS, P], BF16)
        proj_nat = sb("proj_nat", [P, 3, FEAT])
        proj_cut = sb("proj_cut", [P, PARTS, FEAT], BF16)
        proj_parts = sb("proj_parts", [P, PARTS, P], BF16)
        head_of_row = sb("head_of_row", [P, HEADS])
        place = sb("place", [P, 2])
        gw_nat = sb("gw_nat", [EXPERTS, E])
        gwT = sb("gwT", [P, EXPERTS])
        gb_row = sb("gb_row", [P, EXPERTS])
        eb_row = sb("eb_row", [P, EXPERTS])
        gbias = sb("gbias", [P, EXPERTS])
        w1_sb = sb("w1_sb", [P, EXPERTS, WW])
        w2_sb = sb("w2_sb", [P, EXPERTS, CHUNKS * E])
        c_sb = sb("c_sb", [BATCH, E])
        c_tmp = sb("c_tmp", [BATCH, 3, E])
        cT = sb("cT", [P, BATCH])
        mod_rows = sb("mod_rows", [BATCH, 6, E])
        mod_bc = sb("mod_bc", [P, GROUPS, 3, E])
        saT = sb("saT", [P, BATCH, 2])
        caT = sb("caT", [P, BATCH, 2])
        wo_g = sb("wo_g", [P, GROUPS, E])
        ob_g = sb("ob_g", [P, GROUPS, E])

        x_in = [sb(f"x_in{k}", [P, E]) for k in range(4)]
        stats1, mv1, std1, xn1 = sb("stats1", [P, 6]), sb("mv1", [P, 2]), sb("std1", [P, 2]), sb("xn1", [P, 2, E])
        hT = sb("hT", [P, P])
        qkT = sb("qkT", [P, 2, 2, P])
        vaug = [sb(f"vaug{k}", [P, VW]) for k in range(4)]
        qfT = [sb(f"qfT{k}", [P, PAIRS, P]) for k in range(2)]
        kf_blk = sb("kf_blk", [P, PAIRS, 2, P])
        kf = [sb(f"kf{k}", [P, HEADS * FEAT]) for k in range(2)]
        scoresT = sb("scoresT", [P, HEADS, P])
        split_r = sb("split_r", [P, 2, P])
        parts = [sb(f"parts{k}", [P, PARTS, 2, P], BF16) for k in range(2)]
        stack = [sb(f"stack{k}", [STACK, PAIRS, 2, P], BF16) for k in range(2)]
        wmod_sb = kf[1][:, 0:6 * E]
        mod_raw = kf[0][0:BATCH, 0:6 * E].rearrange("p (k e) -> p k e", k=6)
        mod_tmp = scoresT[0:BATCH, 0:6, :].rearrange("p (a b) e -> p a b e", a=3)
        state = [sb(f"state{k}", [P, SW]) for k in range(2)]
        state_sum = sb("state_sum", [P, 2, P])
        o_sb = [sb(f"o_sb{k}", [P, 2 * P]) for k in range(2)]
        den, o_n, onT = sb("den", [P, 2, HEADS]), sb("o_n", [P, HEADS, HD]), sb("onT", [P, P])
        xg = sb("xg", [P, 4, E])
        stats2, mv2, std2, xn2 = sb("stats2", [P, 6]), sb("mv2", [P, 2]), sb("std2", [P, 2]), sb("xn2", [P, E])
        h_tmp = sb("h_tmp", [P, E])
        stage = [sb(f"stage{k}", [P, RW]) for k in range(4)]
        h2T = sb("h2T", [P, P])
        logits, top, score, best = sb("logits", [P, EXPERTS]), sb("top", [P, 1]), sb("score", [P, EXPERTS]), sb("best", [P, 1])
        onehot = sb("onehot", [P, EXPERTS], BF16)
        pos, pos_m, slot = sb("pos", [P, EXPERTS]), sb("pos_m", [P, EXPERTS]), sb("slot", [P, 1])
        slot_i = [sb(f"slot_i{k}", [P, 1], U32) for k in range(4)]
        filled = sb("filled", [P, EXPERTS])

        n_f, n_i, n_s = sb("n_f", [P, EXPERTS]), sb("n_i", [P, EXPERTS], I32), sb("n_s", [P, EXPERTS], I32)
        n_t, t_end, t_jump = (sb(n, [P, EXPERTS]) for n in ("n_t", "t_end", "t_jump"))
        ee = sb("ee", [P, EXPERTS, EXPERTS])
        behind, jumps = (kf_blk[:, :, :, :].rearrange("p j h t -> p (j h t)")[:, k * 1024:k * 1024 + FTILES * EXPERTS]
                         .rearrange("p (j e) -> p j e", e=EXPERTS) for k in range(2))
        valid, exps_all, rows_f, rows_a, nowhere = (sb(n, [P, FTILES]) for n in ("valid", "exps_all", "rows_f", "rows_a", "nowhere"))
        rows_i, exps_i = sb("rows_i", [P, FTILES], I32), sb("exps_i", [P, FTILES], I32)
        pad_i = sb("pad_i", [P, EXPERTS], I32)
        pad_at = sb("pad_at", [P, EXPERTS], U32)
        xt = [sb(f"xt{k}", [P, RW]) for k in range(4)]
        xt += [qfT[k // 2][:, :, :].rearrange("p j t -> p (j t)")[:, (k % 2) * RW:(k % 2 + 1) * RW] for k in range(FUNROLL - 4)]
        xtT = sb("xtT", [P, 2, P])
        w1_now = [kf[k][:, 0:WW] for k in range(2)] + [sb(f"w1_now{k}", [P, WW])[:, :] for k in range(2)]
        w2_now = [wo_g[:, :, :].rearrange("p g e -> p (g e)")[:, k * CHUNKS * E:(k + 1) * CHUNKS * E] for k in range(4)]
        hidT = [scoresT[:, CHUNKS * k:CHUNKS * k + CHUNKS, :] for k in range(2)]
        y1, y2 = sb("y1", [P, 2, E]), sb("y2", [P, 2, E])
        res = [kf_blk[:, k, 0, :] for k in range(FUNROLL)]
        res_i = [sb(f"res_i{k}", [P, 1], U32) for k in range(FUNROLL)]

        ring = pb("ring", [P, 4, 512])
        o_ps = pb("o_ps", [P, 512])
        f_ps = pb("f_ps", [P, 2, 512])
        m_ps = pb("m_ps", [P, 512])

        s = {n: sem(n) for n in (
            "waited", "mod_in", "weights_in", "proj_in", "proj_out", "proj_stacked", "spread_ready", "spread_done", "split_act", "split_pool", "parts_out", "stack0", "stack1", "ffn_weights_in", "pool_consts", "dve_setup", "pe_setup", "act_setup", "pool_setup",
            "x_in0", "x_in1", "x_in2", "x_in3", "ln1_steps", "std1_done", "xT_ready", "hT_done", "qkv_ready",
            "qk_done", "v_done", "s_ready", "s_masked", "q_ready", "q_done", "k_ready", "k_act_done", "k_dve_done",
            "kf_ready", "kf_done", "o_ready", "o_copied", "f_ready", "state_steps", "state_turned", "state_done", "oT_ready", "norm_steps",
            "onT_ready", "onT_done", "proj_ready", "ln2_steps", "std2_done", "xg_done", "h_steps", "payload_done",
            "h2T_ready", "h2T_done", "gate_ready", "gate_steps", "rank_ready", "rank_steps",
            "scat0", "scat1", "scat2", "scat3", "pads_out", "pads_out_sp", "pads_out_act", "table_steps",
            *(f"xt{k}" for k in range(FUNROLL)), "w1_set", "w2_set", "xtT_ready", "xtT_done", "hid_ready", "hid_lo_done",
            "hid_hi_done", "y_ready", "y_steps", "res_done", "res_i_done", *(f"out{k}" for k in range(FUNROLL)))}
        stacked = [s[f"stack{k}"] for k in range(2)]
        x_loaded = [s[f"x_in{k}"] for k in range(4)]
        scattered = [s[f"scat{k}"] for k in range(4)]
        xt_loaded = [s[f"xt{k}"] for k in range(FUNROLL)]
        stored = [s[f"out{k}"] for k in range(FUNROLL)]

        IDENT_KNOWN, HEADS_KNOWN, POOL_CONSTS = 8, 10, 20
        N_W = 9
        N_FFN_LOADS = 4 * EXPERTS
        SETUP_SILU, SETUP_CT, SETUP_PROJ, SETUP_ROWS, SETUP_MOD, SETUP_DONE = 11, 12, 20, 32, 35, 56
        SPREAD = {-3: (0,), -2: (1, 2), -1: (3, 4, 5, 6, 7)}
        PAD_I_KNOWN, PADS_KNOWN, ROWS_KNOWN, TABLES_DONE = 1, 2, 21, 25
        PADS_BY_POOL, PADS_BY_SP = range(0, 2), range(2, 5)
        PADS_BY_ACT = range(5, EXPERTS)
        x_t = x.rearrange("b (n p) e -> (b n) p e", p=P).rearrange("t p e -> (t p) e")
        out_rows = out.rearrange("b s e -> (b s) e")

        def steps(engine, body, first, last, lo=1):
            hi = GROUPS - 1
            for n in range(first, lo * UNROLL):
                body(n, n // UNROLL, n % UNROLL, lambda k, n=n: 0 <= n + k < TILES)
            with engine.Fori(lo, hi) as i:
                for u in range(UNROLL):
                    body(i * UNROLL + u, i, u, lambda k: True)
            for n in range(hi * UNROLL, last + 1):
                body(n, n // UNROLL, n % UNROLL, lambda k, n=n: 0 <= n + k < TILES)

        def ffn_steps(engine, body, lo=1):
            last = FTILES // FUNROLL - 1
            for m in range(-3, lo * FUNROLL):
                body(m, m // FUNROLL, m % FUNROLL, lambda k, m=m: 0 <= m + k < FTILES)
            with engine.Fori(lo, last) as i:
                for u in range(FUNROLL):
                    body(i * FUNROLL + u, i, u, lambda k: True)
            for m in range(last * FUNROLL, FTILES + 1):
                body(m, m // FUNROLL, m % FUNROLL, lambda k, m=m: 0 <= m + k < FTILES)

        def y_ps(k):
            return o_ps[:, 0:E] if k == 0 else f_ps[:, 0, 0:E]

        def spread_ps(b):
            return (o_ps[:, :], f_ps[:, 0, :], f_ps[:, 1, :])[b % 3]

        def hid_ps(k, q):
            return ring[:, 2 * k + q // 2, (q % 2) * P:(q % 2 + 1) * P]

        def turn2(n, gr, u):
            return n // 2 + 1 if isinstance(n, int) else 2 * gr + u // 2 + 1

        def settled(eng):
            eng.sem_inc(s["waited"], 1)

        FIRST, LAST = -3, TILES + 2

        block = ctx.enter_context(nc.Block())

        @block.sync
        def _(sp):
            def load(dst, src, signal):
                sp.dma_start(dst, src).then_inc(s[signal], 16)

            def load_x(t):
                sp.dma_start(x_in[t][:, :], x_t[t * P:(t + 1) * P, :]).then_inc(x_loaded[t], 16)

            load(c_sb[:, :], c, "mod_in")
            load(wmod_sb[:, :], wmod, "mod_in")
            load_x(0)
            load(proj_nat[:, 0, :], proj.rearrange("h d m -> (h d) m"), "proj_in")
            load(wqkv_sb[:, :], qkv_w, "weights_in")
            load(gw_nat[:, :], gate_w, "weights_in")
            load(vb_row[:, :], qkv_b[2 * E:3 * E][None, :].to_broadcast([P, E]), "weights_in")
            with nc.allow_non_contiguous_dma(reason="bias columns"):
                load(qb_col[:, :], qkv_b[0:E][:, None], "weights_in")
                load(kb_col[:, :], qkv_b[E:2 * E][:, None], "weights_in")
            load_x(1)
            load(wo_sb[:, :], out_w, "weights_in")
            load(ob_row[:, :], out_b[None, :].to_broadcast([P, E]), "weights_in")
            load(gb_row[:, :], gate_b[None, :].to_broadcast([P, EXPERTS]), "weights_in")
            load(eb_row[:, :], expert_bias[None, :].to_broadcast([P, EXPERTS]), "weights_in")
            load_x(2)
            load_x(3)
            sp.wait_ge(s["dve_setup"], SETUP_PROJ)
            sp.dma_start(proj_dram.rearrange("k j r c -> (j r) k c"), proj_parts[:, :, :]).then_inc(s["proj_out"], 16)
            sp.wait_ge(s["proj_out"], 16)
            for k, part in enumerate(SLOT_W):
                load(proj_st[k * ROWS2:(k + 1) * ROWS2, :, :], proj_dram[part].rearrange("j r c -> r j c"), "proj_stacked")

            def load_experts(es):
                for e in es:
                    load(w1_sb[:, e, 0:DFF], w1[e], "ffn_weights_in")
                    load(w2_sb[:, e, :].rearrange("p (c d) -> p c d", c=CHUNKS),
                         w2[e, :, :].rearrange("(c p) d -> p c d", p=P), "ffn_weights_in")
                    load(w1_sb[:, e, COL_B2:WW], b2[e][None, :].to_broadcast([P, E]), "ffn_weights_in")
                    with nc.allow_non_contiguous_dma(reason="bias columns"):
                        load(w1_sb[:, e, COL_B1:COL_B2], b1[e].rearrange("(c p) -> p c", p=P), "ffn_weights_in")

            def step(n, gr, u, exists):
                t_now = n + 4
                if exists(4) and not (isinstance(n, int) and t_now < 4):
                    sp.wait_ge(s["ln1_steps"], 4 * n + 4)
                    settled(sp)
                    sp.wait_ge(s["xg_done"], n + 1)
                    settled(sp)
                    sp.dma_start(x_in[u][:, :], x_t[bass.ds(t_now * P, P), :]).then_inc(x_loaded[u], 16)
                if exists(2):
                    t, par = n + 2, u % 2
                    wait(sp, stacked[par], turn2(n, gr, u) * 48)
                    for k, (signal, value) in enumerate((("split_act", 2 * t + 1), ("split_act", 2 * t + 2), ("split_pool", 2 * t + 2))):
                        sp.wait_ge(s[signal], value)
                        if k == 0:
                            settled(sp)
                        sp.dma_start(parts_dram[par, :, k, :, :],
                                     parts[par][:, k, :, :].rearrange("p q t -> p (q t)")).then_inc(s["parts_out"], 16)
                    settled(sp)
                    sp.wait_ge(s["parts_out"], 48 * t + 48)
                    settled(sp)
                    wait(sp, s["kf_ready"], 2 * n + 2)
                    for rows, first in ((3, 0), (2, 3), (1, 5)):
                        sp.dma_start(stack[par][first * ROWS2:(first + rows) * ROWS2, :, :, :].rearrange("p j q t -> p j (q t)"),
                                     parts_dram[par, :, 0:rows, :, :].rearrange("j k r c -> (k r) j c")).then_inc(stacked[par], 16)

                if isinstance(n, int) and 0 <= n < UNROLL:
                    load_experts(range(n * EXPERTS // UNROLL, (n + 1) * EXPERTS // UNROLL))

            steps(sp, step, FIRST, LAST)

            sp.wait_ge(s["table_steps"], PAD_I_KNOWN)
            for e in PADS_BY_SP:
                at = sp.value_load(pad_i[0:1, e:e + 1], min_val=0, max_val=EXPERTS * REGION - P)
                sp.dma_start(dispatch[bass.ds(at, P), :], pad_rows[:, :]).then_inc(s["pads_out_sp"], 16)

            sp.wait_ge(s["table_steps"], ROWS_KNOWN)

            def first_row(j):
                return sp.value_load(rows_i[0:1, bass.ds(j, 1)], min_val=0, max_val=EXPERTS * REGION - P)

            def load_rows(at, u):
                sp.dma_start(xt[u][:, :], dispatch[bass.ds(at, P), :]).then_inc(xt_loaded[u], 16)
            begin = [first_row(u) for u in range(4)]
            for k in range(4):
                sp.wait_ge(scattered[k], 16 * GROUPS)
            sp.wait_ge(s["pads_out"], 16 * len(PADS_BY_POOL))
            sp.wait_ge(s["pads_out_sp"], 16 * len(PADS_BY_SP))
            sp.wait_ge(s["pads_out_act"], 16 * len(PADS_BY_ACT))
            for u in range(FUNROLL):
                load_rows(begin[u] if u < 4 else first_row(u), u)
            with sp.Fori(1, FTILES // FUNROLL) as i:
                for u in range(FUNROLL):
                    sp.wait_ge(s["res_done"], (i - 1) * FUNROLL + u + 1)
                    settled(sp)
                    sp.wait_ge(s["res_i_done"], (i - 1) * FUNROLL + u + 1)
                    settled(sp)
                    load_rows(first_row(i * FUNROLL + u), u)

        @block.gpsimd
        def _(pool):
            g = nc.gpsimd
            g.memset(ident[:, :], 0.0).then_inc(s["pool_consts"], 1)
            g.memset(head_of_row[:, :], 1.0).then_inc(s["pool_consts"], 1)
            g.memset(causal[:, :], 1.0).then_inc(s["pool_consts"], 1)
            g.memset(earlier[:, :], 1.0).then_inc(s["pool_consts"], 1)
            g.memset(batch_sel[:, :, :], 0.0).then_inc(s["pool_consts"], 1)
            g.memset(upto[:, :, :], 1.0).then_inc(s["pool_consts"], 1)
            g.memset(ones[:, :], 1.0).then_inc(s["pool_consts"], 1)
            pool.wait_ge(s["pool_consts"], 7)
            g.affine_select(out=ident[:, :], in_=ident[:, :], compare_op=ALU.not_equal, fill=1.0, base=0,
                            pattern=[[-1, P]], channel_multiplier=1).then_inc(s["pool_consts"], 1)
            g.affine_select(out=head_of_row[:, :], in_=head_of_row[:, :], compare_op=ALU.is_ge, fill=0.0,
                            base=0, pattern=[[-HD, HEADS]], channel_multiplier=1).then_inc(s["pool_consts"], 1)
            pool.wait_ge(s["pool_consts"], 9)
            g.affine_select(out=head_of_row[:, :], in_=head_of_row[:, :], compare_op=ALU.is_gt, fill=0.0,
                            base=HD, pattern=[[HD, HEADS]], channel_multiplier=-1).then_inc(s["pool_consts"], 1)
            g.affine_select(out=causal[:, :], in_=causal[:, :], compare_op=ALU.is_ge, fill=0.0, base=0,
                            pattern=[[1, P]], channel_multiplier=-1).then_inc(s["pool_consts"], 1)
            g.affine_select(out=earlier[:, :], in_=earlier[:, :], compare_op=ALU.is_gt, fill=0.0, base=0,
                            pattern=[[1, P]], channel_multiplier=-1).then_inc(s["pool_consts"], 1)
            g.affine_select(out=batch_sel[:, :, :], in_=batch_sel[:, :, :], compare_op=ALU.not_equal, fill=1.0,
                            base=0, pattern=[[-1, BATCH], [0, P]], channel_multiplier=1).then_inc(s["pool_consts"], 1)
            g.affine_select(out=upto[:, :, :], in_=upto[:, :, :], compare_op=ALU.is_ge, fill=0.0, base=0,
                            pattern=[[1, EXPERTS], [-1, EXPERTS]], channel_multiplier=0).then_inc(s["pool_consts"], 1)
            g.iota(iota_i[:, 0:FTILES], pattern=[[1, FTILES]], base=0, channel_multiplier=0).then_inc(s["pool_consts"], 1)
            g.iota(iota_i[:, 80:88], pattern=[[-1, EXPERTS]], base=EXPERTS, channel_multiplier=0).then_inc(s["pool_consts"], 1)
            g.iota(iota_i[:, 88:96], pattern=[[REGION, EXPERTS]], base=0, channel_multiplier=0).then_inc(s["pool_consts"], 1)
            g.iota(iota_i[:, 96:97], pattern=[[1, 1]], base=0, channel_multiplier=1).then_inc(s["pool_consts"], 1)
            g.iota(iota_i[:, 128:128 + TILES], pattern=[[P, TILES]], base=0, channel_multiplier=1).then_inc(s["pool_consts"], 1)
            g.memset(kf_blk[:, :, :, :], 0.0).then_inc(s["pool_consts"], 1)
            pool.wait_ge(s["dve_setup"], SETUP_DONE)

            def step(n, gr, u, exists):
                def grp(k):
                    return gr + (u + k) // 4
                if isinstance(n, int) and n in (-1, 0):
                    pool.wait_ge(s["spread_done"], 3 if n == -1 else 3 * BATCH)
                if exists(1):
                    t, k = n + 1, (u + 1) % 4
                    pool.wait_ge(x_loaded[k], 16 * (grp(1) + 1))
                    wait(pool, s["ln2_steps"], 5 * (n - 3) + 1)
                    settled(pool)
                    g.tensor_tensor(xg[:, k, :], x_in[k][:, :], ob_g[:, grp(1), :], ALU.add).then_inc(s["xg_done"], 1)
                if exists(2):
                    t, par = n + 2, u % 2
                    wait(pool, s["split_pool"], 2 * t)
                    pool.wait_ge(s["split_act"], 2 * t + 1)
                    g.tensor_tensor(split_r[:, :, :], qkT[:, par, :, :], parts[par][:, 0, :, :],
                                    ALU.subtract).then_inc(s["split_pool"], 1)
                    pool.wait_ge(s["split_act"], 2 * t + 2)
                    g.tensor_tensor(parts[par][:, 2, :, :], split_r[:, :, :], parts[par][:, 1, :, :],
                                    ALU.subtract).then_inc(s["split_pool"], 1)
                if exists(-1):
                    t, k = n - 1, (u - 1) % 4
                    wait(pool, scattered[k], 16 * grp(-1))
                    settled(pool)
                    g.tensor_copy(stage[k][:, COL_G:COL_G + E], mod_bc[:, grp(-1), 2, :]).then_inc(s["payload_done"], 1)
                    g.tensor_copy(stage[k][:, COL_ID:COL_ID + 1], token_no[:, bass.ds(t, 1)]).then_inc(s["payload_done"], 1)
                    wait(pool, s["h_steps"], 2 * t)
                    pool.wait_ge(s["ln2_steps"], 5 * t + 5)
                    settled(pool)
                    g.tensor_tensor(h_tmp[:, :], xn2[:, :], mod_bc[:, grp(-1), 1, :], ALU.mult).then_inc(s["h_steps"], 1)
                    pool.wait_ge(s["h_steps"], 2 * t + 1)
                    settled(pool)
                    g.tensor_tensor(stage[k][:, 0:E], h_tmp[:, :], mod_bc[:, grp(-1), 0, :],
                                    ALU.add).then_inc(s["h_steps"], 1)
                if exists(-3):
                    t, k = n - 3, (u - 3) % 4
                    pool.wait_ge(s["rank_steps"], 4 * t + 4)
                    pool.wait_ge(s["h_steps"], 2 * t + 2)
                    pool.wait_ge(s["payload_done"], 2 * t + 2)
                    pool.wait_ge(s["ln2_steps"], 5 * t + 1)
                    settled(pool)
                    g.indirect_dma_start(out=dispatch[:, :], out_offset=bass.IndirectOffsetOnAxis(ap=slot_i[k][:, 0:1], axis=0),
                                         in_=stage[k][:, :], in_offset=None).then_inc(scattered[k], 16)
            steps(pool, step, FIRST, LAST, lo=2)

            pool.wait_ge(s["table_steps"], PADS_KNOWN)
            for e in PADS_BY_POOL:
                g.indirect_dma_start(out=dispatch[:, :], out_offset=bass.IndirectOffsetOnAxis(ap=pad_at[:, e:e + 1], axis=0),
                                     in_=pad_rows[:, :], in_offset=None).then_inc(s["pads_out"], 16)

            def finish(j, u, i):
                wait(pool, stored[u], 16 * i)
                pool.wait_ge(s["y_steps"], 3 * j + 3)
                g.tensor_tensor(res[u][:, :], y2[:, u % 2, :], xt[u][:, COL_X:COL_X + E], ALU.add).then_inc(s["res_done"], 1)
                pool.wait_ge(s["res_done"], j + 1)
                pool.wait_ge(s["res_i_done"], j + 1)
                settled(pool)
                g.indirect_dma_start(out=out_rows, out_offset=bass.IndirectOffsetOnAxis(ap=res_i[u][:, 0:1], axis=0),
                                     in_=res[u][:, :], in_offset=None, bounds_check=TOKENS - 1,
                                     oob_is_err=False).then_inc(stored[u], 16)
            for u in range(FUNROLL):
                finish(u, u, 0)
            with pool.Fori(1, FTILES // FUNROLL) as i:
                for u in range(FUNROLL):
                    finish(i * FUNROLL + u, u, i)
            for u in range(FUNROLL):
                pool.wait_ge(stored[u], 16 * (FTILES // FUNROLL))

        @block.scalar
        def _(act):
            a = nc.scalar
            act.wait_ge(s["mod_in"], 16 * 2)
            a.activation(c_tmp[:, 0, :], c_sb[:, :], ACT.Exp, scale=-1.0).then_inc(s["act_setup"], 1)

            def step(n, gr, u, exists):
                def grp(k):
                    return gr + (u + k) // 4
                if exists(2):
                    t = n + 2
                    act.wait_ge(s["qkv_ready"], t + 1)
                    wait(act, s["split_pool"], 2 * n + 1)
                    a.activation(qkT[:, u % 2, 0, :], m_ps[:, 0:P], ACT.Identity, bias=qb_col[:, 0:1]).then_inc(s["qk_done"], 1)
                    a.activation(qkT[:, u % 2, 1, :], m_ps[:, P:2 * P], ACT.Identity, bias=kb_col[:, 0:1]).then_inc(s["qk_done"], 1)
                    par = u % 2
                    wait(act, s["parts_out"], 48 * n + 48)
                    act.wait_ge(s["qk_done"], 2 * t + 2)
                    a.activation(parts[par][:, 0, :, :], qkT[:, par, :, :], ACT.Copy).then_inc(s["split_act"], 1)
                if exists(3):
                    act.wait_ge(s["ln1_steps"], 4 * (n + 3) + 2)
                    a.activation(std1[:, 0:1], mv1[:, 1:2], ACT.Sqrt, bias=eps_ln[:, 0:1]).then_inc(s["std1_done"], 1)
                if exists(2):
                    t, par = n + 2, u % 2
                    act.wait_ge(s["split_pool"], 2 * t + 1)
                    a.activation(parts[par][:, 1, :, :], split_r[:, :, :], ACT.Copy).then_inc(s["split_act"], 1)
                base = 2 * (u + 1)

                def natural_keys(h):
                    act.wait_ge(s["kf_ready"], 2 * (n + 1) + h + 1)
                    a.activation(kf[(u + 1) % 2][:, 512 * h:512 * h + 512], ring[:, (base + 8 + h) % 4, :],
                                 ACT.Relu).then_inc(s["kf_done"], 1)
                if exists(1):
                    t, par = n + 1, (u + 1) % 2
                    wait(act, s["o_ready"], n)
                    for h in range(2):
                        act.wait_ge(s["q_ready"], 2 * t + h + 1)
                        a.activation(qfT[par][:, 4 * h:4 * h + 4, :],
                                     ring[:, (base + 4 + h) % 4, :].rearrange("p (j t) -> p j t", j=4),
                                     ACT.Relu).then_inc(s["q_done"], 1)
                if exists(-1):
                    act.wait_ge(s["onT_ready"], n)
                    wait(act, s["proj_ready"], n - 1)
                    a.activation(onT[:, :], m_ps[:, 0:P], ACT.Copy).then_inc(s["onT_done"], 1)
                if exists(1):
                    t = n + 1
                    wait(act, s["s_ready"], 4 * n + 4)
                    for h in range(2):
                        act.wait_ge(s["k_ready"], 2 * t + h + 1)
                        a.activation(kf_blk[0:FEAT, 4 * h:4 * h + 4, 0, :],
                                     ring[0:FEAT, (base + 6 + h) % 4, :].rearrange("p (j t) -> p j t", j=4),
                                     ACT.Relu).then_inc(s["k_act_done"], 1)
                    a.activation(kf_blk[FEAT:P, 4:8, 1, :], ring[FEAT:P, (base + 7) % 4, :].rearrange("p (j t) -> p j t", j=4),
                                 ACT.Relu).then_inc(s["k_act_done"], 1)
                if exists(-2):
                    act.wait_ge(s["h2T_ready"], n - 1)
                    wait(act, s["gate_ready"], n - 2)
                    a.activation(h2T[:, :], m_ps[:, 0:P], ACT.Copy).then_inc(s["h2T_done"], 1)
                if exists(-1):
                    act.wait_ge(s["ln2_steps"], 5 * (n - 1) + 3)
                    a.activation(std2[:, 0:1], mv2[:, 1:2], ACT.Sqrt, bias=eps_ln[:, 0:1]).then_inc(s["std2_done"], 1)
                if exists(0):
                    act.wait_ge(s["o_ready"], n + 1)
                    wait(act, s["oT_ready"], n - 1)
                    a.activation(o_sb[u % 2][:, :], o_ps[:, 0:2 * P], ACT.Copy).then_inc(s["o_copied"], 1)
                    act.wait_ge(s["state_turned"], n + 1)
                    turned = f_ps[:, 1, 0:2 * P].rearrange("p (j c) -> p j c", c=WIN)
                    new = state[(u + 1) % 2][:, 0:PAIRS * VH].rearrange("p (j c) -> p j c", c=VH)
                    for h in range(2):
                        a.activation(new[FEAT * h:FEAT * h + FEAT, :, HW * h:HW * h + HW],
                                     turned[FEAT * h:FEAT * h + FEAT, :, VH * h:VH * h + HW],
                                     ACT.Copy).then_inc(s["state_done"], 1)
                if exists(1):
                    wait(act, s["f_ready"], n)
                    natural_keys(0)
                if exists(3):
                    if isinstance(n, int) and n == FIRST:
                        act.wait_ge(s["dve_setup"], SETUP_MOD)
                        act.wait_ge(s["pool_consts"], POOL_CONSTS)
                        act.wait_ge(s["weights_in"], 16 * N_W)
                    act.wait_ge(s["xT_ready"], n + 4)
                    wait(act, s["qkv_ready"], n + 3)
                    settled(act)
                    a.activation(hT[:, :], m_ps[:, 0:P], ACT.Identity, scale=caT_g(grp(3)),
                                 bias=saT_g(grp(3))).then_inc(s["hT_done"], 1)
                if exists(1):
                    natural_keys(1)

            def caT_g(i):
                return caT[:, :, :].rearrange("p b k -> p (b k)")[:, bass.ds(i, 1)]

            def saT_g(i):
                return saT[:, :, :].rearrange("p b k -> p (b k)")[:, bass.ds(i, 1)]

            steps(act, step, FIRST, LAST)

            act.wait_ge(s["table_steps"], PAD_I_KNOWN)
            for e in PADS_BY_ACT:
                at = act.value_load(pad_i[0:1, e:e + 1], min_val=0, max_val=EXPERTS * REGION - P)
                act.dma_start(dispatch[bass.ds(at, P), :], pad_rows[:, :]).then_inc(s["pads_out_act"], 16)

            def ffn(m, gr, u, exists):
                if exists(3):
                    e = act.value_load(exps_i[0:1, bass.ds(m + 3, 1)], min_val=0, max_val=EXPERTS - 1)
                if exists(2):
                    act.wait_ge(s["xtT_ready"], m + 3)
                    wait(act, s["hid_ready"], m + 1)
                    a.activation(xtT[:, u % 2, :], m_ps[:, 0:P], ACT.Copy).then_inc(s["xtT_done"], 1)
                if exists(1):
                    k = (u + 1) % 2
                    act.wait_ge(s["hid_ready"], m + 2)
                    wait(act, s["y_ready"], m)
                    for q in range(CHUNKS // 2):
                        a.activation(hidT[k][:, q, :], hid_ps(k, q), ACT.Relu,
                                     bias=w1_now[(u + 1) % 4][:, COL_B1 + q:COL_B1 + q + 1]).then_inc(s["hid_lo_done"], 1)
                if exists(3):
                    wait(act, s["y_steps"], 3 * (m - 1) + 1)
                    settled(act)
                    a.activation(w1_now[(u + 3) % 4], w1_sb[:, e, :], ACT.Copy).then_inc(s["w1_set"], 1)
            act.wait_ge(s["table_steps"], TABLES_DONE)
            act.wait_ge(s["ffn_weights_in"], 16 * N_FFN_LOADS)
            ffn_steps(act, ffn)

        @block.vector
        def _(dve):
            v = nc.vector
            count = [0]

            def setup(ins, chained=True):
                count[0] += 1
                ins.then_inc(s["dve_setup"], 1)
                if chained:
                    dve.wait_ge(s["dve_setup"], count[0])

            def step(n, gr, u, exists):
                def grp(k):
                    return gr + (u + k) // 4
                base = 2 * (u + 1)

                def mask(k):
                    dve.wait_ge(s["s_ready"], 4 * n + k + 1)
                    v.tensor_tensor(scoresT[:, 4 * k:4 * k + 4, :],
                                    ring[:, (base + k) % 4, :].rearrange("p (j t) -> p j t", j=4),
                                    causal[:, None, :].to_broadcast([P, 4, P]), ALU.mult).then_inc(s["s_masked"], 1)
                if exists(-3):
                    dve.wait_ge(s["gate_steps"], 5 * (n - 3) + 1)
                    v.reduce_max(top[:, :], logits[:, :], AX.X).then_inc(s["gate_steps"], 1)
                if exists(3):
                    t, k = n + 3, (u + 3) % 4
                    dve.wait_ge(x_loaded[k], 16 * (grp(3) + 1))
                    v.bn_stats(stats1[:, :], x_in[k][:, :]).then_inc(s["ln1_steps"], 1)
                if exists(-3):
                    dve.wait_ge(s["gate_steps"], 5 * (n - 3) + 2)
                    v.scalar_tensor_tensor(out=score[:, :], in0=logits[:, :], scalar=top[:, 0:1], in1=expert_rank[:, :],
                                           op0=ALU.is_equal, op1=ALU.mult).then_inc(s["gate_steps"], 1)
                if exists(0):
                    wait(dve, s["o_ready"], n)
                    mask(0)
                if exists(-3):
                    dve.wait_ge(s["gate_steps"], 5 * (n - 3) + 3)
                    v.reduce_max(best[:, :], score[:, :], AX.X).then_inc(s["gate_steps"], 1)
                if exists(3):
                    dve.wait_ge(s["ln1_steps"], 4 * (n + 3) + 1)
                    settled(dve)
                    v.bn_aggr(mv1[:, :], stats1[:, :]).then_inc(s["ln1_steps"], 1)
                if exists(-3):
                    dve.wait_ge(s["gate_steps"], 5 * (n - 3) + 4)
                    v.tensor_scalar(onehot[:, :], expert_rank[:, :], best[:, 0:1], None, ALU.is_equal).then_inc(s["gate_steps"], 1)
                if exists(0):
                    mask(1)
                if exists(2):
                    t, k = n + 2, (u + 2) % 4
                    dve.wait_ge(s["qk_done"], 2 * t + 2)
                    wait(dve, s["o_ready"], n - 1)
                    v.tensor_tensor(vaug[k][:, 0:HEADS * VH].rearrange("p (h d) -> p h d", h=HEADS)[:, :, 0:HD],
                                    m_ps[:, 2 * P:3 * P].rearrange("p (h d) -> p h d", h=HEADS),
                                    vb_row[:, :].rearrange("p (h d) -> p h d", h=HEADS), ALU.add).then_inc(s["v_done"], 1)
                if exists(0):
                    mask(2)
                    mask(3)
                if exists(-1):
                    t = n - 1
                    sums = m_ps[:, 0:2 * P].rearrange("p (j c) -> p j c", c=WIN)[:, :, 0:VH].rearrange(
                        "p j (h d) -> p j h d", h=2)
                    dve.wait_ge(s["oT_ready"], t + 1)
                    wait(dve, s["onT_ready"], n - 1)
                    v.tensor_scalar(den[:, 0, :].rearrange("p (j h) -> p j h", h=2), sums[:, :, :, HD], EPS_NORM, None, ALU.add).then_inc(s["norm_steps"], 1)
                    dve.wait_ge(s["norm_steps"], 3 * t + 1)
                    v.reciprocal(den[:, 1, :], den[:, 0, :]).then_inc(s["norm_steps"], 1)
                    dve.wait_ge(s["norm_steps"], 3 * t + 2)
                    v.tensor_tensor(o_n[:, :, :].rearrange("p (j h) d -> p j h d", h=2), sums[:, :, :, 0:HD],
                                    den[:, 1, :].rearrange("p (j h) -> p j h", h=2)[:, :, :, None].to_broadcast([P, PAIRS, 2, HD]),
                                    ALU.mult).then_inc(s["norm_steps"], 1)
                if exists(3):
                    t, k, par = n + 3, (u + 3) % 4, (u + 3) % 2
                    dve.wait_ge(s["std1_done"], t + 1)
                    v.reciprocal(std1[:, 1:2], std1[:, 0:1]).then_inc(s["ln1_steps"], 1)
                    dve.wait_ge(s["ln1_steps"], 4 * t + 3)
                    wait(dve, s["xT_ready"], n + 3 - 1)
                    v.tensor_scalar(xn1[:, par, :], x_in[k][:, :], mv1[:, 0:1], std1[:, 1:2],
                                    ALU.subtract, ALU.mult).then_inc(s["ln1_steps"], 1)
                if isinstance(n, int) and FIRST < n < 0:
                    spread(n)
                if exists(0):
                    done = 5 * gr + u
                    dve.wait_ge(s["f_ready"], n + 1)
                    wait(dve, s["state_steps"], done)
                    wait(dve, s["state_turned"], n)
                    v.tensor_tensor(state_sum[:, :, :], f_ps[:, 0, 0:2 * P].rearrange("p (a f) -> p a f", a=2),
                                    state_sum[:, :, :], ALU.add).then_inc(s["state_steps"], 1)
                    if u == 3:
                        dve.wait_ge(s["state_steps"], done + 1)
                        v.tensor_scalar(state_sum[:, :, :], state_sum[:, :, :], lim_hi[:, bass.ds(gr + 1, 1)],
                                        lim_lo[:, bass.ds(gr + 1, 1)], ALU.min, ALU.max).then_inc(s["state_steps"], 1)
                if exists(1):
                    t = n + 1
                    wait(dve, s["s_ready"], 4 * n + 4)
                    dve.wait_ge(s["k_ready"], 2 * t + 1)
                    v.tensor_scalar(kf_blk[FEAT:P, 0:4, 1, :], ring[FEAT:P, (base + 6) % 4, :].rearrange("p (j t) -> p j t", j=4),
                                    0.0, None, ALU.max).then_inc(s["k_dve_done"], 1)
                if exists(-1):
                    t, k = n - 1, (u - 1) % 4
                    dve.wait_ge(s["proj_ready"], t + 1)
                    dve.wait_ge(s["xg_done"], t + 1)
                    wait(dve, scattered[k], 16 * grp(-1))
                    x1 = stage[k][:, COL_X:COL_X + E]
                    v.tensor_tensor(x1, m_ps[:, P:2 * P], xg[:, k, :], ALU.add).then_inc(s["ln2_steps"], 1)
                    dve.wait_ge(s["ln2_steps"], 5 * t + 1)
                    v.bn_stats(stats2[:, :], x1).then_inc(s["ln2_steps"], 1)
                    dve.wait_ge(s["ln2_steps"], 5 * t + 2)
                    settled(dve)
                    v.bn_aggr(mv2[:, :], stats2[:, :]).then_inc(s["ln2_steps"], 1)
                    dve.wait_ge(s["std2_done"], n)
                    v.reciprocal(std2[:, 1:2], std2[:, 0:1]).then_inc(s["ln2_steps"], 1)
                    dve.wait_ge(s["ln2_steps"], 5 * (n - 1) + 4)
                    wait(dve, s["h_steps"], 2 * (n - 2) + 1)
                    v.tensor_scalar(xn2[:, :], stage[(u - 1) % 4][:, COL_X:COL_X + E], mv2[:, 0:1], std2[:, 1:2],
                                    ALU.subtract, ALU.mult).then_inc(s["ln2_steps"], 1)
                if exists(-3):
                    t = n - 3
                    dve.wait_ge(s["rank_ready"], t + 1)
                    if exists(-2):
                        dve.wait_ge(s["gate_ready"], n - 1)
                    wait(dve, s["rank_steps"], 4 * (n - 4) + 2)
                    v.tensor_tensor(pos[:, :], f_ps[:, 0, 400:408], filled[:, :], ALU.add).then_inc(s["rank_steps"], 1)
                    dve.wait_ge(s["rank_steps"], 4 * t + 1)
                    v.tensor_tensor(filled[:, :], f_ps[:, 0, 408:416], filled[:, :], ALU.add).then_inc(s["rank_steps"], 1)
                if isinstance(n, int) and n == LAST:
                    dve.wait_ge(s["rank_steps"], 4 * t + 2)
                    v.tensor_copy(pad_i[:, :], filled[:, :]).then_inc(s["table_steps"], 1)
                    v.tensor_scalar(pad_at[:, :], filled[:, :], row_no[:, 0:1], None, ALU.add).then_inc(s["table_steps"], 1)
                if exists(-2):
                    dve.wait_ge(s["gate_ready"], n - 1)
                    v.tensor_tensor(logits[:, :], f_ps[:, 0, 384:392], gbias[:, :], ALU.add).then_inc(s["gate_steps"], 1)
                if exists(-3):
                    t, k = n - 3, (u - 3) % 4
                    v.tensor_tensor_reduce(out=pos_m[:, :], in0=pos[:, :], in1=onehot[:, :], scale=1.0, scalar=0.0,
                                           op0=ALU.mult, op1=ALU.add, accum_out=slot[:, 0:1]).then_inc(s["rank_steps"], 1)
                    dve.wait_ge(s["rank_steps"], 4 * t + 3)
                    wait(dve, scattered[k], 16 * grp(-3))
                    v.tensor_copy(slot_i[k][:, :], slot[:, :]).then_inc(s["rank_steps"], 1)
            setup(v.memset(eps_ln[:, :], EPS_LN), False)
            setup(v.memset(state_sum[:, :, :], 0.0), False)
            for k in range(2):
                setup(v.memset(state[k][:, :], 0.0), False)
            for k in range(4):
                setup(v.memset(vaug[k][:, :], 0.0), k == 3)
            dve.wait_ge(s["act_setup"], 1)
            setup(v.tensor_scalar(c_tmp[:, 1, :], c_tmp[:, 0, :], 1.0, None, ALU.add))
            setup(v.reciprocal(c_tmp[:, 2, :], c_tmp[:, 1, :]))
            setup(v.tensor_tensor(c_sb[:, :], c_sb[:, :], c_tmp[:, 2, :], ALU.mult))
            assert count[0] == SETUP_SILU, count[0]
            dve.wait_ge(s["pe_setup"], 1)
            setup(v.tensor_copy(cT[:, :], m_ps[:, 0:BATCH]))
            assert count[0] == SETUP_CT, count[0]
            dve.wait_ge(s["pool_consts"], HEADS_KNOWN)
            dve.wait_ge(s["proj_in"], 16)
            setup(v.reduce_sum(place[:, :], head_of_row[:, :].rearrange("p (j h) -> p h j", h=2), AX.X), False)
            for k in range(PARTS):
                setup(v.tensor_copy(proj_cut[:, k, :], proj_nat[:, k, :]))
                if k < PARTS - 1:
                    setup(v.tensor_tensor(proj_nat[:, k + 1, :], proj_nat[:, k, :], proj_cut[:, k, :], ALU.subtract))
            for h in range(2):
                setup(v.tensor_scalar(proj_parts[:, :, FEAT * h:FEAT * h + FEAT], proj_cut[:, :, :], place[:, h:h + 1], None,
                                      ALU.mult), h == 1)
            assert count[0] == SETUP_PROJ, count[0]
            step(FIRST, -1, 1, lambda k: k == 3)
            dve.wait_ge(s["pe_setup"], 3)
            setup(v.tensor_copy(mod_raw[:, 0:3, :], ring[0:BATCH, 0, 0:384].rearrange("p (k e) -> p k e", k=3)), False)
            setup(v.tensor_copy(mod_raw[:, 3:6, :], ring[0:BATCH, 1, 0:384].rearrange("p (k e) -> p k e", k=3)))
            gates = mod_raw[:, 2:6:3, :]
            setup(v.tensor_scalar(mod_tmp[:, 0, :, :], gates, -1.0, None, ALU.mult))
            setup(v.tensor_tensor(mod_tmp[:, 1, :, :], mod_tmp[:, 0, :, :], gates, ALU.max))
            setup(v.tensor_scalar(mod_tmp[:, 0, :, :], mod_tmp[:, 1, :, :], 0.25, None, ALU.max))
            setup(v.tensor_scalar(mod_tmp[:, 1, :, :], gates, 0.0, 2.0, ALU.is_ge, ALU.mult))
            setup(v.tensor_scalar(mod_tmp[:, 2, :, :], mod_tmp[:, 1, :, :], -1.0, None, ALU.add))
            setup(v.tensor_tensor(mod_rows[:, 0:4:3, :], mod_tmp[:, 0, :, :], mod_tmp[:, 2, :, :], ALU.mult), False)
            setup(v.tensor_copy(mod_rows[:, 1, :], mod_raw[:, 3, :]), False)
            setup(v.tensor_scalar(mod_rows[:, 2, :], mod_raw[:, 4, :], 1.0, None, ALU.add), False)
            setup(v.tensor_copy(mod_rows[:, 4, :], mod_raw[:, 0, :]), False)
            setup(v.tensor_scalar(mod_rows[:, 5, :], mod_raw[:, 1, :], 1.0, None, ALU.add))
            assert count[0] == SETUP_ROWS, count[0]
            dve.wait_ge(s["pe_setup"], 4)
            setup(v.tensor_copy(gwT[:, :], m_ps[:, 8:8 + EXPERTS]), False)
            setup(v.tensor_copy(saT[:, :, :], m_ps[:, 16:24][:, :, None].to_broadcast([P, BATCH, 2])), False)
            setup(v.tensor_copy(caT[:, :, :], m_ps[:, 24:32][:, :, None].to_broadcast([P, BATCH, 2])), False)
            assert count[0] == SETUP_MOD, count[0]
            dve.wait_ge(s["pool_consts"], POOL_CONSTS)
            for k in range(4):
                setup(v.memset(vaug[k][:, 0:HEADS * VH].rearrange("p (h c) -> p h c", c=VH)[:, :, HD:HW], 1.0), False)
                setup(v.memset(stage[k][:, COL_ID:RW], 0.0), False)
            setup(v.memset(pad_rows[:, :], 0.0), False)
            setup(v.memset(lim_hi[:, :], BIG), False)
            setup(v.memset(lim_lo[:, :], -BIG))
            setup(v.memset(pad_rows[:, COL_ID:COL_ID + 1], float(TOKENS)), False)
            setup(v.memset(lim_hi[:, 0:GROUPS:2], 0.0), False)
            setup(v.memset(lim_lo[:, 0:GROUPS:2], 0.0), False)
            setup(v.tensor_copy(tile_no[:, :], iota_i[:, 0:FTILES]), False)
            setup(v.tensor_copy(expert_rank[:, :], iota_i[:, 80:88]), False)
            setup(v.tensor_copy(region_at[:, :], iota_i[:, 88:96]), False)
            setup(v.tensor_copy(filled[:, :], iota_i[:, 88:96]), False)
            setup(v.tensor_copy(row_no[:, :], iota_i[:, 96:97]), False)
            setup(v.tensor_copy(token_no[:, :], iota_i[:, 128:128 + TILES]), False)
            dve.wait_ge(s["weights_in"], 16 * N_W)
            setup(v.tensor_tensor(gbias[:, :], gb_row[:, :], eb_row[:, :], ALU.add))
            assert count[0] == SETUP_DONE, count[0]

            def spread(n):
                for b in SPREAD[n]:
                    dve.wait_ge(s["spread_ready"], b + 1)
                    two, rows = slice(2 * b, 2 * b + 2), spread_ps(b)
                    v.tensor_tensor(ob_g[:, two, :], rows[:, None, 0:E].to_broadcast([P, 2, E]),
                                    ob_row[:, None, :].to_broadcast([P, 2, E]), ALU.mult).then_inc(s["spread_done"], 1)
                    v.tensor_tensor(wo_g[:, two, :], rows[:, None, 0:E].to_broadcast([P, 2, E]),
                                    wo_sb[:, None, :].to_broadcast([P, 2, E]), ALU.mult).then_inc(s["spread_done"], 1)
                    v.tensor_copy(mod_bc[:, two, :, :].rearrange("p g k e -> p g (k e)"),
                                  rows[:, None, E:4 * E].to_broadcast([P, 2, 3 * E])).then_inc(s["spread_done"], 1)
            spread(FIRST)
            steps(dve, step, FIRST + 1, LAST, lo=2)

            n_table = [PADS_KNOWN]

            def table(ins, chained=True):
                n_table[0] += 1
                ins.then_inc(s["table_steps"], 1)
                if chained:
                    dve.wait_ge(s["table_steps"], n_table[0])
            dve.wait_ge(s["rank_steps"], 4 * TILES)
            table(v.tensor_tensor(n_f[:, :], filled[:, :], region_at[:, :], ALU.subtract))
            table(v.tensor_scalar(n_i[:, :], n_f[:, :], float(P - 1), None, ALU.add))
            table(v.tensor_scalar(n_s[:, :], n_i[:, :], 7, None, ALU.logical_shift_right))
            table(v.tensor_copy(n_t[:, :], n_s[:, :]))
            table(v.tensor_tensor(ee[:, :, :], upto[:, :, :], n_t[:, None, :].to_broadcast([P, EXPERTS, EXPERTS]), ALU.mult))
            table(v.reduce_sum(t_end[:, :], ee[:, :, :], AX.X))
            table(v.tensor_scalar(t_jump[:, :], n_t[:, :], -float(P), float(REGION), ALU.mult, ALU.add))

            table(v.tensor_scalar(valid[:, :], tile_no[:, :], t_end[:, EXPERTS - 1:EXPERTS], None, ALU.is_lt), False)
            for e in range(EXPERTS):
                table(v.tensor_scalar(jumps[:, :, e], tile_no[:, :], t_end[:, e:e + 1], t_jump[:, e:e + 1], ALU.is_ge, ALU.mult),
                      e == EXPERTS - 1)
            table(v.reduce_sum(rows_f[:, :], jumps[:, :, :], AX.X))
            table(v.scalar_tensor_tensor(out=rows_a[:, :], in0=tile_no[:, :], scalar=float(P), in1=rows_f[:, :],
                                         op0=ALU.mult, op1=ALU.add))
            table(v.tensor_tensor(rows_i[:, :], rows_a[:, :], valid[:, :], ALU.mult), False)
            assert n_table[0] == ROWS_KNOWN, n_table[0]
            table(v.tensor_tensor(behind[:, :, :], tile_no[:, :][:, :, None].to_broadcast([P, FTILES, EXPERTS]),
                                  t_end[:, None, :].to_broadcast([P, FTILES, EXPERTS]), ALU.is_ge))
            table(v.reduce_sum(exps_all[:, :], behind[:, :, :], AX.X))
            table(v.tensor_tensor(exps_i[:, :], exps_all[:, :], valid[:, :], ALU.mult), False)
            table(v.tensor_scalar(nowhere[:, :], valid[:, :], -NOWHERE, NOWHERE, ALU.mult, ALU.add))
            assert n_table[0] == TABLES_DONE, n_table[0]

            def ffn(m, gr, u, exists):
                j, slot_ = m - 1, (u - 1) % FUNROLL

                if exists(2):
                    e = dve.value_load(exps_i[0:1, bass.ds(m + 2, 1)], min_val=0, max_val=EXPERTS - 1)

                def relu(q):
                    dve.wait_ge(s["hid_ready"], m + 2)
                    dve.wait_ge(s["w1_set"], m + 2)
                    wait(dve, s["y_ready"], m)
                    v.tensor_scalar(hidT[(u + 1) % 2][:, q, :], hid_ps((u + 1) % 2, q),
                                    w1_now[(u + 1) % 4][:, COL_B1 + q:COL_B1 + q + 1], 0.0,
                                    ALU.add, ALU.max).then_inc(s["hid_hi_done"], 1)
                if exists(-1):
                    dve.wait_ge(s["y_ready"], j + 1)
                    wait(dve, s["res_done"], j - 1)
                    v.tensor_tensor(y1[:, slot_ % 2, :], y_ps(slot_ % 2), w1_now[slot_ % 4][:, COL_B2:WW], ALU.add).then_inc(s["y_steps"], 1)
                if exists(1):
                    relu(2)
                if exists(-1):
                    dve.wait_ge(s["y_steps"], 3 * j + 1)
                    v.tensor_tensor(y2[:, slot_ % 2, :], y1[:, slot_ % 2, :], xt[slot_][:, COL_G:COL_G + E], ALU.mult).then_inc(s["y_steps"], 2)
                if exists(1):
                    relu(3)
                if exists(-1):
                    wait(dve, stored[slot_], 16 * (gr + (u - 1) // FUNROLL))
                    v.tensor_scalar(res_i[slot_][:, :], xt[slot_][:, COL_ID:COL_ID + 1], nowhere[:, bass.ds(j, 1)], None,
                                    ALU.add).then_inc(s["res_i_done"], 1)
                if exists(2):
                    wait(dve, s["y_ready"], m - 1)
                    v.tensor_copy(w2_now[(u + 2) % 4], w2_sb[:, e, :]).then_inc(s["w2_set"], 1)

            dve.wait_ge(s["ffn_weights_in"], 16 * N_FFN_LOADS)
            ffn_steps(dve, ffn, lo=2)

        @block.tensor
        def _(pe):
            mm = nc.tensor.matmul

            def tp(dst, src, n_part=P):
                return nc.tensor.transpose(dst, src, ident[0:n_part, 0:n_part])

            pe.wait_ge(s["pool_consts"], IDENT_KNOWN)
            pe.wait_ge(s["dve_setup"], SETUP_SILU)
            tp(m_ps[:, 0:BATCH], c_sb[:, :], BATCH).then_inc(s["pe_setup"], 1)
            pe.wait_ge(s["dve_setup"], SETUP_CT)
            for k in range(2):
                mm(ring[0:BATCH, k, 0:384], cT[:, :], wmod_sb[:, 384 * k:384 * k + 384], start=True, stop=True).then_inc(s["pe_setup"], 1)
            pe.wait_ge(s["weights_in"], 16 * N_W)
            tp(m_ps[:, 8:8 + EXPERTS], gw_nat[:, :], EXPERTS)
            pe.wait_ge(s["dve_setup"], SETUP_ROWS)
            tp(m_ps[:, 16:24], mod_rows[:, 4, :], BATCH)
            tp(m_ps[:, 24:32], mod_rows[:, 5, :], BATCH).then_inc(s["pe_setup"], 1)

            def spread(n):
                for b in SPREAD[n]:
                    wait(pe, s["spread_done"], 3 * (b - 2))
                    mm(spread_ps(b), batch_sel[:, b, :], mod_rows[:, 0:4, :], start=True, stop=True).then_inc(s["spread_ready"], 1)
            pe.wait_ge(s["pool_consts"], POOL_CONSTS)
            spread(FIRST)
            pe.wait_ge(s["dve_setup"], SETUP_MOD)

            USES = [("qkv", 2, [("qk_done", 2, 2), ("v_done", 1, 1)]),
                    ("oT", -1, [("norm_steps", 3, 3)]),
                    ("onT", -1, [("onT_done", 1, 1)]),
                    ("proj", -1, [("ln2_steps", 5, 1)]),
                    ("h2T", -2, [("h2T_done", 1, 1)]),
                    ("xT", 3, [("hT_done", 1, 1)])]

            def small_bank_free(use, n, exists):
                at = [name for name, _, _ in USES].index(use)
                back = 0
                while True:
                    at -= 1
                    if at < 0:
                        at, back = len(USES) - 1, back + 1
                    name, off, readers = USES[at]
                    if isinstance(n, int) and back > 3:
                        return
                    if exists(off - back):
                        for signal, per_tile, k in readers:
                            wait(pe, s[signal], per_tile * (n - back + off) + k)
                        return

            def step(n, gr, u, exists):
                def grp(k):
                    return gr + (u + k) // 4
                base = 2 * (u + 1)
                def scores(k):
                    if k >= 2:
                        pe.wait_ge(s["kf_done"], 2 * n + k - 1)
                    for h in range(4 * k, 4 * k + 4):
                        last = mm(ring[:, (base + k) % 4, P * (h % 4):P * (h % 4) + P], kf_blk[:, h // 2, h % 2, :],
                                  qfT[u % 2][:, h // 2, :], start=True, stop=True)
                    last.then_inc(s["s_ready"], 1)
                if exists(0):
                    pe.wait_ge(s["q_done"], 2 * n + 2)
                    pe.wait_ge(s["k_act_done"], 3 * n + 3)
                    pe.wait_ge(s["k_dve_done"], n + 1)
                    scores(0)
                    scores(1)
                if exists(2):
                    pe.wait_ge(s["hT_done"], n + 3)
                    mm(m_ps[:, 0:P], wqkv_sb[:, 0:E], hT[:, :], start=True, stop=True)
                    mm(m_ps[:, P:2 * P], wqkv_sb[:, E:2 * E], hT[:, :], start=True, stop=True)
                    mm(m_ps[:, 2 * P:3 * P], hT[:, :], wqkv_sb[:, 2 * E:3 * E], start=True, stop=True).then_inc(s["qkv_ready"], 1)
                if isinstance(n, int) and FIRST < n < 0:
                    spread(n)
                if exists(0):
                    scores(2)
                    scores(3)
                if exists(-1):
                    small_bank_free("oT", n, exists)
                    pe.wait_ge(s["o_copied"], n)
                    for k in range(2):
                        last = tp(m_ps[:, k * P:(k + 1) * P], o_sb[(u - 1) % 2][:, k * P:(k + 1) * P])
                    last.then_inc(s["oT_ready"], 1)

                def features(signal, k, pos, src):
                    for j in range(4 * k, 4 * k + 4):
                        last = mm(ring[:, (base + pos) % 4, P * (j % 4):P * (j % 4) + P], proj_st[:, j, :],
                                  stack[(u + 1) % 2][:, j, src, :], start=True, stop=True)
                    last.then_inc(s[signal], 1)
                if isinstance(n, int) and n == -1:
                    pe.wait_ge(s["proj_stacked"], 16 * len(SLOT_W))
                if isinstance(n, int) and n == 0:
                    pe.wait_ge(s["spread_done"], 3 * BATCH)
                if exists(1):
                    pe.wait_ge(stacked[(u + 1) % 2], 48 * turn2(n + 1, gr, u + 1))
                    for k in range(2):
                        wait(pe, s["s_masked"], 4 * n + k + 1)
                        features("q_ready", k, 4 + k, 0)

                if exists(0):
                    wait(pe, s["state_steps"], 5 * gr + u)
                    wait(pe, s["rank_steps"], 4 * (n - 4) + 2)
                    wait(pe, s["gate_steps"], 5 * (n - 3) + 1)
                    pe.wait_ge(s["v_done"], n + 1)
                    pe.wait_ge(s["kf_done"], 2 * n + 2)
                    for j in range(PAIRS):
                        last = mm(f_ps[WIN * (j % 4):WIN * (j % 4) + WIN, 0, (j // 4) * P:(j // 4 + 1) * P],
                                  vaug[u % 4][:, 2 * VH * j:2 * VH * j + WIN], kf[u % 2][:, P * j:P * j + P],
                                  start=True, stop=True, tile_position=(0, WIN * (j % 4)))
                    last.then_inc(s["f_ready"], 1)

                def key_features(k):
                    wait(pe, s["s_masked"], 4 * n + k + 3)
                    features("k_ready", k, 6 + k, 1)
                if exists(1):
                    key_features(0)
                    key_features(1)
                if exists(-1):
                    pe.wait_ge(s["norm_steps"], 3 * (n - 1) + 3)
                    tp(m_ps[:, 0:P], o_n[:, :, :].rearrange("p h d -> p (h d)")).then_inc(s["onT_ready"], 1)

                def sums(G):
                    def dst(j):
                        return o_ps[WIN * (j % 4):WIN * (j % 4) + WIN, G * P:(G + 1) * P]
                    for j in range(4 * G, 4 * G + 4):
                        mm(dst(j), state[u % 2][:, VH * j:VH * j + WIN], qfT[u % 2][:, j, :], start=True, stop=False,
                           tile_position=(0, WIN * (j % 4)))
                    for h in range(2):
                        wait(pe, s["s_masked"], 4 * n + 2 * G + 2)
                        for j in range(4 * G, 4 * G + 4):
                            at = VH * 2 * j + HW * h
                            last = mm(dst(j), vaug[u % 4][:, at:at + WIN], scoresT[:, 2 * j + h, :], start=False, stop=(h == 1),
                                      tile_position=(0, WIN * (j % 4)))
                    return last
                if exists(0):
                    wait(pe, s["o_copied"], n)
                    wait(pe, s["state_done"], 2 * n)
                    sums(0)
                if exists(-1):
                    pe.wait_ge(s["onT_done"], n)
                    mm(m_ps[:, P:2 * P], onT[:, :], wo_g[:, grp(-1), :], start=True, stop=True).then_inc(s["proj_ready"], 1)
                if exists(0):
                    sums(1).then_inc(s["o_ready"], 1)
                if exists(-2):
                    small_bank_free("h2T", n, exists)
                    pe.wait_ge(s["h_steps"], 2 * (n - 2) + 2)
                    tp(m_ps[:, 0:P], stage[(u - 2) % 4][:, 0:E]).then_inc(s["h2T_ready"], 1)
                if exists(0):
                    pe.wait_ge(s["state_steps"], 5 * gr + u + (2 if u == 3 else 1))
                    wait(pe, s["state_done"], 2 * n)
                    for k in range(2):
                        last = tp(f_ps[:, 1, k * P:(k + 1) * P], state_sum[:, k, :])
                    last.then_inc(s["state_turned"], 1)
                if exists(1):
                    for k in range(2):
                        pe.wait_ge(s["q_done"], 2 * (n + 1) + k + 1)
                        for j in range(4 * k, 4 * k + 4):
                            last = mm(ring[:, (base + 8 + k) % 4, P * (j % 4):P * (j % 4) + P], stack[(u + 1) % 2][:, j, 1, :],
                                      proj_st[:, j, :], start=True, stop=True)
                        last.then_inc(s["kf_ready"], 1)
                if exists(3):
                    small_bank_free("xT", n, exists)
                    pe.wait_ge(s["ln1_steps"], 4 * (n + 3) + 4)
                    tp(m_ps[:, 0:P], xn1[:, (u + 3) % 2, :]).then_inc(s["xT_ready"], 1)
                if exists(-3):
                    wait(pe, s["rank_steps"], 4 * (n - 4) + 2)
                    pe.wait_ge(s["gate_steps"], 5 * (n - 3) + 5)
                    mm(f_ps[:, 0, 400:408], earlier[:, :], onehot[:, :], start=True, stop=True)
                    mm(f_ps[:, 0, 408:416], ones[:, :], onehot[:, :], start=True, stop=True).then_inc(s["rank_ready"], 1)
                if exists(-2):
                    wait(pe, s["gate_steps"], 5 * (n - 3) + 1)
                    pe.wait_ge(s["h2T_done"], n - 1)
                    mm(f_ps[:, 0, 384:392], h2T[:, :], gwT[:, :], start=True, stop=True).then_inc(s["gate_ready"], 1)
            steps(pe, step, FIRST, LAST)

            def ffn(m, gr, u, exists):
                if exists(2):
                    wait(pe, s["xtT_done"], m + 2)
                    pe.wait_ge(xt_loaded[(u + 2) % FUNROLL], 16 * (gr + (u + 2) // FUNROLL + 1))
                    tp(m_ps[:, 0:P], xt[(u + 2) % FUNROLL][:, 0:E]).then_inc(s["xtT_ready"], 1)
                if exists(1):
                    pe.wait_ge(s["xtT_done"], m + 2)
                    pe.wait_ge(s["w1_set"], m + 2)
                    wait(pe, s["hid_lo_done"], CHUNKS // 2 * m)
                    wait(pe, s["hid_hi_done"], CHUNKS // 2 * m)
                    for q in range(CHUNKS):
                        last = mm(hid_ps((u + 1) % 2, q), w1_now[(u + 1) % 4][:, q * P:(q + 1) * P], xtT[:, (u + 1) % 2, :],
                                  start=True, stop=True)
                    last.then_inc(s["hid_ready"], 1)
                if exists(0):
                    pe.wait_ge(s["w2_set"], m + 1)
                    pe.wait_ge(s["hid_lo_done"], CHUNKS // 2 * (m + 1))
                    pe.wait_ge(s["hid_hi_done"], CHUNKS // 2 * (m + 1))
                    wait(pe, s["y_steps"], 3 * (m - 2) + 1)
                    for q in range(CHUNKS):
                        last = mm(y_ps(u % 2), hidT[u % 2][:, q, :], w2_now[u % 4][:, q * E:(q + 1) * E],
                                  start=(q == 0), stop=(q == CHUNKS - 1))
                    last.then_inc(s["y_ready"], 1)
            pe.wait_ge(s["table_steps"], TABLES_DONE)
            ffn_steps(pe, ffn)


_INS = ["L0_attn_x", "L0_attn_qkv_w", "L0_attn_qkv_b", "L0_attn_out_w", "L0_attn_out_b", "L0_attn_proj",
        "L0_ffn_gate_w", "L0_ffn_gate_b", "L0_ffn_expert_bias", "L0_ffn_w1", "L0_ffn_b1", "L0_ffn_w2", "L0_ffn_b2",
        "L0_c", "L0_wmod"]
_OUT = ((BATCH, SEQ, E), "float32")


def kernel(**inputs):
    import numpy as _np
    import concourse.bacc as _bacc
    from concourse.bass_utils import run_bass_kernel_spmd as _run

    nc = _bacc.Bacc("TRN2", target_bir_lowering=False, num_devices=1)
    arrays, args = {}, []
    for name in _INS:
        a = _np.ascontiguousarray(inputs[name])
        arrays[f"in_{name}"] = a
        args.append(nc.dram_tensor(f"in_{name}", a.shape, mybir.dt.from_np(a.dtype), kind="ExternalInput").ap())
    shape, dtype = _OUT
    args.append(nc.dram_tensor("out_x", shape, mybir.dt.from_np(_np.dtype(dtype)), kind="ExternalOutput").ap())
    adaln_block(nc, *args)
    r = _run(nc, [arrays], core_ids=[0])
    return r.results[0]["out_x"]
```
